# Optimizing a Trainium2 kernel written in Bass

```python
import numpy as np
import jax
import jax.numpy as jnp

def _softmax(x, axis=-1):
    return jax.nn.softmax(x, axis=axis)
def _gelu(x):
    return jax.nn.gelu(x, approximate=True)
def _silu(x):
    return jax.nn.silu(x)
def _sigmoid(x):
    return jax.nn.sigmoid(x)
def _layernorm(x, axis=-1, eps=1e-5):
    m = jnp.mean(x, axis=axis, keepdims=True)
    v = jnp.var(x, axis=axis, keepdims=True)
    return (x - m) / jnp.sqrt(v + eps)
def _scatter_add(tgt, idx, src, axis=0):
    return tgt.at[idx].add(src)
def _segment_sum(src, seg, n):
    return jax.ops.segment_sum(src, seg, n)

kernel_name = 'mk_conv_preact_d2_conv_nhwc128_6dde46'

def setup_inputs(seed: int = 0):
    np.random.seed(seed)
    _w = jnp.asarray
    def _rec_inputs():
        import jax
        import jax.numpy as jnp
        _gk = jax.random.key(seed)
        x = -0.0003482 + 1 * jax.random.normal(jax.random.fold_in(_gk, 1), (1, 384, 384, 128), jnp.float32)
        return x
    x = _rec_inputs()
    def _L0_conv_setup():
        import jax, jax.numpy as jnp
        import numpy as np
        D_MODEL = 128
        CHANNEL = 128
        EPS = 1e-05

        def _layernorm(x, gamma, beta):
            mu = jnp.mean(x, axis=-1, keepdims=True)
            var = jnp.var(x, axis=-1, keepdims=True)
            return (x - mu) * jax.lax.rsqrt(var + EPS) * gamma + beta
        key = jax.random.key(seed)
        ks = jax.random.split(key, 8)
        B, N = (1, 384)
        d, c = (D_MODEL, CHANNEL)
        x = jax.random.normal(ks[0], (B, N, N, d), dtype=jnp.float32)
        ln1_g = jnp.ones((d,), jnp.float32)
        ln1_b = jnp.zeros((d,), jnp.float32)
        W_proj = jax.random.normal(ks[1], (d, 4 * c), dtype=jnp.float32) / np.sqrt(d)
        W_gate = jax.random.normal(ks[2], (d, d), dtype=jnp.float32) / np.sqrt(d)
        ln2_g = jnp.ones((c,), jnp.float32)
        ln2_b = jnp.zeros((c,), jnp.float32)
        W_ab = jax.random.normal(ks[3], (c, d), dtype=jnp.float32) / np.sqrt(c)
        return {'x': x, 'ln1_g': ln1_g, 'ln1_b': ln1_b, 'W_proj': W_proj, 'W_gate': W_gate, 'ln2_g': ln2_g, 'ln2_b': ln2_b, 'W_ab': W_ab}
    _L0_conv_all = _L0_conv_setup()
    _L0_conv_in = {k: v for k, v in _L0_conv_all.items() if k in ('ln1_g', 'ln1_b', 'W_proj', 'W_gate', 'ln2_g', 'ln2_b', 'W_ab', )}
    del _L0_conv_all

    def _L1_conv_setup():
        import jax, jax.numpy as jnp
        import numpy as np
        B, N, D = (1, 384, 128)
        key = jax.random.key(seed)
        k1, k2, k3, k4, k5 = jax.random.split(key, 5)
        s = 1.0 / np.sqrt(D)
        return {'pair': jax.random.normal(k1, (B, N, N, D), dtype=jnp.float32), 'Wa': jax.random.normal(k2, (D, D), dtype=jnp.float32) * s, 'ba': jax.random.normal(k3, (D,), dtype=jnp.float32) * s, 'Wb': jax.random.normal(k4, (D, D), dtype=jnp.float32) * s, 'bb': jax.random.normal(k5, (D,), dtype=jnp.float32) * s}
    _L1_conv_all = _L1_conv_setup()
    _L1_conv_in = {k: v for k, v in _L1_conv_all.items() if k in ('Wa', 'ba', 'Wb', 'bb', )}
    del _L1_conv_all

    return {
        "x": x,
        "L0_conv_ln1_g": _L0_conv_in["ln1_g"],
        "L0_conv_ln1_b": _L0_conv_in["ln1_b"],
        "L0_conv_W_proj": _L0_conv_in["W_proj"],
        "L0_conv_W_gate": _L0_conv_in["W_gate"],
        "L0_conv_ln2_g": _L0_conv_in["ln2_g"],
        "L0_conv_ln2_b": _L0_conv_in["ln2_b"],
        "L0_conv_W_ab": _L0_conv_in["W_ab"],
        "L1_conv_Wa": _L1_conv_in["Wa"],
        "L1_conv_ba": _L1_conv_in["ba"],
        "L1_conv_Wb": _L1_conv_in["Wb"],
        "L1_conv_bb": _L1_conv_in["bb"],
    }

def reference(x, L0_conv_ln1_g, L0_conv_ln1_b, L0_conv_W_proj, L0_conv_W_gate, L0_conv_ln2_g, L0_conv_ln2_b, L0_conv_W_ab, L1_conv_Wa, L1_conv_ba, L1_conv_Wb, L1_conv_bb):
    import jax
    import jax.numpy as jnp
    def _L0_conv_ref(x, ln1_g, ln1_b, W_proj, W_gate, ln2_g, ln2_b, W_ab):
        import jax, jax.numpy as jnp
        import numpy as np
        D_MODEL = 128
        CHANNEL = 128
        EPS = 1e-05

        def _layernorm(x, gamma, beta):
            mu = jnp.mean(x, axis=-1, keepdims=True)
            var = jnp.var(x, axis=-1, keepdims=True)
            return (x - mu) * jax.lax.rsqrt(var + EPS) * gamma + beta
        xn = _layernorm(x, ln1_g, ln1_b)
        proj = xn @ W_proj
        a1, a2, b1, b2 = jnp.split(proj, 4, axis=-1)
        g = jax.nn.sigmoid(xn @ W_gate)
        a = jax.nn.sigmoid(a1) * a2
        b = jax.nn.sigmoid(b1) * b2
        ab = jnp.einsum('bikc,bjkc->bijc', a, b)
        out = _layernorm(ab, ln2_g, ln2_b) @ W_ab
        return g * out

    def _L1_conv_ref(pair, Wa, ba, Wb, bb):
        import jax, jax.numpy as jnp
        import numpy as np
        B, N, D = (1, 384, 128)
        left = jnp.einsum('bikd,ed->bike', pair, Wa) + ba
        right = jnp.einsum('bkjd,ed->bkje', pair, Wb) + bb
        upd = jnp.einsum('bikd,bkjd->bijd', left, right)
        return pair + upd

    def _gn(v, G=32, eps=1e-5):
        B_, H_, W_, C_ = v.shape
        g = v.reshape(B_, H_, W_, G, C_ // G)
        m = jnp.mean(g, axis=(1, 2, 4), keepdims=True)
        s = jnp.var(g, axis=(1, 2, 4), keepdims=True)
        return ((g - m) / jnp.sqrt(s + eps)).reshape(v.shape)

    def _ln_c(v, eps=1e-6):
        m = jnp.mean(v, axis=-1, keepdims=True)
        s = jnp.var(v, axis=-1, keepdims=True)
        return (v - m) / jnp.sqrt(s + eps)

    def _ln_t(v, eps=1e-5):
        m = jnp.mean(v, axis=-1, keepdims=True)
        s = jnp.var(v, axis=-1, keepdims=True)
        return (v - m) / jnp.sqrt(s + eps)

    def _to_tokens(v):
        B_, H_, W_, C_ = v.shape
        return v.reshape(B_, H_ * W_, C_)
    def _from_tokens(t, like):
        return t.reshape(like.shape)

    x = x + _L0_conv_ref(_gn(x), L0_conv_ln1_g, L0_conv_ln1_b, L0_conv_W_proj, L0_conv_W_gate, L0_conv_ln2_g, L0_conv_ln2_b, L0_conv_W_ab)
    x = x + _L1_conv_ref(_gn(x), L1_conv_Wa, L1_conv_ba, L1_conv_Wb, L1_conv_bb)
    return x


_drawn_inputs = setup_inputs


def setup_inputs(seed=0):
    import zlib

    import numpy as np

    out = dict(_drawn_inputs(seed))
    spreads = {'L0_conv_ln1_g': (1.0, 0.2),
     'L0_conv_ln1_b': (0.0, 0.1),
     'L0_conv_ln2_g': (1.0, 0.2),
     'L0_conv_ln2_b': (0.0, 0.1)}
    factors = {}
    for name, (base, spread) in spreads.items():
        noise = np.random.default_rng([zlib.crc32(name.encode()), seed]).standard_normal(out[name].shape)
        drawn = base * np.exp(spread * noise) if base else spread * noise
        out[name] = jnp.asarray(drawn.astype(out[name].dtype))
    for name, factor in factors.items():
        out[name] = (out[name] * factor).astype(out[name].dtype)
    return out
```

```python
import concourse.bass as bass
from concourse import mybir
from contextlib import ExitStack

F32 = mybir.dt.float32
F16 = mybir.dt.float16
ALU = mybir.AluOpType
ACT = mybir.ActivationFunctionType
AX = mybir.AxisListType

C = 128
GROUP = 4
NG = C // GROUP
IB = 16
CH = 8
NCH = C // CH
WS = 64.0
EPS = 1e-5
QT = 4


class Plan:
    pass


def chained(engine, sem):
    count = [0]

    def step(ins):
        count[0] += 1
        ins.then_inc(sem, 1)
        engine.wait_ge(sem, count[0])
        return ins
    return step


def prepare_weights(nc, p, io):
    with ExitStack() as ctx:
        sb = lambda n, s, d: ctx.enter_context(nc.sbuf_tensor(n, s, d))
        w_proj = sb("w_proj", [C, 4 * C], F32)
        w_gate = sb("w_gate", [C, C], F32)
        w_ab = sb("w_ab", [C, C], F32)
        vec = sb("vec", [C, 4], F32)
        center = sb("center", [C, C], F32)
        scaled = sb("scaled", [C, 4 * C], F32)
        b1_bc = sb("b1_bc", [C, C], F32)
        psw = ctx.enter_context(nc.psum_tensor("psw", [C, 512], F32))
        psv = ctx.enter_context(nc.psum_tensor("psv", [C, 512], F32))
        loaded = p.sem("weights_loaded")
        dve_step = p.sem("w_dve_step")
        ready = p.sem("w_operand_ready")
        product = p.sem("w_product")
        with nc.Block() as block:
            @block.sync
            def _(sp):
                for dst, src in ((w_proj, io["W_proj"]), (w_gate, io["W_gate"]), (w_ab, io["W_ab"]),
                                 (vec, io["ln_vectors"]), (center, io["centering"]),
                                 (p.wa_t, io["WaT"]), (p.wb_t, io["WbT"]),
                                 (p.ident, io["identity"]), (p.masks, io["row_masks"]),
                                 (p.expand, io["expand"]), (p.bias_ab, io["bias_ab"]),
                                 (p.group_mat, io["group_mean"])):
                    sp.dma_start(dst[:, :], src).then_inc(loaded, 16)

            @block.vector
            def _(dve):
                step = chained(dve, dve_step)
                dve.wait_ge(loaded, 16 * 12)
                step(dve.memset(p.ones[:, :], 1.0))
                step(dve.memset(p.mean_mat[:, :], 1.0 / C))
                step(dve.tensor_copy(p.ident16[:, :], p.ident[:, :]))
                jobs = [(w_proj, vec[:, 0:1], 4 * C, p.w64, p.wh, p.wl),
                        (w_gate, vec[:, 0:1], C, None, p.gh, p.gl),
                        (w_ab, vec[:, 2:3], C, None, p.ah, p.al)]
                for n, (w, gain, width, keep, hi, lo) in enumerate(jobs):
                    dve.tensor_scalar(scaled[:, 0:width], w[:, 0:width], gain, None, ALU.mult).then_inc(ready, 1)
                    dve.wait_ge(product, n + 1)
                    dst = keep if keep is not None else scaled
                    if width == 4 * C:
                        out = dst[:, :].rearrange("c (h s f) -> c s h f", h=2, s=2)
                        step(dve.tensor_scalar(out, psw[:, :].rearrange("c (s h f) -> c s h f", s=2, h=2),
                                               WS, None, ALU.mult))
                    else:
                        step(dve.tensor_scalar(dst[:, 0:width], psw[:, 0:width], WS, None, ALU.mult))
                    step(dve.tensor_copy(hi[:, :], dst[:, 0:width]))
                    step(dve.tensor_tensor(lo[:, :], dst[:, 0:width], hi[:, :], ALU.subtract))
                step(dve.tensor_scalar(b1_bc[:, :], p.ones[:, :], vec[:, 1:2], None, ALU.mult))
                dve.sem_inc(ready, 1)
                dve.wait_ge(product, 4)
                out = scaled[:, :].rearrange("c (h s f) -> c s h f", h=2, s=2)
                step(dve.tensor_scalar(out, psw[:, :].rearrange("c (s h f) -> c s h f", s=2, h=2),
                                       WS, None, ALU.mult))
                step(dve.tensor_copy(p.vh[:, :], scaled[:, :]))
                step(dve.tensor_tensor(p.vl[:, :], scaled[:, :], p.vh[:, :], ALU.subtract))
                dve.wait_ge(product, 5)
                step(dve.tensor_copy(p.vg[:, :], psv[:, 0:1]))
                step(dve.tensor_scalar(p.v2[:, :], psv[:, 1:2], WS, None, ALU.mult))
                for w, hi, lo in ((p.wa_t, p.lah, p.lal), (p.wb_t, p.lbh, p.lbl)):
                    step(dve.tensor_scalar(scaled[:, 0:C], w[:, :], WS, None, ALU.mult))
                    step(dve.tensor_copy(hi[:, :], scaled[:, 0:C]))
                    step(dve.tensor_tensor(lo[:, :], scaled[:, 0:C], hi[:, :], ALU.subtract))

            @block.tensor
            def _(pe):
                for n, width in enumerate((4 * C, C, C)):
                    pe.wait_ge(ready, n + 1)
                    pe.matmul(psw[:, 0:width], lhsT=center[:, :], rhs=scaled[:, 0:width],
                              start=True, stop=True).then_inc(product, 1)
                pe.wait_ge(ready, 4)
                pe.matmul(psw[:, :], lhsT=b1_bc[:, :], rhs=w_proj[:, :], start=True, stop=True).then_inc(product, 1)
                pe.matmul(psv[:, 0:1], lhsT=w_gate[:, :], rhs=vec[:, 1:2], start=True, stop=True)
                pe.matmul(psv[:, 1:2], lhsT=w_ab[:, :], rhs=vec[:, 3:4], start=True, stop=True).then_inc(product, 1)


def stats0(nc, p, io):
    N, KT = p.N, p.KT
    ROW = KT * N
    x_by_channel = io["x"].rearrange("c (t p) k -> c p t k", p=128)
    with ExitStack() as ctx:
        sb = lambda n, s, d: ctx.enter_context(nc.sbuf_tensor(n, s, d))
        ps = lambda n: ctx.enter_context(nc.psum_tensor(n, [128, 512], F32))
        xg = [sb(f"xg{k}", [128, GROUP, KT, N], F32) for k in range(2)]
        sq = [sb(f"sq{k}", [128, GROUP, ROW], F32) for k in range(2)]
        csum = [sb(f"csum{k}", [128, ROW], F32) for k in range(2)]
        S1 = sb("S1", [128, ROW], F32)
        zeros = sb("zeros", [128, N], F32)
        bn = [sb(f"bn{k}", [128, GROUP * KT, 6], F32) for k in range(2)]
        mv = [sb(f"mv{k}", [128, 4], F32) for k in range(2)]
        gst = [sb(f"gst{k}", [128, 8], F32) for k in range(2)]
        all_st = sb("all_st", [128, 3, NG], F32)
        expo = sb("expo", [128, 2], F32)
        diag = sb("diag", [NG, 3, NG], F32)
        cols = sb("cols", [NG, 3], F32)
        tbar = sb("tbar", [128, 2], F32)
        t_bc = sb("t_bc", [C, C], F32)
        kap = sb("kap", [C, 512], F32)
        kh = sb("kh", [C, 512], F16)
        kl = sb("kl", [C, 512], F16)
        base = sb("base", [C, 512], F16)
        mu = sb("mu", [128, ROW], F32)
        var = sb("var", [128, ROW], F32)
        expos = sb("expos", [128, 2, ROW], F32)
        rstd = sb("rstd", [128, 2, ROW], F32)
        halves = sb("halves", [128, 2, 2, ROW], F16)
        s3 = sb("s3", [C, 4], F16)
        psS2 = [ps(f"psS2_{t}") for t in range(KT)]
        psG = ps("psG")
        psK = ps("psK")
        psT = ps("psT")
        psH = ctx.enter_context(nc.psum_tensor("psH", [128, 128], F16))
        xload = [p.sem(f"xg_loaded{k}") for k in range(2)]
        consts = p.sem("stats_consts")
        dve_step = p.sem("stats_dve_step")
        bn_done = p.sem("bn_done")
        bn_seen = p.sem("bn_seen")
        mv_ready = p.sem("mv_ready")
        gmean = p.sem("gmean_ready")
        gvar = p.sem("gvar_ready")
        s_ready = p.sem("s_ready")
        st_ready = p.sem("st_ready")
        sq_ready = p.sem("sq_ready")
        s2_added = p.sem("s2_added")
        csum_ready = p.sem("csum_ready")
        s1_added = p.sem("s1_added")
        pool_step = p.sem("stats_pool_step")
        col_ready = p.sem("col_ready")
        prod = p.sem("stats_product")
        var_ready = p.sem("var_ready")
        rstd_ready = p.sem("rstd_ready")
        evac = p.sem("stats_evacuated")
        halves_ready = p.sem("halves_ready")
        stored = p.sem("rstd_stored")
        PAIRS = NG // 2

        with nc.Block() as block:
            @block.sync
            def _(sp):
                def load(k, first):
                    for c in range(GROUP):
                        sp.dma_start(xg[k][:, c, :, :], x_by_channel[first + c]).then_inc(xload[k], 16)
                for k in range(2):
                    load(k, GROUP * k)
                with sp.Fori(0, PAIRS - 1) as i:
                    for k in range(2):
                        sp.wait_ge(bn_done, 2 * i + k + 1)
                        sp.wait_ge(csum_ready, 2 * i + k + 1)
                        sp.wait_ge(sq_ready, 2 * i + k + 1)
                        for c in range(GROUP):
                            sp.dma_start(xg[k][:, c, :, :],
                                         x_by_channel[(2 * i + 2 + k) * GROUP + c]).then_inc(xload[k], 16)
                sp.wait_ge(halves_ready, 1)
                for q, d in ((0, p.r1_rows), (1, p.std_rows)):
                    for row, half in enumerate((0, 1, 0)):
                        sp.dma_start(d[row].rearrange("(t p) k -> p t k", p=128),
                                     halves[:, q, half, :].rearrange("p (t k) -> p t k", t=KT)).then_inc(stored, 16)
                sp.wait_ge(stored, 16 * 6)

            @block.gpsimd
            def _(pool):
                pool.memset(expo[:, 0:1], -0.5).then_inc(pool_step, 1)
                pool.memset(expos[:, 0, :], -0.5).then_inc(pool_step, 1)
                pool.memset(expos[:, 1, :], 0.5).then_inc(pool_step, 1)
                pool.wait_ge(pool_step, 3)
                with pool.Fori(0, PAIRS) as i:
                    for k in range(2):
                        g = 2 * i + k
                        pool.wait_ge(xload[k], (i + 1) * (16 * GROUP))
                        pool.wait_ge(s1_added, g + 1)
                        flat = [xg[k][:, c, :, :].rearrange("p t k -> p (t k)") for c in range(GROUP)]
                        pool.tensor_tensor(csum[k][:, :], flat[0], flat[1], ALU.add).then_inc(pool_step, 1)
                        pool.wait_ge(pool_step, g * 2 + 4)
                        pool.tensor_tensor(csum[k][:, :], csum[k][:, :], flat[2], ALU.add).then_inc(pool_step, 1)
                        pool.wait_ge(gvar, g + 1)
                        pool.tensor_tensor(gst[k][:, 3:4], gst[k][:, 2:3], expo[:, 0:1], ALU.pow).then_inc(s_ready, 1)
                        pool.wait_ge(pool_step, g * 2 + 5)
                        pool.tensor_tensor(csum[k][:, :], csum[k][:, :], flat[3], ALU.add).then_inc(csum_ready, 1)
                for q in range(2):
                    pool.wait_ge(var_ready, 1)
                    pool.tensor_tensor(rstd[:, q, :], var[:, :], expos[:, q, :], ALU.pow).then_inc(rstd_ready, 1)

            @block.scalar
            def _(act):
                with act.Fori(0, PAIRS) as i:
                    for k in range(2):
                        act.wait_ge(st_ready, 2 * i + k + 1)
                        act.wait_ge(s2_added, 2 * i + k + 1)
                        act.activation(sq[k][:, :, :].rearrange("p c n -> p (c n)"),
                                       xg[k][:, :, :, :].rearrange("p c t k -> p (c t k)"),
                                       ACT.Square, scale=gst[k][:, 3:4], bias=gst[k][:, 4:5]).then_inc(sq_ready, 1)

            @block.tensor
            def _(pe):
                pe.wait_ge(consts, 1)
                for t in range(KT):
                    pe.matmul(psS2[t][:, 0:N], lhsT=p.ident[:, :], rhs=zeros[:, :], start=True, stop=False)
                pe.sem_inc(s2_added, 2)
                with pe.Fori(0, PAIRS) as i:
                    for k in range(2):
                        pe.wait_ge(mv_ready, 2 * i + k + 1)
                        pe.matmul(psG[:, 0:2], lhsT=p.mean_mat[:, :], rhs=mv[k][:, 0:2],
                                  start=True, stop=True).then_inc(gmean, 1)
                        pe.wait_ge(sq_ready, 2 * i + k + 1)
                        for c in range(GROUP):
                            for t in range(KT):
                                last = pe.matmul(psS2[t][:, 0:N], lhsT=p.ident[:, :],
                                                 rhs=sq[k][:, c, t * N:(t + 1) * N], start=False, stop=False)
                        last.then_inc(s2_added, 1)
                for t in range(KT):
                    last = pe.matmul(psS2[t][:, 0:N], lhsT=p.ident[:, :], rhs=zeros[:, :], start=False, stop=True)
                last.then_inc(prod, 1)
                pe.wait_ge(col_ready, 1)
                pe.matmul(psG[:, 0:3], lhsT=p.expand[:, :], rhs=cols[:, :], start=True, stop=True).then_inc(prod, 1)
                pe.wait_ge(col_ready, 2)
                pe.matmul(psK[:, :], lhsT=t_bc[:, :], rhs=p.w64[:, :], start=True, stop=True).then_inc(prod, 1)
                pe.wait_ge(col_ready, 3)
                pe.transpose(psH[0:4, :], s3[:, :], p.ident16[:, :]).then_inc(prod, 1)
                pe.wait_ge(rstd_ready, 1)
                n = 0
                for kt in range(KT):
                    for t in range(KT):
                        if n:
                            pe.wait_ge(evac, n)
                        pe.transpose(psT[:, 0:128], rstd[:, 0, t * N + kt * 128:t * N + kt * 128 + 128],
                                     p.ident[:, :]).then_inc(prod, 1)
                        n += 1

            @block.vector
            def _(dve):
                step = chained(dve, dve_step)
                step(dve.memset(S1[:, :], 0.0))
                dve.memset(zeros[:, :], 0.0).then_inc(consts, 1)
                dve.sem_inc(s1_added, 2)
                LOOP0 = 1
                PER = 2 * 8

                def add_s1(k, g):
                    dve.wait_ge(csum_ready, g + 1)
                    dve.scalar_tensor_tensor(out=S1[:, :], in0=csum[k][:, :], scalar=gst[k][:, 3:4],
                                             in1=S1[:, :], op0=ALU.mult, op1=ALU.add).then_inc(s1_added, 1)
                    dve.wait_ge(s1_added, g + 3)

                with dve.Fori(0, PAIRS) as i:
                    for k in range(2):
                        g = 2 * i + k
                        done = [0]

                        def link(ins):
                            done[0] += 1
                            ins.then_inc(dve_step, 1)
                            dve.wait_ge(dve_step, i * PER + (LOOP0 + 8 * k + done[0]))
                        dve.wait_ge(xload[k], (i + 1) * (16 * GROUP))
                        for c in range(GROUP):
                            for t in range(KT):
                                last = dve.bn_stats(bn[k][:, c * KT + t, :], xg[k][:, c, t, :])
                        last.then_inc(bn_done, 1)
                        dve.wait_ge(bn_done, g + 1)
                        dve.sem_inc(bn_seen, 1)
                        link(dve.bn_aggr(mv[k][:, 0:2], bn[k][:, :, :].rearrange("p a b -> p (a b)")))
                        dve.scalar_tensor_tensor(out=mv[k][:, 1:2], in0=mv[k][:, 0:1], scalar=mv[k][:, 0:1],
                                                 in1=mv[k][:, 1:2], op0=ALU.mult, op1=ALU.add).then_inc(mv_ready, 1)
                        if k:
                            add_s1(0, g - 1)
                        dve.wait_ge(gmean, g + 1)
                        link(dve.tensor_copy(gst[k][:, 0:1], psG[:, 0:1]))
                        link(dve.tensor_tensor(gst[k][:, 1:2], gst[k][:, 0:1], gst[k][:, 0:1], ALU.mult))
                        link(dve.tensor_tensor(gst[k][:, 2:3], psG[:, 1:2], gst[k][:, 1:2], ALU.subtract))
                        link(dve.tensor_scalar(gst[k][:, 5:6], gst[k][:, 0:1], -1.0, None, ALU.mult))
                        dve.tensor_scalar(gst[k][:, 2:3], gst[k][:, 2:3], 0.0, EPS, ALU.max, ALU.add).then_inc(gvar, 1)
                        dve.wait_ge(s_ready, g + 1)
                        dve.tensor_tensor(gst[k][:, 4:5], gst[k][:, 5:6], gst[k][:, 3:4], ALU.mult).then_inc(st_ready, 1)
                        dve.wait_ge(st_ready, g + 1)
                        link(dve.tensor_copy(all_st[:, 0, bass.ds(g, 1)], gst[k][:, 3:4]))
                        link(dve.tensor_copy(all_st[:, 1, bass.ds(g, 1)], gst[k][:, 4:5]))
                        link(dve.tensor_copy(all_st[:, 2, bass.ds(g, 1)], gst[k][:, 5:6]))
                    add_s1(1, 2 * i + 1)
                total = [LOOP0 + PER * PAIRS]

                def step(ins):
                    total[0] += 1
                    ins.then_inc(dve_step, 1)
                    dve.wait_ge(dve_step, total[0])
                for q in range(3):
                    step(dve.tensor_tensor(diag[:, q, :], all_st[0:NG, q, :], p.ident[0:NG, 0:NG], ALU.mult))
                step(dve.tensor_reduce(cols[:, :], diag[:, :, :], axis=AX.X, op=ALU.add))
                dve.sem_inc(col_ready, 1)
                dve.wait_ge(prod, 2)
                step(dve.tensor_copy(p.st0[:, 0:3], psG[:, 0:3]))
                step(dve.tensor_scalar(t_bc[:, :], p.ones[:, :], p.st0[:, 1:2], None, ALU.mult))
                dve.sem_inc(col_ready, 1)
                step(dve.tensor_copy(s3[:, 0:1], p.st0[:, 0:1]))
                step(dve.tensor_copy(s3[:, 1:2], p.st0[:, 0:1]))
                step(dve.tensor_tensor(s3[:, 2:3], p.st0[:, 0:1], s3[:, 0:1], ALU.subtract))
                step(dve.memset(s3[:, 3:4], 0.0))
                dve.sem_inc(col_ready, 1)
                step(dve.tensor_reduce(tbar[:, 0:1], all_st[:, 1, :], axis=AX.X, op=ALU.add))
                step(dve.tensor_scalar(tbar[:, 1:2], tbar[:, 0:1], 1.0 / NG, None, ALU.mult))
                step(dve.tensor_scalar(mu[:, :], S1[:, :], 1.0 / C, tbar[:, 1:2], ALU.mult, ALU.add))
                step(dve.tensor_tensor(mu[:, :], mu[:, :], mu[:, :], ALU.mult))
                for t in range(KT):
                    step(dve.scalar_tensor_tensor(out=var[:, t * N:(t + 1) * N], in0=psS2[t][:, 0:N], scalar=1.0 / C,
                                                  in1=mu[:, t * N:(t + 1) * N], op0=ALU.mult, op1=ALU.subtract))
                dve.tensor_scalar(var[:, :], var[:, :], 0.0, EPS, ALU.max, ALU.add).then_inc(var_ready, 1)
                dve.wait_ge(prod, 3)
                step(dve.tensor_copy(kap[:, :], psK[:, :]))
                step(dve.tensor_copy(kh[:, :], kap[:, :]))
                step(dve.tensor_tensor(kl[:, :], kap[:, :], kh[:, :], ALU.subtract))
                step(dve.tensor_scalar(base[:, :], kh[:, :], p.masks[:, 2 * IB:2 * IB + 1], None, ALU.mult))
                step(dve.scalar_tensor_tensor(out=base[:, :], in0=kl[:, :], scalar=p.masks[:, 2 * IB + 1:2 * IB + 2],
                                              in1=base[:, :], op0=ALU.mult, op1=ALU.add))
                for t in range(IB):
                    step(dve.scalar_tensor_tensor(out=p.const_rows[:, t, :], in0=p.vh[0:64, :],
                                                  scalar=p.masks[0:64, t:t + 1], in1=base[0:64, :],
                                                  op0=ALU.mult, op1=ALU.add))
                    step(dve.scalar_tensor_tensor(out=p.const_rows[:, t, :], in0=p.vl[0:64, :],
                                                  scalar=p.masks[0:64, IB + t:IB + t + 1], in1=p.const_rows[:, t, :],
                                                  op0=ALU.mult, op1=ALU.add))
                dve.wait_ge(prod, 4)
                step(dve.tensor_copy(p.s_rows[:, :], psH[0:4, :]))
                n = 0
                for kt in range(KT):
                    for t in range(KT):
                        dve.wait_ge(prod, 5 + n)
                        n += 1
                        dve.tensor_scalar(p.r64[:, kt, t * 128:(t + 1) * 128], psT[:, 0:128], 1.0 / WS, None,
                                          ALU.mult).then_inc(evac, 1)
                dve.wait_ge(rstd_ready, 2)
                for q in range(2):
                    step(dve.tensor_copy(halves[:, q, 0, :], rstd[:, q, :]))
                    step(dve.tensor_tensor(halves[:, q, 1, :], rstd[:, q, :], halves[:, q, 0, :], ALU.subtract))
                dve.sem_inc(halves_ready, 1)


def project0(nc, p, io):
    N, KT, NB = p.N, p.KT, p.NB
    NK = 3 * IB + 2
    with ExitStack() as ctx:
        sb = lambda n, s, d: ctx.enter_context(nc.sbuf_tensor("pj_" + n, s, d))
        x = [sb(f"x{k}", [C, IB, N], F32) for k in range(2)]
        yh = [sb(f"yh{k}", [C, IB, 128], F16) for k in range(2)]
        yl = [sb(f"yl{k}", [C, IB, 128], F16) for k in range(2)]
        std = [sb(f"std{k}", [64, N], F16) for k in range(2)]
        r_body = sb("r_body", [128, KT, 2 * IB], F32)
        sig = sb("sig", [128, 8, 2 * C], F32)
        prod = sb("prod", [128, 8, 2, C], F32)
        stage_a = [sb(f"stage_a{k}", [128, NCH, IB, CH, 2], F16) for k in range(2)]
        stage_b = [sb(f"stage_b{k}", [128, NCH, 2, CH, IB], F16) for k in range(2)]
        bank = [ctx.enter_context(nc.psum_tensor(f"bank{k}", [128, 4 * C], F32)) for k in range(8)]
        x_loaded = [p.sem(f"x_loaded{k}") for k in range(2)]
        split = p.sem("y_split")
        projected = p.sem("projected")
        sig_done = p.sem("sig_done")
        prod_done = p.sem("prod_done")
        hi_done = p.sem("ab_hi_done")
        lo_a = p.sem("a_lo_done")
        lo_b = p.sem("b_lo_done")
        stored = [p.sem(f"ab_stored{k}") for k in range(2)]
        ones_set = p.sem("ones_set")
        yh_done = p.sem("yh_done")
        r_copied = p.sem("r_copied")
        CREDIT = 2 * IB

        BODY = 2 * KT
        TILES = BODY * IB
        BATCH = TILES // QT
        BODIES = NB // 2

        def staged(b, ab, half, m):
            return batch_of(stage_b[b % 2] if ab else stage_a[b % 2], ab, half, m % (IB // QT))

        with nc.Block() as block:
            @block.sync
            def _(sp):
                def load(row, k):
                    sp.dma_start(x[k][:, :, :], io["x"][:, bass.ds(row * IB, IB), :]).then_inc(x_loaded[k], 16)
                    for h in range(3):
                        sp.dma_start(std[k][h * IB:(h + 1) * IB, :],
                                     p.std_rows[h, bass.ds(row * IB, IB), :]).then_inc(x_loaded[k], 16)

                def store(i, b):
                    sp.wait_ge(lo_a, i * BATCH + (b + 1) * IB // QT)
                    sp.wait_ge(lo_b, i * BATCH + (b + 1) * IB // QT)
                    for stage, dst in ((stage_a, p.a_parts), (stage_b, p.b_parts)):
                        store_stage(sp, stage[b % 2], dst, b % KT, 2 * i + b // KT).then_inc(stored[b % 2], 16)
                sp.wait_ge(ones_set, 1)
                for k in range(2):
                    load(k, k)

                def body(i, more):
                    for b in range(BODY):
                        store(i, b)
                        if more and b % KT == KT - 1:
                            k = b // KT
                            load(2 * i + 2 + k, k)
                with sp.Fori(0, BODIES - 1) as i:
                    body(i, True)
                body(BODIES - 1, False)
                for k in range(2):
                    sp.wait_ge(stored[k], 32 * (BODIES * BODY // 2 + 1))

            @block.vector
            def _(dve):
                for k in range(2):
                    last = dve.memset(std[k][32:64, :], 1.0)
                last.then_inc(ones_set, 1)
                dve.sem_inc(prod_done, 8)

                def split_block(i, b):
                    k, kt = (b // KT) % 2, b % KT
                    it = i + (b // BODY)
                    if b % KT == 0:
                        dve.wait_ge(x_loaded[k], (it + 1) * 64)
                    blk = i * BODY + b
                    dve.wait_ge(projected, blk * IB + IB)
                    src = x[k][:, :, kt * 128:(kt + 1) * 128]
                    dve.tensor_scalar(yh[b % 2][:, :, :], src, p.st0[:, 0:1], None, ALU.mult).then_inc(yh_done, 1)
                    dve.wait_ge(yh_done, blk + 1)
                    dve.scalar_tensor_tensor(out=yl[b % 2][:, :, :], in0=src, scalar=p.st0[:, 0:1],
                                             in1=yh[b % 2][:, :, :], op0=ALU.mult, op1=ALU.subtract
                                             ).then_inc(split, 1)

                def lo_of_a(i, m):
                    b = m // (IB // QT)
                    dve.wait_ge(hi_done, i * BATCH + m + 1)
                    slot = QT * (m % 2)
                    dve.tensor_tensor(staged(b, 0, 1, m),
                                      prod[:, slot:slot + QT, 0, :].rearrange("p i (h c) -> p i h c", c=CH),
                                      staged(b, 0, 0, m), ALU.subtract).then_inc(lo_a, 1)

                def body(i, more):
                    dve.tensor_copy(r_body[:, :, :], p.r64[:, :, bass.ds(i * (2 * IB), 2 * IB)]).then_inc(r_copied, 1)
                    dve.wait_ge(r_copied, i + 1)
                    for b in range(BODY):
                        k, kt = b // KT, b % KT
                        for m in range(b * IB // QT, (b + 1) * IB // QT):
                            if m >= 2:
                                dve.wait_ge(lo_b, i * BATCH + m - 1)
                                dve.wait_ge(lo_a, i * BATCH + m - 1)
                            for q in range(QT):
                                n = m * QT + q
                                dve.wait_ge(sig_done, i * TILES + n + 1)
                                dve.scalar_tensor_tensor(
                                    out=prod[:, n % 8, :, :].rearrange("p s c -> p (s c)"),
                                    in0=bank[n % 8][:, 2 * C:4 * C],
                                    scalar=r_body[:, kt, k * IB + n % IB:k * IB + n % IB + 1],
                                    in1=sig[:, n % 8, :], op0=ALU.mult, op1=ALU.mult).then_inc(prod_done, 1)
                            if m >= 1:
                                lo_of_a(i, m - 1)
                            if m == b * IB // QT + 1 and (more or b + 1 < BODY):
                                split_block(i, b + 1)
                    lo_of_a(i, BATCH - 1)
                    dve.wait_ge(lo_b, i * BATCH + BATCH)
                    dve.wait_ge(lo_a, i * BATCH + BATCH)
                split_block(0, 0)
                with dve.Fori(0, BODIES - 1) as i:
                    body(i, True)
                body(BODIES - 1, False)

            @block.gpsimd
            def _(pool):
                def body(i):
                    for m in range(BATCH):
                        b = m // (IB // QT)
                        pool.wait_ge(hi_done, i * BATCH + m + 1)
                        slot = QT * (m % 2)
                        pool.tensor_tensor(staged(b, 1, 1, m),
                                           prod[:, slot:slot + QT, 1, :].rearrange("p i (h c) -> p i h c", c=CH),
                                           staged(b, 1, 0, m), ALU.subtract).then_inc(lo_b, 1)
                with pool.Fori(0, BODIES) as i:
                    body(i)

            @block.scalar
            def _(act):
                act.sem_inc(stored[0], 32)
                act.sem_inc(stored[1], 32)

                def hi_of(i, m):
                    b = m // (IB // QT)
                    if m % (IB // QT) == 0:
                        act.wait_ge(stored[b % 2], (i * (BODY // 2) + b // 2 + 1) * 32)
                    act.wait_ge(prod_done, i * TILES + (m + 1) * QT + 8)
                    slot = QT * (m % 2)
                    for ab in range(2):
                        last = act.activation(staged(b, ab, 0, m),
                                              prod[:, slot:slot + QT, ab, :].rearrange("p i (h c) -> p i h c", c=CH),
                                              ACT.Copy)
                    last.then_inc(hi_done, 1)

                with act.Fori(0, BODIES) as i:
                    act.wait_ge(r_copied, i + 1)
                    for m in range(BATCH):
                        for q in range(QT):
                            n = m * QT + q
                            kt, at = (n // IB) % KT, n // (IB * KT) * IB + n % IB
                            act.wait_ge(projected, i * TILES + (n + 1 + CREDIT))
                            act.activation(sig[:, n % 8, :], bank[n % 8][:, 0:2 * C], ACT.Sigmoid,
                                           scale=r_body[:, kt, at:at + 1]).then_inc(sig_done, 1)
                        if m:
                            hi_of(i, m - 1)
                    hi_of(i, BATCH - 1)

            @block.tensor
            def _(pe):
                pe.sem_inc(projected, CREDIT)
                with pe.Fori(0, BODIES) as i:
                    for b in range(BODY):
                        k, kt = b // KT, b % KT
                        pe.wait_ge(split, i * BODY + b + 1)
                        for t in range(IB):
                            n = b * IB + t
                            out = bank[n % 8][:, :]
                            pe.wait_ge(prod_done, i * TILES + n + 1)
                            pe.matmul(out, lhsT=yh[b % 2][:, t, :], rhs=p.wh[:, :], start=True, stop=False)
                            pe.matmul(out, lhsT=yh[b % 2][:, t, :], rhs=p.wl[:, :], start=False, stop=False)
                            pe.matmul(out, lhsT=yl[b % 2][:, t, :], rhs=p.wh[:, :], start=False, stop=False)
                            pe.matmul(out, lhsT=std[k][0:NK, kt * 128:(kt + 1) * 128],
                                      rhs=p.const_rows[0:NK, t, :], start=False, stop=True).then_inc(projected, 1)


def mix(nc, p, name, out, residual):
    N, KT, NB = p.N, p.KT, p.NB
    ROW = KT * N
    with ExitStack() as ctx:
        sb = lambda n, s, d: ctx.enter_context(nc.sbuf_tensor(name + n, s, d))
        pa = [sb(f"pa{k}", [128, KT, N, CH, 2], F16) for k in range(2)]
        pb = [sb(f"pb{k}", [128, KT, NB, 2, CH, IB], F16) for k in range(2)]
        res = [sb(f"res{k}", [128, KT, N], F32) for k in range(2)]
        o = [sb(f"o{k}", [128, KT, N], F32) for k in range(2)]
        bank = [[ctx.enter_context(nc.psum_tensor(f"{name}bank{k}_{t}", [128, 512], F32)) for t in range(KT)]
                for k in range(2)]
        loaded = [p.sem(f"{name}_parts_loaded{k}") for k in range(2)]
        res_loaded = [p.sem(f"{name}_res_loaded{k}") for k in range(2)]
        mixed = p.sem(f"{name}_mixed")
        evacuated = p.sem(f"{name}_evacuated")
        stored = [p.sem(f"{name}_stored{k}") for k in range(2)]
        out_v = out.rearrange("c (t p) j -> c p t j", p=128)
        sums = residual is None
        if sums:
            sq = [sb(f"sq{k}", [128, ROW], F32) for k in range(2)]
            S1 = sb("S1", [128, ROW], F32)
            S2 = sb("S2", [128, ROW], F32)
            expos = res[1][:, :, :].rearrange("p t j -> p (t j)")
            halves = sb("halves", [128, 2, ROW], F16)
            sq_ready = p.sem(f"{name}_sq_ready")
            s1_added = p.sem(f"{name}_s1_added")
            s2_added = p.sem(f"{name}_s2_added")
            var_ready = p.sem(f"{name}_var_ready")
            r_ready = p.sem(f"{name}_r_ready")
            tail = p.sem(f"{name}_tail")
            halves_ready = p.sem(f"{name}_halves_ready")
            rows_stored = p.sem(f"{name}_rows_stored")
            init = p.sem(f"{name}_init")
        else:
            res_v = residual.rearrange("c (t p) j -> c p t j", p=128)
            st = sb("st", [128, 2, 2 * CH], F32)
            scaled = p.sem(f"{name}_residual_scaled")
            st_ready = p.sem(f"{name}_factors_ready")
        BODY = 2 * CH
        BODIES = NCH // 2

        def flat(t3):
            return t3[:, :, :].rearrange("p t j -> p (t j)")

        with nc.Block() as block:
            @block.sync
            def _(sp):
                def load(chunk, k):
                    for kt in range(KT):
                        sp.dma_start(pa[k][:, kt, :, :, :].rearrange("p i c q -> p (i c q)"),
                                     p.a_parts[chunk, kt].rearrange("p b n -> p (b n)")).then_inc(loaded[k], 16)
                        sp.dma_start(pb[k][:, kt, :, :, :, :].rearrange("p b q c i -> p (b q c i)"),
                                     p.b_parts[chunk, kt].rearrange("p b n -> p (b n)")).then_inc(loaded[k], 16)
                for k in range(2):
                    load(k, k)
                if not sums:
                    for k in range(2):
                        sp.dma_start(res[k][:, :, :], res_v[k]).then_inc(res_loaded[k], 16)

                def body(i, more):
                    for n in range(BODY):
                        sp.wait_ge(evacuated, i * BODY + n + 3)
                        sp.dma_start(out_v[i * BODY + n], o[n % 2][:, :, :]).then_inc(stored[n % 2], 16)
                        if not sums and (more or n + 2 < BODY):
                            sp.dma_start(res[n % 2][:, :, :], res_v[i * BODY + n + 2]).then_inc(res_loaded[n % 2], 16)
                        if more and n % CH == CH - 1:
                            load(2 * i + 2 + n // CH, n // CH)
                with sp.Fori(0, BODIES - 1) as i:
                    body(i, True)
                body(BODIES - 1, False)
                if sums:
                    sp.wait_ge(halves_ready, 1)
                    for row in range(2):
                        sp.dma_start(p.r2_rows[row].rearrange("(t p) k -> p t k", p=128),
                                     halves[:, row, :].rearrange("p (t k) -> p t k", t=KT)).then_inc(rows_stored, 16)
                    sp.wait_ge(rows_stored, 32)
                for k in range(2):
                    sp.wait_ge(stored[k], 16 * (C // 2 + 1))

            @block.tensor
            def _(pe):
                with pe.Fori(0, BODIES) as i:
                    for n in range(BODY):
                        k, c = n // CH, n % CH
                        if c == 0:
                            pe.wait_ge(loaded[k], (i + 1) * (32 * KT))
                        pe.wait_ge(evacuated, i * BODY + n + 1)
                        for t in range(KT):
                            dst = bank[n % 2][t][:, 0:N]
                            for kt in range(KT):
                                a_hi, a_lo = (pa[k][:, kt, t * 128:(t + 1) * 128, c, q] for q in (0, 1))
                                b_hi, b_lo = (pb[k][:, kt, :, q, c, :] for q in (0, 1))
                                pe.matmul(dst, lhsT=a_hi, rhs=b_hi, start=(kt == 0), stop=False)
                                pe.matmul(dst, lhsT=a_hi, rhs=b_lo, start=False, stop=False)
                                last = pe.matmul(dst, lhsT=a_lo, rhs=b_hi, start=False, stop=(kt == KT - 1))
                            last.then_inc(mixed, 1)

            if sums:
                @block.scalar
                def _(act):
                    act.sem_inc(evacuated, 2)
                    act.sem_inc(stored[0], 16)
                    act.sem_inc(stored[1], 16)
                    with act.Fori(0, BODIES) as i:
                        for n in range(BODY):
                            act.wait_ge(stored[n % 2], (i * (BODY // 2) + n // 2 + 1) * 16)
                            act.wait_ge(s1_added, i * BODY + n + 1)
                            for t in range(KT):
                                act.wait_ge(mixed, i * (BODY * KT) + n * KT + t + 1)
                                last = act.activation(o[n % 2][:, t, :], bank[n % 2][t][:, 0:N], ACT.Copy)
                            last.then_inc(evacuated, 1)
                            act.wait_ge(evacuated, i * BODY + n + 3)
                            act.wait_ge(s2_added, i * BODY + n + 1)
                            act.activation(sq[n % 2][:, :], flat(o[n % 2]), ACT.Square).then_inc(sq_ready, 1)

                @block.gpsimd
                def _(pool):
                    pool.memset(S2[:, :], 0.0).then_inc(init, 1)
                    pool.memset(expos, -0.5).then_inc(init, 1)
                    pool.wait_ge(init, 2)
                    pool.sem_inc(s2_added, 2)
                    with pool.Fori(0, BODIES) as i:
                        for n in range(BODY):
                            pool.wait_ge(sq_ready, i * BODY + n + 1)
                            pool.tensor_tensor(S2[:, :], S2[:, :], sq[n % 2][:, :], ALU.add).then_inc(s2_added, 1)
                            pool.wait_ge(s2_added, i * BODY + n + 3)
                    pool.wait_ge(var_ready, 1)
                    pool.tensor_tensor(sq[0][:, :], sq[1][:, :], expos, ALU.pow).then_inc(r_ready, 1)

                @block.vector
                def _(dve):
                    dve.memset(S1[:, :], 0.0).then_inc(tail, 1)
                    dve.wait_ge(tail, 1)
                    dve.sem_inc(s1_added, 2)
                    with dve.Fori(0, BODIES) as i:
                        for n in range(BODY):
                            dve.wait_ge(evacuated, i * BODY + n + 3)
                            dve.tensor_tensor(S1[:, :], S1[:, :], flat(o[n % 2]), ALU.add).then_inc(s1_added, 1)
                            dve.wait_ge(s1_added, i * BODY + n + 3)
                    count = [1]

                    def step(ins):
                        count[0] += 1
                        ins.then_inc(tail, 1)
                        dve.wait_ge(tail, count[0])
                    dve.wait_ge(s2_added, C + 2)
                    step(dve.tensor_scalar(S1[:, :], S1[:, :], 1.0 / C, None, ALU.mult))
                    step(dve.tensor_tensor(S1[:, :], S1[:, :], S1[:, :], ALU.mult))
                    step(dve.scalar_tensor_tensor(out=sq[1][:, :], in0=S2[:, :], scalar=1.0 / C, in1=S1[:, :],
                                                  op0=ALU.mult, op1=ALU.subtract))
                    dve.tensor_scalar(sq[1][:, :], sq[1][:, :], 0.0, EPS, ALU.max, ALU.add).then_inc(var_ready, 1)
                    dve.wait_ge(r_ready, 1)
                    step(dve.tensor_copy(halves[:, 0, :], sq[0][:, :]))
                    step(dve.tensor_tensor(halves[:, 1, :], sq[0][:, :], halves[:, 0, :], ALU.subtract))
                    dve.sem_inc(halves_ready, 1)
            else:
                @block.scalar
                def _(act):
                    with act.Fori(0, BODIES) as i:
                        act.wait_ge(scaled, i * BODY + 1)
                        act.activation(st[:, :, :], p.res_st[:, :, bass.ds(i * BODY, BODY)], ACT.Copy).then_inc(st_ready, 1)
                        act.wait_ge(st_ready, i + 1)
                        for n in range(BODY):
                            act.wait_ge(res_loaded[n % 2], (i * (BODY // 2) + n // 2 + 1) * 16)
                            act.activation(flat(res[n % 2]), flat(res[n % 2]), ACT.Identity, scale=st[:, 0, n:n + 1],
                                           bias=st[:, 1, n:n + 1]).then_inc(scaled, 1)

                @block.vector
                def _(dve):
                    dve.sem_inc(evacuated, 2)
                    dve.sem_inc(scaled, 1)
                    dve.sem_inc(stored[0], 16)
                    dve.sem_inc(stored[1], 16)
                    with dve.Fori(0, BODIES) as i:
                        for n in range(BODY):
                            dve.wait_ge(stored[n % 2], (i * (BODY // 2) + n // 2 + 1) * 16)
                            dve.wait_ge(scaled, i * BODY + (n + 2))
                            for t in range(KT):
                                dve.wait_ge(mixed, i * (BODY * KT) + n * KT + t + 1)
                                last = dve.tensor_tensor(o[n % 2][:, t, :], bank[n % 2][t][:, 0:N],
                                                         res[n % 2][:, t, :], ALU.add)
                            last.then_inc(evacuated, 1)


def join0(nc, p, io):
    N = p.N
    SUB = 512
    RING = 4
    TOK = 3 * SUB if (N * N) % (3 * RING * SUB) == 0 else 2 * SUB
    NS = TOK // SUB
    TILES = N * N // TOK
    BODIES = TILES // RING
    with ExitStack() as ctx:
        sb = lambda n, s, d: ctx.enter_context(nc.sbuf_tensor("join_" + n, s, d))
        ring = lambda n, s, d: [sb(f"{n}{k}", s, d) for k in range(RING)]
        two = lambda n, s, d: [sb(f"{n}{k}", s, d) for k in range(2)]
        x = ring("x", [C, TOK], F32)
        ab = ring("ab", [C, TOK], F32)
        r1 = ring("r1", [4, TOK], F16)
        r2 = ring("r2", [2, TOK], F16)
        yn = two("yn", [C, TOK], F32)
        yh = two("yh", [C, TOK], F16)
        yl = two("yl", [C, TOK], F16)
        zn = two("zn", [C, TOK], F32)
        zh = two("zh", [C, TOK], F16)
        zl = two("zl", [C, TOK], F16)
        gate = two("gate", [C, TOK], F32)
        x1 = two("x1", [C, TOK], F32)
        square = sb("square", [C, TOK], F32)
        sum_x1 = sb("sum_x1", [C, TILES], F32)
        sum_sq = sb("sum_sq", [C, TILES], F32)
        ones2 = sb("ones2", [2, C], F16)
        tot = sb("tot", [C, 8], F32)
        t_bc = sb("t_bc", [C, C], F32)
        diag = sb("diag", [C, 2, C], F32)
        psr = [ctx.enter_context(nc.psum_tensor(f"psr{k}", [128, SUB], F32)) for k in range(4)]
        psz = [ctx.enter_context(nc.psum_tensor(f"psz{k}", [128, SUB], F32)) for k in range(4)]
        loaded = [p.sem(f"join_loaded{k}") for k in range(RING)]
        spread = p.sem("join_r_spread")
        normed = p.sem("join_normed")
        hi = p.sem("join_hi")
        lo = p.sem("join_lo")
        prods = p.sem("join_products")
        gated = p.sem("join_gated")
        mul = p.sem("join_times_gate")
        done = p.sem("join_x1_done")
        squared = p.sem("join_squared")
        stored = [p.sem(f"join_stored{k}") for k in range(2)]
        ones_set = p.sem("join_ones_set")
        tail = p.sem("join_tail_step")
        operand = p.sem("join_tail_operand")
        tail_prod = p.sem("join_tail_product")
        s_ready = p.sem("join_s_ready")
        xf = io["x"].rearrange("c i k -> c (i k)")
        abf = p.ab.rearrange("c i k -> c (i k)")
        x1f = p.x1.rearrange("c i k -> c (i k)")
        r1f = p.r1_rows.rearrange("r i k -> r (i k)")
        r2f = p.r2_rows.rearrange("r i k -> r (i k)")
        NORM0, LO0, PROD0, MUL0, SQ0 = 4, 4, 4 * NS, 2, 2

        def cut(u):
            return slice(u * SUB, (u + 1) * SUB)

        def over_tiles(engine, step):
            for k in range(RING):
                step(0, k, k == 0, False)
            with engine.Fori(1, BODIES - 1) as i:
                for k in range(RING):
                    step(i, k, False, False)
            for k in range(RING):
                step(BODIES - 1, k, False, k == RING - 1)

        with nc.Block() as block:
            @block.sync
            def _(sp):
                def load(t, k):
                    at = bass.ds(t * TOK, TOK)
                    sp.dma_start(x[k][:, :], xf[:, at]).then_inc(loaded[k], 16)
                    sp.dma_start(ab[k][:, :], abf[:, at]).then_inc(loaded[k], 16)
                    sp.dma_start(r1[k][0:3, :], r1f[:, at]).then_inc(loaded[k], 16)
                    sp.dma_start(r2[k][:, :], r2f[:, at]).then_inc(loaded[k], 16)
                for k in range(RING):
                    load(k, k)

                def body(i, more):
                    for k in range(RING):
                        sp.wait_ge(done, i * RING + k + 1)
                        sp.dma_start(x1f[:, bass.ds((i * RING + k) * TOK, TOK)],
                                     x1[k % 2][:, :]).then_inc(stored[k % 2], 16)
                        if more:
                            load(i * RING + k + RING, k)
                with sp.Fori(0, BODIES - 1) as i:
                    body(i, True)
                body(BODIES - 1, False)
                for k in range(2):
                    sp.wait_ge(stored[k], 16 * (TILES // 2 + 1))

            @block.tensor
            def _(pe):
                pe.wait_ge(ones_set, 1)
                pe.sem_inc(prods, PROD0)

                def spread_r(i, k):
                    t = RING * i + k
                    pe.wait_ge(loaded[k], (i + 1) * 64)
                    for u in range(NS):
                        bank = 2 * ((NS * k + u) % 2)
                        pe.wait_ge(normed, t * (2 * NS) + 2 * u + (NORM0 - 2))
                        pe.matmul(psr[bank][:, :], lhsT=p.s_rows[0:3, :], rhs=r1[k][0:3, cut(u)],
                                  start=True, stop=True).then_inc(spread, 1)
                        pe.matmul(psr[bank + 1][:, :], lhsT=ones2[:, :], rhs=r2[k][:, cut(u)],
                                  start=True, stop=True).then_inc(spread, 1)

                def products(i, k):
                    t, h = RING * i + k, k % 2
                    pe.wait_ge(lo, t * 2 + (2 + LO0))
                    for u in range(NS):
                        bank = 2 * ((NS * k + u) % 2)
                        pe.wait_ge(mul, t * NS + (u - 1 + MUL0))
                        for q, (wh, wl, vh, vl) in enumerate(((p.gh, p.gl, yh, yl), (p.ah, p.al, zh, zl))):
                            dst = psz[bank + q][:, :]
                            pe.matmul(dst, lhsT=wh[:, :], rhs=vh[h][:, cut(u)], start=True, stop=False)
                            pe.matmul(dst, lhsT=wh[:, :], rhs=vl[h][:, cut(u)], start=False, stop=False)
                            pe.matmul(dst, lhsT=wl[:, :], rhs=vh[h][:, cut(u)], start=False, stop=True
                                      ).then_inc(prods, 1)

                def step(i, k, is_first, is_last):
                    if is_first:
                        spread_r(0, 0)
                    if not is_last:
                        spread_r(*after(i, k))
                    products(i, k)
                over_tiles(pe, step)
                pe.wait_ge(operand, 1)
                pe.matmul(psr[0][:, 0:2], lhsT=p.group_mat[:, :], rhs=tot[:, 0:2],
                          start=True, stop=True).then_inc(tail_prod, 1)
                pe.wait_ge(operand, 3)
                for q, w in enumerate((p.wa_t, p.wb_t)):
                    pe.matmul(psr[1 + q][:, 0:C], lhsT=t_bc[:, :], rhs=w[:, :], start=True, stop=False)
                    pe.matmul(psr[1 + q][:, 0:C], lhsT=p.ones[0:1, :], rhs=p.bias_ab[0:1, q * C:(q + 1) * C],
                              start=False, stop=True).then_inc(tail_prod, 1)
                pe.wait_ge(operand, 4)
                pe.matmul(psr[3][:, 0:2 * C], lhsT=p.ones[:, :], rhs=diag[:, :, :].rearrange("p q c -> p (q c)"),
                          start=True, stop=True).then_inc(tail_prod, 1)

            @block.scalar
            def _(act):
                act.sem_inc(squared, SQ0)

                def halves(i, k):
                    t, h = RING * i + k, k % 2
                    act.wait_ge(prods, t * (2 * NS) + (PROD0 - 2 * NS))
                    act.wait_ge(normed, t * (2 * NS) + (2 * NS + NORM0))
                    act.activation(yh[h][:, :], yn[h][:, :], ACT.Copy).then_inc(hi, 1)
                    act.activation(zh[h][:, :], zn[h][:, :], ACT.Copy).then_inc(hi, 1)

                def gates(i, k):
                    t, h = RING * i + k, k % 2
                    for u in range(NS):
                        bank = 2 * ((NS * k + u) % 2)
                        act.wait_ge(prods, t * (2 * NS) + (2 * u + 1 + PROD0))
                        act.activation(gate[h][:, cut(u)], psz[bank][:, :], ACT.Sigmoid,
                                       scale=1.0 / WS, bias=p.vg[:, :]).then_inc(gated, 1)

                def squares(i, k):
                    t = RING * i + k
                    act.wait_ge(done, t + 1)
                    act.wait_ge(squared, t + SQ0)
                    act.activation(square[:, :], x1[k % 2][:, :], ACT.Square,
                                   accum_out=sum_sq[:, bass.ds(t, 1)]).then_inc(squared, 1)

                def step(i, k, is_first, is_last):
                    if is_first:
                        halves(0, 0)
                    if not is_last:
                        halves(*after(i, k))
                    if not is_first:
                        squares(*before(i, k))
                    gates(i, k)
                    if is_last:
                        squares(i, k)
                over_tiles(act, step)

            @block.gpsimd
            def _(pool):
                pool.sem_inc(lo, LO0)
                with pool.Fori(0, BODIES) as i:
                    for k in range(RING):
                        for q, (src, h, dst) in enumerate(((yn, yh, yl), (zn, zh, zl))):
                            pool.wait_ge(hi, (RING * i + k) * 2 + (q + 1))
                            pool.tensor_tensor(dst[k % 2][:, :], src[k % 2][:, :], h[k % 2][:, :],
                                               ALU.subtract).then_inc(lo, 1)
                pool.wait_ge(operand, 2)
                pool.tensor_tensor(tot[:, 4:5], tot[:, 3:4], tot[:, 5:6], ALU.pow).then_inc(s_ready, 1)

            @block.vector
            def _(dve):
                dve.memset(ones2[:, :], 1.0).then_inc(ones_set, 1)
                dve.sem_inc(normed, NORM0)
                dve.sem_inc(mul, MUL0)
                dve.sem_inc(stored[0], 16)
                dve.sem_inc(stored[1], 16)

                def norm(i, k):
                    t, h = RING * i + k, k % 2
                    dve.wait_ge(loaded[k], (i + 1) * 64)
                    dve.wait_ge(lo, t * 2 + (LO0 - 2))
                    for u in range(NS):
                        bank = 2 * ((NS * k + u) % 2)
                        dve.wait_ge(spread, t * (2 * NS) + (2 * u + 1))
                        dve.scalar_tensor_tensor(out=yn[h][:, cut(u)], in0=x[k][:, cut(u)], scalar=p.st0[:, 2:3],
                                                 in1=psr[bank][:, :], op0=ALU.add, op1=ALU.mult).then_inc(normed, 1)
                        dve.wait_ge(spread, t * (2 * NS) + (2 * u + 2))
                        dve.tensor_tensor(zn[h][:, cut(u)], ab[k][:, cut(u)], psr[bank + 1][:, :],
                                          ALU.mult).then_inc(normed, 1)

                def finish(i, k):
                    t, h = RING * i + k, k % 2
                    for u in range(NS):
                        bank = 2 * ((NS * k + u) % 2)
                        dve.wait_ge(gated, t * NS + (u + 1))
                        dve.wait_ge(prods, t * (2 * NS) + (2 * u + 2 + PROD0))
                        dve.scalar_tensor_tensor(out=gate[h][:, cut(u)], in0=psz[bank + 1][:, :], scalar=p.v2[:, :],
                                                 in1=gate[h][:, cut(u)], op0=ALU.add, op1=ALU.mult).then_inc(mul, 1)
                    dve.wait_ge(mul, t * NS + (NS + MUL0))
                    dve.wait_ge(stored[h], (i * (RING // 2) + k // 2 + 1) * 16)
                    dve.wait_ge(squared, t + (SQ0 - 1))
                    dve.scalar_tensor_tensor(out=x1[h][:, :], in0=gate[h][:, :], scalar=1.0 / WS, in1=x[k][:, :],
                                             op0=ALU.mult, op1=ALU.add,
                                             accum_out=sum_x1[:, bass.ds(t, 1)]).then_inc(done, 1)

                def step(i, k, is_first, is_last):
                    if is_first:
                        norm(0, 0)
                    if not is_last:
                        norm(*after(i, k))
                    finish(i, k)
                over_tiles(dve, step)

                chain = chained(dve, tail)
                dve.wait_ge(squared, TILES + SQ0)
                dve.wait_ge(done, TILES)
                chain(dve.tensor_reduce(tot[:, 0:1], sum_x1[:, :], axis=AX.X, op=ALU.add))
                chain(dve.tensor_reduce(tot[:, 1:2], sum_sq[:, :], axis=AX.X, op=ALU.add))
                chain(dve.tensor_scalar(tot[:, 0:2], tot[:, 0:2], 1.0 / (N * N), None, ALU.mult))
                dve.sem_inc(operand, 1)
                dve.wait_ge(tail_prod, 1)
                chain(dve.tensor_copy(tot[:, 2:3], psr[0][:, 0:1]))
                chain(dve.tensor_tensor(tot[:, 6:7], tot[:, 2:3], tot[:, 2:3], ALU.mult))
                chain(dve.tensor_tensor(tot[:, 3:4], psr[0][:, 1:2], tot[:, 6:7], ALU.subtract))
                chain(dve.tensor_scalar(tot[:, 3:4], tot[:, 3:4], 0.0, EPS, ALU.max, ALU.add))
                chain(dve.memset(tot[:, 5:6], -0.5))
                dve.sem_inc(operand, 1)
                chain(dve.tensor_scalar(tot[:, 7:8], tot[:, 2:3], -1.0, None, ALU.mult))
                dve.wait_ge(s_ready, 1)
                chain(dve.tensor_copy(p.st1[:, 0:1], tot[:, 4:5]))
                chain(dve.tensor_tensor(p.st1[:, 1:2], tot[:, 7:8], tot[:, 4:5], ALU.mult))
                chain(dve.tensor_scalar(t_bc[:, :], p.ones[:, :], p.st1[:, 1:2], None, ALU.mult))
                dve.sem_inc(operand, 1)
                dve.wait_ge(tail_prod, 3)
                for q in range(2):
                    for u in range(QT):
                        chain(dve.tensor_copy(p.const1[:, q, u, :], psr[1 + q][:, 0:C]))
                for q in range(2):
                    chain(dve.tensor_scalar(diag[:, q, :], p.ident[:, :], p.st1[:, q:q + 1], None, ALU.mult))
                dve.sem_inc(operand, 1)
                dve.wait_ge(tail_prod, 4)
                chain(dve.tensor_scalar(p.res_st[:, 0, :], psr[3][:, 0:C], 1.0, None, ALU.add))
                chain(dve.tensor_copy(p.res_st[:, 1, :], psr[3][:, C:2 * C]))


def project1(nc, p):
    KT = p.KT
    G = 128 // IB
    with ExitStack() as ctx:
        sb = lambda n, s, d: ctx.enter_context(nc.sbuf_tensor("sq_" + n, s, d))
        XR, SR = 4, 4
        x = [sb(f"x{k}", [C, IB, 128], F32) for k in range(XR)]
        yh = sb("yh", [C, 128, 128], F16)
        yl = sb("yl", [C, 128, 128], F16)
        value = [sb(f"value{k}", [128, QT, C], F32) for k in range(4)]
        stage = [sb(f"stage{k}", [128, NCH, 2 * CH * IB], F16) for k in range(SR)]
        bank = [ctx.enter_context(nc.psum_tensor(f"sqbank{k}", [128, QT, C], F32)) for k in range(8)]
        loaded = [p.sem(f"sq_loaded{k}") for k in range(XR)]
        x_hi = p.sem("sq_x_hi")
        x_lo = p.sem("sq_x_lo")
        projected = p.sem("sq_projected")
        valued = p.sem("sq_valued")
        v_hi = p.sem("sq_value_hi")
        v_lo = p.sem("sq_value_lo")
        stored = [p.sem(f"sq_stored{k}") for k in range(SR)]
        B = IB // QT
        BATCHES = 2 * G * B
        VAL0, LO0, PROJ0 = 8, 4, 1

        def squares(engine, body):
            with engine.Fori(0, KT) as it:
                with engine.Fori(0, KT) as kt:
                    body(it, kt, it * KT + kt)

        def stage_halves(g, half, m):
            tile = stage[g % SR][:, :, :]
            if g < G:
                return batch_of(tile.rearrange("p h (i c q) -> p h i c q", c=CH, q=2), 0, half, m)
            return batch_of(tile.rearrange("p h (q c i) -> p h q c i", q=2, c=CH), 1, half, m)

        def value_of(batch):
            return value[batch % 4][:, :, :].rearrange("p i (h c) -> p i h c", c=CH)

        with nc.Block() as block:
            @block.sync
            def _(sp):
                def body(it, kt, q):
                    def load(g):
                        sp.wait_ge(x_lo, q * G + (g + 1))
                        sp.dma_start(x[g % XR][:, :, :],
                                     p.x1[:, bass.ds(it * 128 + g * IB, IB), bass.ds(kt * 128, 128)]
                                     ).then_inc(loaded[g % XR], 16)
                    for g in range(XR):
                        load(g)
                    for g in range(2 * G):
                        sp.wait_ge(v_lo, q * BATCHES + ((g + 1) * B + LO0))
                        parts, rows, blk = (p.b_parts, it, kt * G + (g - G)) if g >= G else (p.a_parts, kt, it * G + g)
                        store_stage(sp, stage[g % SR], parts, rows, blk).then_inc(stored[g % SR], 16)
                        if g + XR < G:
                            load(g + XR)
                squares(sp, body)
                for k in range(SR):
                    sp.wait_ge(stored[k], 16 * (KT * KT * 2 * G // SR + 1))

            @block.tensor
            def _(pe):
                def body(it, kt, q):
                    for g in range(2 * G):
                        right = g >= G
                        if right:
                            wh, wl = p.lbh, p.lbl
                        else:
                            wh, wl = p.lah, p.lal
                            pe.wait_ge(x_lo, q * G + (g + 1 + XR))
                        for m in range(B):
                            n = g * B + m
                            pe.wait_ge(valued, q * BATCHES + (n + 1))
                            for u in range(QT):
                                t = (g % G) * IB + m * QT + u
                                hi = yh[:, :, t] if right else yh[:, t, :]
                                lo = yl[:, :, t] if right else yl[:, t, :]
                                dst = bank[n % 8][:, u, :]
                                pe.matmul(dst, lhsT=hi, rhs=wh[:, :], start=True, stop=False)
                                pe.matmul(dst, lhsT=hi, rhs=wl[:, :], start=False, stop=False)
                                last = pe.matmul(dst, lhsT=lo, rhs=wh[:, :], start=False, stop=True)
                            last.then_inc(projected, 1)
                pe.sem_inc(projected, PROJ0)
                squares(pe, body)

            @block.scalar
            def _(act):
                for k in range(SR):
                    act.sem_inc(stored[k], 16)

                def body(it, kt, q):
                    def split(g):
                        act.wait_ge(loaded[g % XR], (q * (G // XR) + (g // XR + 1)) * 16)
                        if g == 0:
                            act.wait_ge(projected, q * BATCHES + PROJ0)
                        act.activation(yh[:, g * IB:(g + 1) * IB, :], x[g % XR][:, :, :], ACT.Copy,
                                       scale=p.st1[:, 0:1]).then_inc(x_hi, 1)

                    def value_hi(g, m):
                        if m == 0:
                            act.wait_ge(stored[g % SR], (q * (2 * G // SR) + (g // SR + 1)) * 16)
                        n = g * B + m
                        act.wait_ge(valued, q * BATCHES + (n + 1 + VAL0))
                        act.activation(stage_halves(g, 0, m), value_of(n), ACT.Copy).then_inc(v_hi, 1)
                    split(0)
                    for g in range(2 * G):
                        if g + 1 < G:
                            split(g + 1)
                        for m in range(B):
                            value_hi(g, m)
                squares(act, body)

            @block.gpsimd
            def _(pool):
                pool.sem_inc(v_lo, LO0)

                def body(it, kt, q):
                    for g in range(2 * G):
                        for m in range(B):
                            n = g * B + m
                            pool.wait_ge(v_hi, q * BATCHES + (n + 1))
                            pool.tensor_tensor(stage_halves(g, 1, m), value_of(n), stage_halves(g, 0, m),
                                               ALU.subtract).then_inc(v_lo, 1)
                squares(pool, body)

            @block.vector
            def _(dve):
                dve.sem_inc(valued, VAL0)
                dve.sem_inc(x_lo, XR)

                def body(it, kt, q):
                    def split(g):
                        dve.wait_ge(x_hi, q * G + (g + 1))
                        at = slice(g * IB, (g + 1) * IB)
                        dve.scalar_tensor_tensor(out=yl[:, at, :], in0=x[g % XR][:, :, :], scalar=p.st1[:, 0:1],
                                                 in1=yh[:, at, :], op0=ALU.mult, op1=ALU.subtract).then_inc(x_lo, 1)
                    split(0)
                    for g in range(2 * G):
                        if g + 1 < G:
                            split(g + 1)
                        for m in range(B):
                            n = g * B + m
                            dve.wait_ge(v_lo, q * BATCHES + (n + 1))
                            dve.wait_ge(projected, q * BATCHES + (n + 1 + PROJ0))
                            dve.scalar_tensor_tensor(
                                out=value[n % 4][:, :, :].rearrange("p i c -> p (i c)"),
                                in0=bank[n % 8][:, :, :].rearrange("p i c -> p (i c)"), scalar=1.0 / WS,
                                in1=p.const1[:, int(g >= G), :, :].rearrange("p i c -> p (i c)"),
                                op0=ALU.mult, op1=ALU.add).then_inc(valued, 1)
                squares(dve, body)


def batch_of(stage, ab, half, m):
    at = slice(m * QT, (m + 1) * QT)
    if ab:
        return stage[:, :, half, :, at].rearrange("p h c i -> p i h c")
    return stage[:, :, at, :, half].rearrange("p h i c -> p i h c")


def store_stage(engine, stage, parts, k_tile, block):
    src = stage[:]
    if len(src.shape) == 5:
        src = src.rearrange("p h a b c -> p h (a b c)")
    dst = parts[:, bass.ds(k_tile, 1), :, bass.ds(block, 1), :]
    return engine.dma_start(dst.rearrange("h t p b n -> p (h t b) n"), src)


def after(i, k):
    return (i, k + 1) if k < 3 else (i + 1, 0)


def before(i, k):
    return (i, k - 1) if k else (i - 1, 3)


def build(nc, x, ln_vectors, W_proj, W_gate, W_ab, WaT, WbT, bias_ab, identity, centering, group_mean,
          expand, row_masks, out):
    io = dict(x=x, ln_vectors=ln_vectors, W_proj=W_proj, W_gate=W_gate, W_ab=W_ab, WaT=WaT, WbT=WbT,
              bias_ab=bias_ab, identity=identity, centering=centering, group_mean=group_mean,
              expand=expand, row_masks=row_masks)
    p = Plan()
    p.N = x.shape[1]
    p.KT = p.N // 128
    p.NB = p.N // IB
    N, KT = p.N, p.KT
    with ExitStack() as ctx:
        sb = lambda n, s, d: ctx.enter_context(nc.sbuf_tensor(n, s, d))
        p.sem = lambda n: ctx.enter_context(nc.semaphore(n))
        p.a_parts = nc.dram_tensor("a_parts", [NCH, KT, 128, p.NB, 2 * CH * IB], F16, kind="Internal").ap()
        p.b_parts = nc.dram_tensor("b_parts", [NCH, KT, 128, p.NB, 2 * CH * IB], F16, kind="Internal").ap()
        p.ab = nc.dram_tensor("ab_sum", [C, N, N], F32, kind="Internal").ap()
        p.x1 = nc.dram_tensor("x1", [C, N, N], F32, kind="Internal").ap()
        p.r1_rows = nc.dram_tensor("r1_rows", [3, N, N], F16, kind="Internal").ap()
        p.std_rows = nc.dram_tensor("std_rows", [3, N, N], F16, kind="Internal").ap()
        p.r2_rows = nc.dram_tensor("r2_rows", [2, N, N], F16, kind="Internal").ap()
        p.ident = sb("ident", [C, C], F32)
        p.ident16 = sb("ident16", [C, C], F16)
        p.ones = sb("ones", [C, C], F32)
        p.mean_mat = sb("mean_mat", [C, C], F32)
        p.group_mat = sb("group_mat", [C, C], F32)
        p.expand = sb("expand_sb", [NG, C], F32)
        p.wa_t, p.wb_t = sb("wa_t", [C, C], F32), sb("wb_t", [C, C], F32)
        p.bias_ab = sb("bias_sb", [1, 2 * C], F32)
        p.gh, p.gl, p.ah, p.al = (sb(n, [C, C], F16) for n in ("gh", "gl", "ah", "al"))
        p.lah, p.lal, p.lbh, p.lbl = (sb(n, [C, C], F16) for n in ("lah", "lal", "lbh", "lbl"))
        p.vg, p.v2 = sb("vg", [C, 1], F32), sb("v2", [C, 1], F32)
        p.st0 = sb("st0", [C, 4], F32)
        p.st1 = sb("st1", [C, 2], F32)
        p.s_rows = sb("s_rows", [4, C], F16)
        p.res_st = sb("res_st", [128, 2, C], F32)
        p.const1 = sb("const1", [C, 2, QT, C], F32)
        with ExitStack() as first:
            sf = lambda n, s, d: first.enter_context(nc.sbuf_tensor(n, s, d))
            p.wh, p.wl = sf("wh", [C, 4 * C], F16), sf("wl", [C, 4 * C], F16)
            p.r64 = sf("r64", [C, KT, N], F32)
            p.const_rows = sf("const_rows", [64, IB, 4 * C], F16)
            with ExitStack() as prep:
                sp_ = lambda n, s, d: prep.enter_context(nc.sbuf_tensor(n, s, d))
                p.w64 = sp_("w64", [C, 4 * C], F32)
                p.vh, p.vl = sp_("vh", [C, 4 * C], F16), sp_("vl", [C, 4 * C], F16)
                p.masks = sp_("masks", [C, 2 * IB + 2], F32)
                prepare_weights(nc, p, io)
                stats0(nc, p, io)
            project0(nc, p, io)
        mix(nc, p, "mix0_", p.ab, None)
        join0(nc, p, io)
        project1(nc, p)
        mix(nc, p, "mix1_", out, p.x1)


def shape_constants():
    import numpy as np
    eye = np.eye(C, dtype=np.float32)
    group = np.kron(np.eye(NG, dtype=np.float32), np.ones((GROUP, GROUP), np.float32))
    expand = np.kron(np.eye(NG, dtype=np.float32), np.ones((1, GROUP), np.float32))
    masks = np.zeros((C, 2 * IB + 2), np.float32)
    for t in range(IB):
        masks[t, t] = masks[IB + t, t] = 1
        masks[2 * IB + t, IB + t] = 1
    masks[3 * IB, 2 * IB] = masks[3 * IB + 1, 2 * IB + 1] = 1
    return dict(identity=eye, centering=eye - np.float32(1.0 / C), group_mean=group / np.float32(GROUP),
                expand=expand, row_masks=masks)


def kernel(x, L0_conv_ln1_g, L0_conv_ln1_b, L0_conv_W_proj, L0_conv_W_gate, L0_conv_ln2_g, L0_conv_ln2_b,
           L0_conv_W_ab, L1_conv_Wa, L1_conv_ba, L1_conv_Wb, L1_conv_bb):
    import numpy as np
    import concourse.bacc as bacc
    from concourse.bass_utils import run_bass_kernel_spmd

    f = lambda a: np.ascontiguousarray(a)
    arrays = dict(
        x=f(np.transpose(np.asarray(x)[0], (2, 0, 1))),
        ln_vectors=f(np.stack([L0_conv_ln1_g, L0_conv_ln1_b, L0_conv_ln2_g, L0_conv_ln2_b], axis=1)),
        W_proj=f(L0_conv_W_proj), W_gate=f(L0_conv_W_gate), W_ab=f(L0_conv_W_ab),
        WaT=f(np.transpose(L1_conv_Wa)), WbT=f(np.transpose(L1_conv_Wb)),
        bias_ab=f(np.concatenate([np.asarray(L1_conv_ba), np.asarray(L1_conv_bb)])[None, :]),
        **shape_constants())
    nc = bacc.Bacc("TRN2", target_bir_lowering=False, num_devices=1)
    args = {n: nc.dram_tensor("in_" + n, a.shape, F32, kind="ExternalInput").ap() for n, a in arrays.items()}
    N = arrays["x"].shape[1]
    out = nc.dram_tensor("out_0", (C, N, N), F32, kind="ExternalOutput").ap()
    build(nc, out=out, **args)
    r = run_bass_kernel_spmd(nc, [{"in_" + n: a for n, a in arrays.items()}], core_ids=[0])
    return np.transpose(r.results[0]["out_0"], (1, 2, 0))[None]
```

```python
import concourse.bass as bass
from concourse import mybir
from contextlib import ExitStack

F32 = mybir.dt.float32
F16 = mybir.dt.float16
ALU = mybir.AluOpType
ACT = mybir.ActivationFunctionType
AX = mybir.AxisListType

C = 128
GROUP = 4
NG = C // GROUP
IB = 16
CH = 8
NCH = C // CH
WS = 64.0
EPS = 1e-5
QT = 4


class Plan:
    pass


def chained(engine, sem):
    count = [0]

    def step(ins):
        count[0] += 1
        ins.then_inc(sem, 1)
        engine.wait_ge(sem, count[0])
        return ins
    return step


def refined_rsqrt(dve, step, r, var, scratch):
    step(dve.tensor_tensor(scratch, r, r, ALU.mult))
    step(dve.tensor_tensor(scratch, scratch, var, ALU.mult))
    step(dve.tensor_scalar(scratch, scratch, -0.5, 1.5, ALU.mult, ALU.add))
    step(dve.tensor_tensor(r, r, scratch, ALU.mult))


def prepare_weights(nc, p, io):
    with ExitStack() as ctx:
        sb = lambda n, s, d: ctx.enter_context(nc.sbuf_tensor(n, s, d))
        w_proj = sb("w_proj", [C, 4 * C], F32)
        w_gate = sb("w_gate", [C, C], F32)
        w_ab = sb("w_ab", [C, C], F32)
        vec = sb("vec", [C, 4], F32)
        center = sb("center", [C, C], F32)
        scaled = sb("scaled", [C, 4 * C], F32)
        b1_bc = sb("b1_bc", [C, C], F32)
        psw = ctx.enter_context(nc.psum_tensor("psw", [C, 512], F32))
        psv = ctx.enter_context(nc.psum_tensor("psv", [C, 512], F32))
        loaded = p.sem("weights_loaded")
        dve_step = p.sem("w_dve_step")
        ready = p.sem("w_operand_ready")
        product = p.sem("w_product")
        with nc.Block() as block:
            @block.sync
            def _(sp):
                for dst, src in ((w_proj, io["W_proj"]), (w_gate, io["W_gate"]), (w_ab, io["W_ab"]),
                                 (vec, io["ln_vectors"]), (center, io["centering"]),
                                 (p.wa_t, io["WaT"]), (p.wb_t, io["WbT"]),
                                 (p.ident, io["identity"]), (p.masks, io["row_masks"]),
                                 (p.expand, io["expand"]), (p.bias_ab, io["bias_ab"]),
                                 (p.group_mat, io["group_mean"])):
                    sp.dma_start(dst[:, :], src).then_inc(loaded, 16)

            @block.vector
            def _(dve):
                step = chained(dve, dve_step)
                dve.wait_ge(loaded, 16 * 12)
                step(dve.memset(p.ones[:, :], 1.0))
                step(dve.memset(p.mean_mat[:, :], 1.0 / C))
                step(dve.tensor_copy(p.ident16[:, :], p.ident[:, :]))
                jobs = [(w_proj, vec[:, 0:1], 4 * C, p.w64, p.wh, p.wl),
                        (w_gate, vec[:, 0:1], C, None, p.gh, p.gl),
                        (w_ab, vec[:, 2:3], C, None, p.ah, p.al)]
                for n, (w, gain, width, keep, hi, lo) in enumerate(jobs):
                    dve.tensor_scalar(scaled[:, 0:width], w[:, 0:width], gain, None, ALU.mult).then_inc(ready, 1)
                    dve.wait_ge(product, n + 1)
                    dst = keep if keep is not None else scaled
                    if width == 4 * C:
                        out = dst[:, :].rearrange("c (h s f) -> c s h f", h=2, s=2)
                        step(dve.tensor_scalar(out, psw[:, :].rearrange("c (s h f) -> c s h f", s=2, h=2),
                                               WS, None, ALU.mult))
                    else:
                        step(dve.tensor_scalar(dst[:, 0:width], psw[:, 0:width], WS, None, ALU.mult))
                    step(dve.tensor_copy(hi[:, :], dst[:, 0:width]))
                    step(dve.tensor_tensor(lo[:, :], dst[:, 0:width], hi[:, :], ALU.subtract))
                step(dve.tensor_scalar(b1_bc[:, :], p.ones[:, :], vec[:, 1:2], None, ALU.mult))
                dve.sem_inc(ready, 1)
                dve.wait_ge(product, 4)
                out = scaled[:, :].rearrange("c (h s f) -> c s h f", h=2, s=2)
                step(dve.tensor_scalar(out, psw[:, :].rearrange("c (s h f) -> c s h f", s=2, h=2),
                                       WS, None, ALU.mult))
                step(dve.tensor_copy(p.vh[:, :], scaled[:, :]))
                step(dve.tensor_tensor(p.vl[:, :], scaled[:, :], p.vh[:, :], ALU.subtract))
                dve.wait_ge(product, 5)
                step(dve.tensor_copy(p.vg[:, :], psv[:, 0:1]))
                step(dve.tensor_scalar(p.v2[:, :], psv[:, 1:2], WS, None, ALU.mult))
                for w, hi, lo in ((p.wa_t, p.lah, p.lal), (p.wb_t, p.lbh, p.lbl)):
                    step(dve.tensor_scalar(scaled[:, 0:C], w[:, :], WS, None, ALU.mult))
                    step(dve.tensor_copy(hi[:, :], scaled[:, 0:C]))
                    step(dve.tensor_tensor(lo[:, :], scaled[:, 0:C], hi[:, :], ALU.subtract))

            @block.tensor
            def _(pe):
                for n, width in enumerate((4 * C, C, C)):
                    pe.wait_ge(ready, n + 1)
                    pe.matmul(psw[:, 0:width], lhsT=center[:, :], rhs=scaled[:, 0:width],
                              start=True, stop=True).then_inc(product, 1)
                pe.wait_ge(ready, 4)
                pe.matmul(psw[:, :], lhsT=b1_bc[:, :], rhs=w_proj[:, :], start=True, stop=True).then_inc(product, 1)
                pe.matmul(psv[:, 0:1], lhsT=w_gate[:, :], rhs=vec[:, 1:2], start=True, stop=True)
                pe.matmul(psv[:, 1:2], lhsT=w_ab[:, :], rhs=vec[:, 3:4], start=True, stop=True).then_inc(product, 1)


def stats0(nc, p, io):
    N, KT = p.N, p.KT
    ROW = KT * N
    XR = 4
    x_by_channel = io["x"].rearrange("c (t p) k -> c p t k", p=128)
    with ExitStack() as ctx:
        sb = lambda n, s, d: ctx.enter_context(nc.sbuf_tensor(n, s, d))
        ps = lambda n: ctx.enter_context(nc.psum_tensor(n, [128, 512], F32))
        xg = [sb(f"xg{k}", [128, GROUP, KT, N], F32) for k in range(XR)]
        sq = [sb(f"sq{k}", [128, GROUP, ROW], F32) for k in range(2)]
        csum = [sb(f"csum{k}", [128, ROW], F32) for k in range(2)]
        S1 = sb("S1", [128, ROW], F32)
        zeros = sb("zeros", [128, N], F32)
        bn = [sb(f"bn{k}", [128, GROUP * KT, 6], F32) for k in range(2)]
        mv = [sb(f"mv{k}", [128, 4], F32) for k in range(2)]
        gst = [sb(f"gst{k}", [128, 8], F32) for k in range(2)]
        all_st = sb("all_st", [128, 3, NG], F32)
        expo = sb("expo", [128, 2], F32)
        diag = sb("diag", [NG, 3, NG], F32)
        cols = sb("cols", [NG, 3], F32)
        tbar = sb("tbar", [128, 2], F32)
        t_bc = sb("t_bc", [C, C], F32)
        kap = sb("kap", [C, 512], F32)
        kh = sb("kh", [C, 512], F16)
        kl = sb("kl", [C, 512], F16)
        base = sb("base", [C, 512], F16)
        mu = sb("mu", [128, ROW], F32)
        var = sb("var", [128, ROW], F32)
        rstd = sb("rstd", [128, 2, ROW], F32)
        halves = sb("halves", [128, 2, 2, ROW], F16)
        s3 = sb("s3", [C, 4], F16)
        psS2 = [ps(f"psS2_{t}") for t in range(KT)]
        psG = ps("psG")
        psK = ps("psK")
        psT = ps("psT")
        psH = ctx.enter_context(nc.psum_tensor("psH", [128, 128], F16))
        xload = [p.sem(f"xg_loaded{k}") for k in range(XR)]
        consts = p.sem("stats_consts")
        dve_step = p.sem("stats_dve_step")
        bn_done = p.sem("bn_done")
        bn_seen = p.sem("bn_seen")
        mv_ready = p.sem("mv_ready")
        gmean = p.sem("gmean_ready")
        gvar = p.sem("gvar_ready")
        s_ready = p.sem("s_ready")
        st_ready = p.sem("st_ready")
        sq_ready = p.sem("sq_ready")
        s2_added = p.sem("s2_added")
        csum_ready = p.sem("csum_ready")
        s1_added = p.sem("s1_added")
        pool_step = p.sem("stats_pool_step")
        col_ready = p.sem("col_ready")
        prod = p.sem("stats_product")
        var_ready = p.sem("var_ready")
        rstd_ready = p.sem("rstd_ready")
        evac = p.sem("stats_evacuated")
        halves_ready = p.sem("halves_ready")
        stored = p.sem("rstd_stored")
        root_ready = p.sem("root_ready")
        BODIES = NG // XR

        with nc.Block() as block:
            @block.sync
            def _(sp):
                def load(k, first):
                    for c in range(GROUP):
                        sp.dma_start(xg[k][:, c, :, :], x_by_channel[first + c]).then_inc(xload[k], 16)
                for k in range(XR):
                    load(k, GROUP * k)
                with sp.Fori(0, BODIES - 1) as i:
                    for k in range(XR):
                        sp.wait_ge(bn_done, XR * i + k + 1)
                        sp.wait_ge(csum_ready, XR * i + k + 1)
                        sp.wait_ge(sq_ready, XR * i + k + 1)
                        load(k, (XR * i + XR + k) * GROUP)
                sp.wait_ge(halves_ready, 1)
                for q, d in ((0, p.r1_rows), (1, p.std_rows)):
                    for row, half in enumerate((0, 1, 0)):
                        sp.dma_start(d[row].rearrange("(t p) k -> p t k", p=128),
                                     halves[:, q, half, :].rearrange("p (t k) -> p t k", t=KT)).then_inc(stored, 16)
                sp.wait_ge(stored, 16 * 6)

            @block.gpsimd
            def _(pool):
                pool.memset(expo[:, 0:1], -0.5).then_inc(pool_step, 1)
                pool.wait_ge(pool_step, 1)
                with pool.Fori(0, BODIES) as i:
                    for k in range(XR):
                        g = XR * i + k
                        c2 = csum[k % 2]
                        flat = [xg[k][:, c, :, :].rearrange("p t k -> p (t k)") for c in range(GROUP)]
                        pool.wait_ge(xload[k], (i + 1) * (16 * GROUP))
                        pool.wait_ge(s1_added, g + 1)
                        pool.tensor_tensor(c2[:, :], flat[0], flat[1], ALU.add).then_inc(pool_step, 1)
                        pool.wait_ge(pool_step, g * 2 + 2)
                        pool.tensor_tensor(c2[:, :], c2[:, :], flat[2], ALU.add).then_inc(pool_step, 1)
                        pool.wait_ge(pool_step, g * 2 + 3)
                        pool.tensor_tensor(c2[:, :], c2[:, :], flat[3], ALU.add).then_inc(csum_ready, 1)
                        pool.wait_ge(gvar, g + 1)
                        pool.tensor_tensor(gst[k % 2][:, 3:4], gst[k % 2][:, 2:3], expo[:, 0:1], ALU.pow
                                           ).then_inc(s_ready, 1)

            @block.scalar
            def _(act):
                with act.Fori(0, BODIES) as i:
                    for k in range(XR):
                        act.wait_ge(st_ready, XR * i + k + 1)
                        act.wait_ge(s2_added, XR * i + k + 1)
                        act.activation(sq[k % 2][:, :, :].rearrange("p c n -> p (c n)"),
                                       xg[k][:, :, :, :].rearrange("p c t k -> p (c t k)"),
                                       ACT.Square, scale=gst[k % 2][:, 3:4], bias=gst[k % 2][:, 4:5]
                                       ).then_inc(sq_ready, 1)
                act.wait_ge(var_ready, 1)
                act.activation(rstd[:, 1, :], var[:, :], ACT.Sqrt).then_inc(root_ready, 1)

            @block.tensor
            def _(pe):
                pe.wait_ge(consts, 1)
                for t in range(KT):
                    pe.matmul(psS2[t][:, 0:N], lhsT=p.ident[:, :], rhs=zeros[:, :], start=True, stop=False)
                pe.sem_inc(s2_added, 2)

                def group_mean(i, k):
                    pe.wait_ge(mv_ready, XR * i + k + 1)
                    pe.matmul(psG[:, 0:2], lhsT=p.mean_mat[:, :], rhs=mv[k % 2][:, 0:2],
                              start=True, stop=True).then_inc(gmean, 1)

                def add_squares(i, k):
                    pe.wait_ge(sq_ready, XR * i + k + 1)
                    for c in range(GROUP):
                        for t in range(KT):
                            last = pe.matmul(psS2[t][:, 0:N], lhsT=p.ident[:, :],
                                             rhs=sq[k % 2][:, c, t * N:(t + 1) * N], start=False, stop=False)
                    last.then_inc(s2_added, 1)

                def body(i, more):
                    for k in range(XR):
                        if k + 1 < XR:
                            group_mean(i, k + 1)
                        elif more:
                            group_mean(i + 1, 0)
                        add_squares(i, k)
                group_mean(0, 0)
                with pe.Fori(0, BODIES - 1) as i:
                    body(i, True)
                body(BODIES - 1, False)
                for t in range(KT):
                    last = pe.matmul(psS2[t][:, 0:N], lhsT=p.ident[:, :], rhs=zeros[:, :], start=False, stop=True)
                last.then_inc(prod, 1)
                pe.wait_ge(col_ready, 1)
                pe.matmul(psG[:, 0:3], lhsT=p.expand[:, :], rhs=cols[:, :], start=True, stop=True).then_inc(prod, 1)
                pe.wait_ge(col_ready, 2)
                pe.matmul(psK[:, :], lhsT=t_bc[:, :], rhs=p.w64[:, :], start=True, stop=True).then_inc(prod, 1)
                pe.wait_ge(col_ready, 3)
                pe.transpose(psH[0:4, :], s3[:, :], p.ident16[:, :]).then_inc(prod, 1)
                pe.wait_ge(rstd_ready, 1)
                n = 0
                for kt in range(KT):
                    for t in range(KT):
                        if n:
                            pe.wait_ge(evac, n)
                        pe.transpose(psT[:, 0:128], rstd[:, 0, t * N + kt * 128:t * N + kt * 128 + 128],
                                     p.ident[:, :]).then_inc(prod, 1)
                        n += 1

            @block.vector
            def _(dve):
                step = chained(dve, dve_step)
                step(dve.memset(S1[:, :], 0.0))
                dve.memset(zeros[:, :], 0.0).then_inc(consts, 1)
                dve.sem_inc(s1_added, 2)
                LOOP0 = 1
                FIRST, SECOND = 5, 3

                def moments(i, k):
                    g = XR * i + k
                    dve.wait_ge(xload[k], (i + 1) * (16 * GROUP))
                    for c in range(GROUP):
                        for t in range(KT):
                            last = dve.bn_stats(bn[k % 2][:, c * KT + t, :], xg[k][:, c, t, :])
                    last.then_inc(bn_done, 1)

                def link(g, part, n):
                    base = LOOP0 + (FIRST if part else 0) + n
                    return lambda ins: (ins.then_inc(dve_step, 1),
                                        dve.wait_ge(dve_step, g * (FIRST + SECOND) + base))

                def variance(i, k):
                    g, h = XR * i + k, k % 2
                    dve.wait_ge(bn_done, g + 1)
                    dve.sem_inc(bn_seen, 1)
                    link(g, 0, 1)(dve.bn_aggr(mv[h][:, 0:2], bn[h][:, :, :].rearrange("p a b -> p (a b)")))
                    dve.scalar_tensor_tensor(out=mv[h][:, 1:2], in0=mv[h][:, 0:1], scalar=mv[h][:, 0:1],
                                             in1=mv[h][:, 1:2], op0=ALU.mult, op1=ALU.add).then_inc(mv_ready, 1)
                    dve.wait_ge(gmean, g + 1)
                    link(g, 0, 2)(dve.tensor_copy(gst[h][:, 0:1], psG[:, 0:1]))
                    link(g, 0, 3)(dve.tensor_tensor(gst[h][:, 1:2], gst[h][:, 0:1], gst[h][:, 0:1], ALU.mult))
                    link(g, 0, 4)(dve.tensor_tensor(gst[h][:, 2:3], psG[:, 1:2], gst[h][:, 1:2], ALU.subtract))
                    link(g, 0, 5)(dve.tensor_scalar(gst[h][:, 5:6], gst[h][:, 0:1], -1.0, None, ALU.mult))
                    dve.tensor_scalar(gst[h][:, 2:3], gst[h][:, 2:3], 0.0, EPS, ALU.max, ALU.add).then_inc(gvar, 1)

                def apply(i, k):
                    g, h = XR * i + k, k % 2
                    dve.wait_ge(s_ready, g + 1)
                    dve.tensor_tensor(gst[h][:, 4:5], gst[h][:, 5:6], gst[h][:, 3:4], ALU.mult).then_inc(st_ready, 1)
                    dve.wait_ge(st_ready, g + 1)
                    link(g, 1, 1)(dve.tensor_copy(all_st[:, 0, bass.ds(g, 1)], gst[h][:, 3:4]))
                    link(g, 1, 2)(dve.tensor_copy(all_st[:, 1, bass.ds(g, 1)], gst[h][:, 4:5]))
                    link(g, 1, 3)(dve.tensor_copy(all_st[:, 2, bass.ds(g, 1)], gst[h][:, 5:6]))
                    dve.wait_ge(csum_ready, g + 1)
                    dve.scalar_tensor_tensor(out=S1[:, :], in0=csum[h][:, :], scalar=gst[h][:, 3:4],
                                             in1=S1[:, :], op0=ALU.mult, op1=ALU.add).then_inc(s1_added, 1)
                    dve.wait_ge(s1_added, g + 3)

                def body(i, more):
                    for k in range(XR):
                        if k + 1 < XR:
                            moments(i, k + 1)
                        elif more:
                            moments(i + 1, 0)
                        apply(i, k)
                        if k + 1 < XR:
                            variance(i, k + 1)
                        elif more:
                            variance(i + 1, 0)
                moments(0, 0)
                variance(0, 0)
                with dve.Fori(0, BODIES - 1) as i:
                    body(i, True)
                body(BODIES - 1, False)
                total = [LOOP0 + (FIRST + SECOND) * NG]

                def step(ins):
                    total[0] += 1
                    ins.then_inc(dve_step, 1)
                    dve.wait_ge(dve_step, total[0])
                for q in range(3):
                    step(dve.tensor_tensor(diag[:, q, :], all_st[0:NG, q, :], p.ident[0:NG, 0:NG], ALU.mult))
                step(dve.tensor_reduce(cols[:, :], diag[:, :, :], axis=AX.X, op=ALU.add))
                dve.sem_inc(col_ready, 1)
                dve.wait_ge(prod, 2)
                step(dve.tensor_copy(p.st0[:, 0:3], psG[:, 0:3]))
                step(dve.tensor_scalar(t_bc[:, :], p.ones[:, :], p.st0[:, 1:2], None, ALU.mult))
                dve.sem_inc(col_ready, 1)
                step(dve.tensor_copy(s3[:, 0:1], p.st0[:, 0:1]))
                step(dve.tensor_copy(s3[:, 1:2], p.st0[:, 0:1]))
                step(dve.tensor_tensor(s3[:, 2:3], p.st0[:, 0:1], s3[:, 0:1], ALU.subtract))
                step(dve.memset(s3[:, 3:4], 0.0))
                dve.sem_inc(col_ready, 1)
                step(dve.tensor_reduce(tbar[:, 0:1], all_st[:, 1, :], axis=AX.X, op=ALU.add))
                step(dve.tensor_scalar(tbar[:, 1:2], tbar[:, 0:1], 1.0 / NG, None, ALU.mult))
                step(dve.tensor_scalar(mu[:, :], S1[:, :], 1.0 / C, tbar[:, 1:2], ALU.mult, ALU.add))
                step(dve.tensor_tensor(mu[:, :], mu[:, :], mu[:, :], ALU.mult))
                for t in range(KT):
                    step(dve.scalar_tensor_tensor(out=var[:, t * N:(t + 1) * N], in0=psS2[t][:, 0:N], scalar=1.0 / C,
                                                  in1=mu[:, t * N:(t + 1) * N], op0=ALU.mult, op1=ALU.subtract))
                dve.tensor_scalar(var[:, :], var[:, :], 0.0, EPS, ALU.max, ALU.add).then_inc(var_ready, 1)
                dve.wait_ge(root_ready, 1)
                step(dve.reciprocal(rstd[:, 0, :], rstd[:, 1, :]))
                refined_rsqrt(dve, step, rstd[:, 0, :], var[:, :], mu[:, :])
                dve.sem_inc(rstd_ready, 1)
                step(dve.tensor_tensor(rstd[:, 1, :], rstd[:, 0, :], var[:, :], ALU.mult))
                for q in range(2):
                    step(dve.tensor_copy(halves[:, q, 0, :], rstd[:, q, :]))
                    step(dve.tensor_tensor(halves[:, q, 1, :], rstd[:, q, :], halves[:, q, 0, :], ALU.subtract))
                dve.sem_inc(halves_ready, 1)
                dve.wait_ge(prod, 3)
                step(dve.tensor_copy(kap[:, :], psK[:, :]))
                step(dve.tensor_copy(kh[:, :], kap[:, :]))
                step(dve.tensor_tensor(kl[:, :], kap[:, :], kh[:, :], ALU.subtract))
                step(dve.tensor_scalar(base[:, :], kh[:, :], p.masks[:, 2 * IB:2 * IB + 1], None, ALU.mult))
                step(dve.scalar_tensor_tensor(out=base[:, :], in0=kl[:, :], scalar=p.masks[:, 2 * IB + 1:2 * IB + 2],
                                              in1=base[:, :], op0=ALU.mult, op1=ALU.add))
                for t in range(IB):
                    step(dve.scalar_tensor_tensor(out=p.const_rows[:, t, :], in0=p.vh[0:64, :],
                                                  scalar=p.masks[0:64, t:t + 1], in1=base[0:64, :],
                                                  op0=ALU.mult, op1=ALU.add))
                    step(dve.scalar_tensor_tensor(out=p.const_rows[:, t, :], in0=p.vl[0:64, :],
                                                  scalar=p.masks[0:64, IB + t:IB + t + 1], in1=p.const_rows[:, t, :],
                                                  op0=ALU.mult, op1=ALU.add))
                dve.wait_ge(prod, 4)
                step(dve.tensor_copy(p.s_rows[:, :], psH[0:4, :]))
                n = 0
                for kt in range(KT):
                    for t in range(KT):
                        dve.wait_ge(prod, 5 + n)
                        n += 1
                        dve.tensor_scalar(p.r64[:, kt, t * 128:(t + 1) * 128], psT[:, 0:128], 1.0 / WS, None,
                                          ALU.mult).then_inc(evac, 1)


def project0(nc, p, io):
    N, KT, NB = p.N, p.KT, p.NB
    NK = 3 * IB + 2
    with ExitStack() as ctx:
        sb = lambda n, s, d: ctx.enter_context(nc.sbuf_tensor("pj_" + n, s, d))
        x = [sb(f"x{k}", [C, IB, N], F32) for k in range(2)]
        yh = [sb(f"yh{k}", [C, IB, 128], F16) for k in range(2)]
        yl = [sb(f"yl{k}", [C, IB, 128], F16) for k in range(2)]
        std = [sb(f"std{k}", [64, N], F16) for k in range(2)]
        r_body = sb("r_body", [128, KT, 2 * IB], F32)
        sig = sb("sig", [128, 8, 2 * C], F32)
        prod = sb("prod", [128, 8, 2, C], F32)
        stage_a = [sb(f"stage_a{k}", [128, NCH, IB, CH, 2], F16) for k in range(2)]
        stage_b = [sb(f"stage_b{k}", [128, NCH, 2, CH, IB], F16) for k in range(2)]
        bank = [ctx.enter_context(nc.psum_tensor(f"bank{k}", [128, 4 * C], F32)) for k in range(8)]
        x_loaded = [p.sem(f"x_loaded{k}") for k in range(2)]
        split = p.sem("y_split")
        projected = p.sem("projected")
        sig_done = p.sem("sig_done")
        prod_done = p.sem("prod_done")
        hi_done = p.sem("ab_hi_done")
        lo_a = p.sem("a_lo_done")
        lo_b = p.sem("b_lo_done")
        stored = [p.sem(f"ab_stored{k}") for k in range(2)]
        ones_set = p.sem("ones_set")
        yh_done = p.sem("yh_done")
        r_copied = p.sem("r_copied")
        CREDIT = 2 * IB

        BODY = 2 * KT
        TILES = BODY * IB
        BATCH = TILES // QT
        BODIES = NB // 2

        def staged(b, ab, half, m):
            return batch_of(stage_b[b % 2] if ab else stage_a[b % 2], ab, half, m % (IB // QT))

        with nc.Block() as block:
            @block.sync
            def _(sp):
                def load(row, k):
                    sp.dma_start(x[k][:, :, :], io["x"][:, bass.ds(row * IB, IB), :]).then_inc(x_loaded[k], 16)
                    for h in range(3):
                        sp.dma_start(std[k][h * IB:(h + 1) * IB, :],
                                     p.std_rows[h, bass.ds(row * IB, IB), :]).then_inc(x_loaded[k], 16)

                def store(i, b):
                    sp.wait_ge(lo_a, i * BATCH + (b + 1) * IB // QT)
                    sp.wait_ge(lo_b, i * BATCH + (b + 1) * IB // QT)
                    for stage, dst in ((stage_a, p.a_parts), (stage_b, p.b_parts)):
                        store_stage(sp, stage[b % 2], dst, b % KT, 2 * i + b // KT).then_inc(stored[b % 2], 16)
                sp.wait_ge(ones_set, 1)
                for k in range(2):
                    load(k, k)

                def body(i, more):
                    for b in range(BODY):
                        store(i, b)
                        if more and b % KT == KT - 1:
                            k = b // KT
                            load(2 * i + 2 + k, k)
                with sp.Fori(0, BODIES - 1) as i:
                    body(i, True)
                body(BODIES - 1, False)
                for k in range(2):
                    sp.wait_ge(stored[k], 32 * (BODIES * BODY // 2 + 1))

            @block.vector
            def _(dve):
                for k in range(2):
                    last = dve.memset(std[k][32:64, :], 1.0)
                last.then_inc(ones_set, 1)
                dve.sem_inc(prod_done, 8)

                def split_block(i, b):
                    k, kt = (b // KT) % 2, b % KT
                    it = i + (b // BODY)
                    if b % KT == 0:
                        dve.wait_ge(x_loaded[k], (it + 1) * 64)
                    blk = i * BODY + b
                    dve.wait_ge(projected, blk * IB + IB)
                    src = x[k][:, :, kt * 128:(kt + 1) * 128]
                    dve.tensor_scalar(yh[b % 2][:, :, :], src, p.st0[:, 0:1], None, ALU.mult).then_inc(yh_done, 1)
                    dve.wait_ge(yh_done, blk + 1)
                    dve.scalar_tensor_tensor(out=yl[b % 2][:, :, :], in0=src, scalar=p.st0[:, 0:1],
                                             in1=yh[b % 2][:, :, :], op0=ALU.mult, op1=ALU.subtract
                                             ).then_inc(split, 1)

                def lo_of_b(i, m):
                    b = m // (IB // QT)
                    dve.wait_ge(hi_done, i * BATCH + m + 1)
                    slot = QT * (m % 2)
                    dve.tensor_tensor(staged(b, 1, 1, m),
                                      prod[:, slot:slot + QT, 1, :].rearrange("p i (h c) -> p i h c", c=CH),
                                      staged(b, 1, 0, m), ALU.subtract).then_inc(lo_b, 1)

                def body(i, more):
                    dve.tensor_copy(r_body[:, :, :], p.r64[:, :, bass.ds(i * (2 * IB), 2 * IB)]).then_inc(r_copied, 1)
                    dve.wait_ge(r_copied, i + 1)
                    for b in range(BODY):
                        k, kt = b // KT, b % KT
                        for m in range(b * IB // QT, (b + 1) * IB // QT):
                            if m >= 2:
                                dve.wait_ge(lo_b, i * BATCH + m - 1)
                                dve.wait_ge(lo_a, i * BATCH + m - 1)
                            for q in range(QT):
                                n = m * QT + q
                                dve.wait_ge(sig_done, i * TILES + n + 1)
                                dve.scalar_tensor_tensor(
                                    out=prod[:, n % 8, :, :].rearrange("p s c -> p (s c)"),
                                    in0=bank[n % 8][:, 2 * C:4 * C],
                                    scalar=r_body[:, kt, k * IB + n % IB:k * IB + n % IB + 1],
                                    in1=sig[:, n % 8, :], op0=ALU.mult, op1=ALU.mult).then_inc(prod_done, 1)
                            if m >= 1:
                                lo_of_b(i, m - 1)
                            if m == b * IB // QT + 1 and (more or b + 1 < BODY):
                                split_block(i, b + 1)
                    lo_of_b(i, BATCH - 1)
                    dve.wait_ge(lo_b, i * BATCH + BATCH)
                    dve.wait_ge(lo_a, i * BATCH + BATCH)
                split_block(0, 0)
                with dve.Fori(0, BODIES - 1) as i:
                    body(i, True)
                body(BODIES - 1, False)

            @block.gpsimd
            def _(pool):
                def body(i):
                    for m in range(BATCH):
                        b = m // (IB // QT)
                        pool.wait_ge(hi_done, i * BATCH + m + 1)
                        slot = QT * (m % 2)
                        pool.tensor_tensor(staged(b, 0, 1, m),
                                           prod[:, slot:slot + QT, 0, :].rearrange("p i (h c) -> p i h c", c=CH),
                                           staged(b, 0, 0, m), ALU.subtract).then_inc(lo_a, 1)
                with pool.Fori(0, BODIES) as i:
                    body(i)

            @block.scalar
            def _(act):
                act.sem_inc(stored[0], 32)
                act.sem_inc(stored[1], 32)

                def hi_of(i, m):
                    b = m // (IB // QT)
                    if m % (IB // QT) == 0:
                        act.wait_ge(stored[b % 2], (i * (BODY // 2) + b // 2 + 1) * 32)
                    act.wait_ge(prod_done, i * TILES + (m + 1) * QT + 8)
                    slot = QT * (m % 2)
                    for ab in range(2):
                        last = act.activation(staged(b, ab, 0, m),
                                              prod[:, slot:slot + QT, ab, :].rearrange("p i (h c) -> p i h c", c=CH),
                                              ACT.Copy)
                    last.then_inc(hi_done, 1)

                with act.Fori(0, BODIES) as i:
                    act.wait_ge(r_copied, i + 1)
                    for m in range(BATCH):
                        for q in range(QT):
                            n = m * QT + q
                            kt, at = (n // IB) % KT, n // (IB * KT) * IB + n % IB
                            act.wait_ge(projected, i * TILES + (n + 1 + CREDIT))
                            act.activation(sig[:, n % 8, :], bank[n % 8][:, 0:2 * C], ACT.Sigmoid,
                                           scale=r_body[:, kt, at:at + 1]).then_inc(sig_done, 1)
                        if m:
                            hi_of(i, m - 1)
                    hi_of(i, BATCH - 1)

            @block.tensor
            def _(pe):
                pe.sem_inc(projected, CREDIT)
                with pe.Fori(0, BODIES) as i:
                    for b in range(BODY):
                        k, kt = b // KT, b % KT
                        pe.wait_ge(split, i * BODY + b + 1)
                        for t in range(IB):
                            n = b * IB + t
                            out = bank[n % 8][:, :]
                            pe.wait_ge(prod_done, i * TILES + n + 1)
                            pe.matmul(out, lhsT=yh[b % 2][:, t, :], rhs=p.wh[:, :], start=True, stop=False)
                            pe.matmul(out, lhsT=yh[b % 2][:, t, :], rhs=p.wl[:, :], start=False, stop=False)
                            pe.matmul(out, lhsT=yl[b % 2][:, t, :], rhs=p.wh[:, :], start=False, stop=False)
                            pe.matmul(out, lhsT=std[k][0:NK, kt * 128:(kt + 1) * 128],
                                      rhs=p.const_rows[0:NK, t, :], start=False, stop=True).then_inc(projected, 1)


def mix(nc, p, name, out, residual):
    N, KT, NB = p.N, p.KT, p.NB
    ROW = KT * N
    with ExitStack() as ctx:
        sb = lambda n, s, d: ctx.enter_context(nc.sbuf_tensor(name + n, s, d))
        pa = [sb(f"pa{k}", [128, KT, N, CH, 2], F16) for k in range(2)]
        pb = [sb(f"pb{k}", [128, KT, NB, 2, CH, IB], F16) for k in range(2)]
        res = [sb(f"res{k}", [128, KT, N], F32) for k in range(2)]
        o = [sb(f"o{k}", [128, KT, N], F32) for k in range(2)]
        bank = [[ctx.enter_context(nc.psum_tensor(f"{name}bank{k}_{t}", [128, 512], F32)) for t in range(KT)]
                for k in range(2)]
        loaded = [p.sem(f"{name}_parts_loaded{k}") for k in range(2)]
        res_loaded = [p.sem(f"{name}_res_loaded{k}") for k in range(2)]
        mixed = p.sem(f"{name}_mixed")
        evacuated = p.sem(f"{name}_evacuated")
        stored = [p.sem(f"{name}_stored{k}") for k in range(2)]
        out_v = out.rearrange("c (t p) j -> c p t j", p=128)
        sums = residual is None
        if sums:
            sq = [sb(f"sq{k}", [128, ROW], F32) for k in range(2)]
            S1 = sb("S1", [128, ROW], F32)
            S2 = sb("S2", [128, ROW], F32)
            halves = sb("halves", [128, 2, ROW], F16)
            sq_ready = p.sem(f"{name}_sq_ready")
            s1_added = p.sem(f"{name}_s1_added")
            s2_added = p.sem(f"{name}_s2_added")
            var_ready = p.sem(f"{name}_var_ready")
            root_ready = p.sem(f"{name}_root_ready")
            tail = p.sem(f"{name}_tail")
            halves_ready = p.sem(f"{name}_halves_ready")
            rows_stored = p.sem(f"{name}_rows_stored")
            init = p.sem(f"{name}_init")
        else:
            res_v = residual.rearrange("c (t p) j -> c p t j", p=128)
            st = sb("st", [128, 2, 2 * CH], F32)
            scaled = p.sem(f"{name}_residual_scaled")
            st_ready = p.sem(f"{name}_factors_ready")
        BODY = 2 * CH
        BODIES = NCH // 2

        def flat(t3):
            return t3[:, :, :].rearrange("p t j -> p (t j)")

        with nc.Block() as block:
            @block.sync
            def _(sp):
                def load(chunk, k):
                    for kt in range(KT):
                        sp.dma_start(pa[k][:, kt, :, :, :].rearrange("p i c q -> p (i c q)"),
                                     p.a_parts[chunk, kt].rearrange("p b n -> p (b n)")).then_inc(loaded[k], 16)
                        sp.dma_start(pb[k][:, kt, :, :, :, :].rearrange("p b q c i -> p (b q c i)"),
                                     p.b_parts[chunk, kt].rearrange("p b n -> p (b n)")).then_inc(loaded[k], 16)
                if not sums:
                    for k in range(2):
                        sp.dma_start(res[k][:, :, :], res_v[k]).then_inc(res_loaded[k], 16)
                for k in range(2):
                    load(k, k)

                def body(i, more):
                    for n in range(BODY):
                        sp.wait_ge(evacuated, i * BODY + n + 3)
                        sp.dma_start(out_v[i * BODY + n], o[n % 2][:, :, :]).then_inc(stored[n % 2], 16)
                        if not sums and (more or n + 2 < BODY):
                            sp.dma_start(res[n % 2][:, :, :], res_v[i * BODY + n + 2]).then_inc(res_loaded[n % 2], 16)
                        if more and n % CH == CH - 1:
                            load(2 * i + 2 + n // CH, n // CH)
                with sp.Fori(0, BODIES - 1) as i:
                    body(i, True)
                body(BODIES - 1, False)
                if sums:
                    sp.wait_ge(halves_ready, 1)
                    for row in range(2):
                        sp.dma_start(p.r2_rows[row].rearrange("(t p) k -> p t k", p=128),
                                     halves[:, row, :].rearrange("p (t k) -> p t k", t=KT)).then_inc(rows_stored, 16)
                    sp.wait_ge(rows_stored, 32)
                for k in range(2):
                    sp.wait_ge(stored[k], 16 * (C // 2 + 1))

            @block.tensor
            def _(pe):
                with pe.Fori(0, BODIES) as i:
                    for n in range(BODY):
                        k, c = n // CH, n % CH
                        if c == 0:
                            pe.wait_ge(loaded[k], (i + 1) * (32 * KT))
                        pe.wait_ge(evacuated, i * BODY + n + 1)
                        for t in range(KT):
                            dst = bank[n % 2][t][:, 0:N]
                            for kt in range(KT):
                                a_hi, a_lo = (pa[k][:, kt, t * 128:(t + 1) * 128, c, q] for q in (0, 1))
                                b_hi, b_lo = (pb[k][:, kt, :, q, c, :] for q in (0, 1))
                                pe.matmul(dst, lhsT=a_hi, rhs=b_hi, start=(kt == 0), stop=False)
                                pe.matmul(dst, lhsT=a_hi, rhs=b_lo, start=False, stop=False)
                                last = pe.matmul(dst, lhsT=a_lo, rhs=b_hi, start=False, stop=(kt == KT - 1))
                            last.then_inc(mixed, 1)

            if sums:
                @block.scalar
                def _(act):
                    act.sem_inc(evacuated, 2)
                    act.sem_inc(stored[0], 16)
                    act.sem_inc(stored[1], 16)
                    with act.Fori(0, BODIES) as i:
                        for n in range(BODY):
                            act.wait_ge(stored[n % 2], (i * (BODY // 2) + n // 2 + 1) * 16)
                            act.wait_ge(s1_added, i * BODY + n + 1)
                            for t in range(KT):
                                act.wait_ge(mixed, i * (BODY * KT) + n * KT + t + 1)
                                last = act.activation(o[n % 2][:, t, :], bank[n % 2][t][:, 0:N], ACT.Copy)
                            last.then_inc(evacuated, 1)
                            act.wait_ge(evacuated, i * BODY + n + 3)
                            act.wait_ge(s2_added, i * BODY + n + 1)
                            act.activation(sq[n % 2][:, :], flat(o[n % 2]), ACT.Square).then_inc(sq_ready, 1)
                    act.wait_ge(var_ready, 1)
                    act.activation(sq[0][:, :], sq[1][:, :], ACT.Sqrt).then_inc(root_ready, 1)

                @block.gpsimd
                def _(pool):
                    pool.memset(S2[:, :], 0.0).then_inc(init, 1)
                    pool.wait_ge(init, 1)
                    pool.sem_inc(s2_added, 2)
                    with pool.Fori(0, BODIES) as i:
                        for n in range(BODY):
                            pool.wait_ge(sq_ready, i * BODY + n + 1)
                            pool.tensor_tensor(S2[:, :], S2[:, :], sq[n % 2][:, :], ALU.add).then_inc(s2_added, 1)
                            pool.wait_ge(s2_added, i * BODY + n + 3)

                @block.vector
                def _(dve):
                    dve.memset(S1[:, :], 0.0).then_inc(tail, 1)
                    dve.wait_ge(tail, 1)
                    dve.sem_inc(s1_added, 2)
                    with dve.Fori(0, BODIES) as i:
                        for n in range(BODY):
                            dve.wait_ge(evacuated, i * BODY + n + 3)
                            dve.tensor_tensor(S1[:, :], S1[:, :], flat(o[n % 2]), ALU.add).then_inc(s1_added, 1)
                            dve.wait_ge(s1_added, i * BODY + n + 3)
                    count = [1]

                    def step(ins):
                        count[0] += 1
                        ins.then_inc(tail, 1)
                        dve.wait_ge(tail, count[0])
                    dve.wait_ge(s2_added, C + 2)
                    step(dve.tensor_scalar(S1[:, :], S1[:, :], 1.0 / C, None, ALU.mult))
                    step(dve.tensor_tensor(S1[:, :], S1[:, :], S1[:, :], ALU.mult))
                    step(dve.scalar_tensor_tensor(out=sq[1][:, :], in0=S2[:, :], scalar=1.0 / C, in1=S1[:, :],
                                                  op0=ALU.mult, op1=ALU.subtract))
                    dve.tensor_scalar(sq[1][:, :], sq[1][:, :], 0.0, EPS, ALU.max, ALU.add).then_inc(var_ready, 1)
                    dve.wait_ge(root_ready, 1)
                    step(dve.reciprocal(S2[:, :], sq[0][:, :]))
                    refined_rsqrt(dve, step, S2[:, :], sq[1][:, :], S1[:, :])
                    step(dve.tensor_copy(halves[:, 0, :], S2[:, :]))
                    step(dve.tensor_tensor(halves[:, 1, :], S2[:, :], halves[:, 0, :], ALU.subtract))
                    dve.sem_inc(halves_ready, 1)
            else:
                @block.scalar
                def _(act):
                    with act.Fori(0, BODIES) as i:
                        act.wait_ge(scaled, i * BODY + 1)
                        act.activation(st[:, :, :], p.res_st[:, :, bass.ds(i * BODY, BODY)], ACT.Copy).then_inc(st_ready, 1)
                        act.wait_ge(st_ready, i + 1)
                        for n in range(BODY):
                            act.wait_ge(res_loaded[n % 2], (i * (BODY // 2) + n // 2 + 1) * 16)
                            act.activation(flat(res[n % 2]), flat(res[n % 2]), ACT.Identity, scale=st[:, 0, n:n + 1],
                                           bias=st[:, 1, n:n + 1]).then_inc(scaled, 1)

                @block.vector
                def _(dve):
                    dve.sem_inc(evacuated, 2)
                    dve.sem_inc(scaled, 1)
                    dve.sem_inc(stored[0], 16)
                    dve.sem_inc(stored[1], 16)
                    with dve.Fori(0, BODIES) as i:
                        for n in range(BODY):
                            dve.wait_ge(stored[n % 2], (i * (BODY // 2) + n // 2 + 1) * 16)
                            dve.wait_ge(scaled, i * BODY + (n + 2))
                            for t in range(KT):
                                dve.wait_ge(mixed, i * (BODY * KT) + n * KT + t + 1)
                                last = dve.tensor_tensor(o[n % 2][:, t, :], bank[n % 2][t][:, 0:N],
                                                         res[n % 2][:, t, :], ALU.add)
                            last.then_inc(evacuated, 1)


def join0(nc, p, io):
    N = p.N
    SUB = 512
    RING = 4
    TOK = 3 * SUB if (N * N) % (3 * RING * SUB) == 0 else 2 * SUB
    NS = TOK // SUB
    TILES = N * N // TOK
    BODIES = TILES // RING
    with ExitStack() as ctx:
        sb = lambda n, s, d: ctx.enter_context(nc.sbuf_tensor("join_" + n, s, d))
        ring = lambda n, s, d: [sb(f"{n}{k}", s, d) for k in range(RING)]
        two = lambda n, s, d: [sb(f"{n}{k}", s, d) for k in range(2)]
        x = ring("x", [C, TOK], F32)
        ab = ring("ab", [C, TOK], F32)
        r1 = ring("r1", [4, TOK], F16)
        r2 = ring("r2", [2, TOK], F16)
        yn = two("yn", [C, TOK], F32)
        yh = two("yh", [C, TOK], F16)
        yl = two("yl", [C, TOK], F16)
        zn = two("zn", [C, TOK], F32)
        zh = two("zh", [C, TOK], F16)
        zl = two("zl", [C, TOK], F16)
        gate = two("gate", [C, TOK], F32)
        x1 = two("x1", [C, TOK], F32)
        square = sb("square", [C, TOK], F32)
        sum_x1 = sb("sum_x1", [C, TILES], F32)
        sum_sq = sb("sum_sq", [C, TILES], F32)
        ones2 = sb("ones2", [2, C], F16)
        tot = sb("tot", [C, 8], F32)
        t_bc = sb("t_bc", [C, C], F32)
        diag = sb("diag", [C, 2, C], F32)
        psr = [ctx.enter_context(nc.psum_tensor(f"psr{k}", [128, SUB], F32)) for k in range(4)]
        psz = [ctx.enter_context(nc.psum_tensor(f"psz{k}", [128, SUB], F32)) for k in range(4)]
        loaded = [p.sem(f"join_loaded{k}") for k in range(RING)]
        spread = p.sem("join_r_spread")
        normed = p.sem("join_normed")
        hi = p.sem("join_hi")
        lo = p.sem("join_lo")
        prods = p.sem("join_products")
        gated = p.sem("join_gated")
        mul = p.sem("join_times_gate")
        done = p.sem("join_x1_done")
        squared = p.sem("join_squared")
        stored = [p.sem(f"join_stored{k}") for k in range(2)]
        ones_set = p.sem("join_ones_set")
        tail = p.sem("join_tail_step")
        operand = p.sem("join_tail_operand")
        tail_prod = p.sem("join_tail_product")
        s_ready = p.sem("join_s_ready")
        xf = io["x"].rearrange("c i k -> c (i k)")
        abf = p.ab.rearrange("c i k -> c (i k)")
        x1f = p.x1.rearrange("c i k -> c (i k)")
        r1f = p.r1_rows.rearrange("r i k -> r (i k)")
        r2f = p.r2_rows.rearrange("r i k -> r (i k)")
        NORM0, LO0, PROD0, MUL0, SQ0 = 4, 4, 4 * NS, 2, 2

        def cut(u):
            return slice(u * SUB, (u + 1) * SUB)

        def ahead(i, k, by):
            return i + (k + by) // RING, (k + by) % RING

        def over_tiles(engine, step):
            for k in range(RING):
                step(0, k, k)
            with engine.Fori(1, BODIES - 1) as i:
                for k in range(RING):
                    step(i, k, None)
            for k in range(RING):
                step(BODIES - 1, k, TILES - RING + k)

        def exists(t, by):
            return t is None or 0 <= t + by < TILES

        with nc.Block() as block:
            @block.sync
            def _(sp):
                def load(t, k):
                    at = bass.ds(t * TOK, TOK)
                    sp.dma_start(x[k][:, :], xf[:, at]).then_inc(loaded[k], 16)
                    sp.dma_start(ab[k][:, :], abf[:, at]).then_inc(loaded[k], 16)
                    sp.dma_start(r1[k][0:3, :], r1f[:, at]).then_inc(loaded[k], 16)
                    sp.dma_start(r2[k][:, :], r2f[:, at]).then_inc(loaded[k], 16)
                for k in range(RING):
                    load(k, k)

                def body(i, more):
                    for k in range(RING):
                        sp.wait_ge(done, i * RING + k + 1)
                        sp.dma_start(x1f[:, bass.ds((i * RING + k) * TOK, TOK)],
                                     x1[k % 2][:, :]).then_inc(stored[k % 2], 16)
                        if more:
                            load(i * RING + k + RING, k)
                with sp.Fori(0, BODIES - 1) as i:
                    body(i, True)
                body(BODIES - 1, False)
                for k in range(2):
                    sp.wait_ge(stored[k], 16 * (TILES // 2 + 1))

            @block.tensor
            def _(pe):
                pe.wait_ge(ones_set, 1)
                pe.sem_inc(prods, PROD0)

                def spread_r(i, k, u):
                    t = RING * i + k
                    if u == 0:
                        pe.wait_ge(loaded[k], (i + 1) * 64)
                    bank = 2 * ((NS * k + u) % 2)
                    pe.wait_ge(normed, t * (2 * NS) + (2 * u + NORM0 - 2))
                    pe.matmul(psr[bank][:, :], lhsT=p.s_rows[0:3, :], rhs=r1[k][0:3, cut(u)],
                              start=True, stop=True).then_inc(spread, 1)
                    pe.matmul(psr[bank + 1][:, :], lhsT=ones2[:, :], rhs=r2[k][:, cut(u)],
                              start=True, stop=True).then_inc(spread, 1)

                def products(i, k, u):
                    t, h = RING * i + k, k % 2
                    if u == 0:
                        pe.wait_ge(lo, t * 2 + (2 + LO0))
                    bank = 2 * ((NS * k + u) % 2)
                    pe.wait_ge(mul, t * NS + (u - 1 + MUL0))
                    for q, (wh, wl, vh, vl) in enumerate(((p.gh, p.gl, yh, yl), (p.ah, p.al, zh, zl))):
                        dst = psz[bank + q][:, :]
                        pe.matmul(dst, lhsT=wh[:, :], rhs=vh[h][:, cut(u)], start=True, stop=False)
                        pe.matmul(dst, lhsT=wh[:, :], rhs=vl[h][:, cut(u)], start=False, stop=False)
                        pe.matmul(dst, lhsT=wl[:, :], rhs=vh[h][:, cut(u)], start=False, stop=True
                                  ).then_inc(prods, 1)

                def step(i, k, t):
                    for u in range(NS):
                        if exists(t, 2):
                            spread_r(*ahead(i, k, 2), u)
                        products(i, k, u)
                for k in range(2):
                    for u in range(NS):
                        spread_r(0, k, u)
                over_tiles(pe, step)
                pe.wait_ge(operand, 1)
                pe.matmul(psr[0][:, 0:2], lhsT=p.group_mat[:, :], rhs=tot[:, 0:2],
                          start=True, stop=True).then_inc(tail_prod, 1)
                pe.wait_ge(operand, 3)
                for q, w in enumerate((p.wa_t, p.wb_t)):
                    pe.matmul(psr[1 + q][:, 0:C], lhsT=t_bc[:, :], rhs=w[:, :], start=True, stop=False)
                    pe.matmul(psr[1 + q][:, 0:C], lhsT=p.ones[0:1, :], rhs=p.bias_ab[0:1, q * C:(q + 1) * C],
                              start=False, stop=True).then_inc(tail_prod, 1)
                pe.wait_ge(operand, 4)
                pe.matmul(psr[3][:, 0:2 * C], lhsT=p.ones[:, :], rhs=diag[:, :, :].rearrange("p q c -> p (q c)"),
                          start=True, stop=True).then_inc(tail_prod, 1)

            @block.scalar
            def _(act):
                act.sem_inc(squared, SQ0)

                def halves(i, k):
                    t, h = RING * i + k, k % 2
                    act.wait_ge(prods, t * (2 * NS) + (PROD0 - 2 * NS))
                    act.wait_ge(normed, t * (2 * NS) + (2 * NS + NORM0))
                    act.activation(yh[h][:, :], yn[h][:, :], ACT.Copy).then_inc(hi, 1)
                    act.activation(zh[h][:, :], zn[h][:, :], ACT.Copy).then_inc(hi, 1)

                def gates(i, k):
                    t, h = RING * i + k, k % 2
                    for u in range(NS):
                        bank = 2 * ((NS * k + u) % 2)
                        act.wait_ge(prods, t * (2 * NS) + (2 * u + 1 + PROD0))
                        act.activation(gate[h][:, cut(u)], psz[bank][:, :], ACT.Sigmoid,
                                       scale=1.0 / WS, bias=p.vg[:, :]).then_inc(gated, 1)

                def squares(i, k):
                    t = RING * i + k
                    act.wait_ge(done, t + 1)
                    act.wait_ge(squared, t + SQ0)
                    act.activation(square[:, :], x1[k % 2][:, :], ACT.Square,
                                   accum_out=sum_sq[:, bass.ds(t, 1)]).then_inc(squared, 1)

                def step(i, k, t):
                    if exists(t, 1):
                        halves(*ahead(i, k, 1))
                    if exists(t, -1):
                        squares(*ahead(i, k, -1))
                    gates(i, k)
                halves(0, 0)
                over_tiles(act, step)
                squares(BODIES - 1, RING - 1)

            @block.gpsimd
            def _(pool):
                pool.sem_inc(lo, LO0)
                with pool.Fori(0, BODIES) as i:
                    for k in range(RING):
                        for q, (src, h, dst) in enumerate(((yn, yh, yl), (zn, zh, zl))):
                            pool.wait_ge(hi, (RING * i + k) * 2 + (q + 1))
                            pool.tensor_tensor(dst[k % 2][:, :], src[k % 2][:, :], h[k % 2][:, :],
                                               ALU.subtract).then_inc(lo, 1)
                pool.wait_ge(operand, 2)
                pool.tensor_tensor(tot[:, 4:5], tot[:, 3:4], tot[:, 5:6], ALU.pow).then_inc(s_ready, 1)

            @block.vector
            def _(dve):
                dve.memset(ones2[:, :], 1.0).then_inc(ones_set, 1)
                dve.sem_inc(normed, NORM0)
                dve.sem_inc(mul, MUL0)
                dve.sem_inc(stored[0], 16)
                dve.sem_inc(stored[1], 16)

                def norm(i, k, u):
                    t, h = RING * i + k, k % 2
                    if u == 0:
                        dve.wait_ge(loaded[k], (i + 1) * 64)
                        dve.wait_ge(lo, t * 2 + (LO0 - 2))
                    bank = 2 * ((NS * k + u) % 2)
                    dve.wait_ge(spread, t * (2 * NS) + (2 * u + 1))
                    dve.scalar_tensor_tensor(out=yn[h][:, cut(u)], in0=x[k][:, cut(u)], scalar=p.st0[:, 2:3],
                                             in1=psr[bank][:, :], op0=ALU.add, op1=ALU.mult).then_inc(normed, 1)
                    dve.wait_ge(spread, t * (2 * NS) + (2 * u + 2))
                    dve.tensor_tensor(zn[h][:, cut(u)], ab[k][:, cut(u)], psr[bank + 1][:, :],
                                      ALU.mult).then_inc(normed, 1)

                def times_gate(i, k, u):
                    t, h = RING * i + k, k % 2
                    bank = 2 * ((NS * k + u) % 2)
                    dve.wait_ge(gated, t * NS + (u + 1))
                    dve.wait_ge(prods, t * (2 * NS) + (2 * u + 2 + PROD0))
                    dve.scalar_tensor_tensor(out=gate[h][:, cut(u)], in0=psz[bank + 1][:, :], scalar=p.v2[:, :],
                                             in1=gate[h][:, cut(u)], op0=ALU.add, op1=ALU.mult).then_inc(mul, 1)

                def finish(i, k):
                    t, h = RING * i + k, k % 2
                    dve.wait_ge(mul, t * NS + (NS + MUL0))
                    dve.wait_ge(stored[h], (i * (RING // 2) + k // 2 + 1) * 16)
                    dve.wait_ge(squared, t + (SQ0 - 1))
                    dve.scalar_tensor_tensor(out=x1[h][:, :], in0=gate[h][:, :], scalar=1.0 / WS, in1=x[k][:, :],
                                             op0=ALU.mult, op1=ALU.add,
                                             accum_out=sum_x1[:, bass.ds(t, 1)]).then_inc(done, 1)

                def step(i, k, t):
                    for u in range(NS):
                        if exists(t, 2):
                            norm(*ahead(i, k, 2), u)
                        times_gate(i, k, u)
                    finish(i, k)
                for k in range(2):
                    for u in range(NS):
                        norm(0, k, u)
                over_tiles(dve, step)

                chain = chained(dve, tail)
                dve.wait_ge(squared, TILES + SQ0)
                dve.wait_ge(done, TILES)
                chain(dve.tensor_reduce(tot[:, 0:1], sum_x1[:, :], axis=AX.X, op=ALU.add))
                chain(dve.tensor_reduce(tot[:, 1:2], sum_sq[:, :], axis=AX.X, op=ALU.add))
                chain(dve.tensor_scalar(tot[:, 0:2], tot[:, 0:2], 1.0 / (N * N), None, ALU.mult))
                dve.sem_inc(operand, 1)
                dve.wait_ge(tail_prod, 1)
                chain(dve.tensor_copy(tot[:, 2:3], psr[0][:, 0:1]))
                chain(dve.tensor_tensor(tot[:, 6:7], tot[:, 2:3], tot[:, 2:3], ALU.mult))
                chain(dve.tensor_tensor(tot[:, 3:4], psr[0][:, 1:2], tot[:, 6:7], ALU.subtract))
                chain(dve.tensor_scalar(tot[:, 3:4], tot[:, 3:4], 0.0, EPS, ALU.max, ALU.add))
                chain(dve.memset(tot[:, 5:6], -0.5))
                dve.sem_inc(operand, 1)
                chain(dve.tensor_scalar(tot[:, 7:8], tot[:, 2:3], -1.0, None, ALU.mult))
                dve.wait_ge(s_ready, 1)
                chain(dve.tensor_copy(p.st1[:, 0:1], tot[:, 4:5]))
                chain(dve.tensor_tensor(p.st1[:, 1:2], tot[:, 7:8], tot[:, 4:5], ALU.mult))
                chain(dve.tensor_scalar(t_bc[:, :], p.ones[:, :], p.st1[:, 1:2], None, ALU.mult))
                dve.sem_inc(operand, 1)
                dve.wait_ge(tail_prod, 3)
                for q in range(2):
                    for u in range(QT):
                        chain(dve.tensor_copy(p.const1[:, q, u, :], psr[1 + q][:, 0:C]))
                for q in range(2):
                    chain(dve.tensor_scalar(diag[:, q, :], p.ident[:, :], p.st1[:, q:q + 1], None, ALU.mult))
                dve.sem_inc(operand, 1)
                dve.wait_ge(tail_prod, 4)
                chain(dve.tensor_scalar(p.res_st[:, 0, :], psr[3][:, 0:C], 1.0, None, ALU.add))
                chain(dve.tensor_copy(p.res_st[:, 1, :], psr[3][:, C:2 * C]))


def project1(nc, p):
    KT = p.KT
    G = 128 // IB
    with ExitStack() as ctx:
        sb = lambda n, s, d: ctx.enter_context(nc.sbuf_tensor("sq_" + n, s, d))
        XR, SR = 4, 4
        x = [sb(f"x{k}", [C, IB, 128], F32) for k in range(XR)]
        yh = sb("yh", [C, 128, 128], F16)
        yl = sb("yl", [C, 128, 128], F16)
        value = [sb(f"value{k}", [128, QT, C], F32) for k in range(4)]
        stage = [sb(f"stage{k}", [128, NCH, 2 * CH * IB], F16) for k in range(SR)]
        bank = [ctx.enter_context(nc.psum_tensor(f"sqbank{k}", [128, QT, C], F32)) for k in range(8)]
        loaded = [p.sem(f"sq_loaded{k}") for k in range(XR)]
        x_hi = p.sem("sq_x_hi")
        x_lo = p.sem("sq_x_lo")
        projected = p.sem("sq_projected")
        valued = p.sem("sq_valued")
        v_hi = p.sem("sq_value_hi")
        lo_pool = p.sem("sq_value_lo_by_pool")
        lo_dve = p.sem("sq_value_lo_by_dve")
        seen = p.sem("sq_lo_by_pool_seen")
        stored = [p.sem(f"sq_stored{k}") for k in range(SR)]
        B = IB // QT
        BATCHES = 2 * G * B
        VAL0, LO0, PROJ0 = 8, 1, 1

        def pool_takes(n):
            return n < BATCHES // 2 or n % B == 0

        def wait_lo(engine, q, n):
            pool_n = sum(pool_takes(m) for m in range(n))
            pool_all = sum(pool_takes(m) for m in range(BATCHES))
            engine.wait_ge(lo_pool, q * pool_all + (pool_n + LO0))
            if engine is nc.sync:
                engine.sem_inc(seen, 1)
            engine.wait_ge(lo_dve, q * (BATCHES - pool_all) + (n - pool_n + LO0))

        def squares(engine, body):
            with engine.Fori(0, KT) as it:
                with engine.Fori(0, KT) as kt:
                    body(it, kt, it * KT + kt)

        def stage_halves(g, half, m):
            tile = stage[g % SR][:, :, :]
            if g < G:
                return batch_of(tile.rearrange("p h (i c q) -> p h i c q", c=CH, q=2), 0, half, m)
            return batch_of(tile.rearrange("p h (q c i) -> p h q c i", q=2, c=CH), 1, half, m)

        def value_of(batch):
            return value[batch % 4][:, :, :].rearrange("p i (h c) -> p i h c", c=CH)

        with nc.Block() as block:
            @block.sync
            def _(sp):
                def body(it, kt, q):
                    def load(g):
                        sp.wait_ge(x_lo, q * G + (g + 1))
                        sp.dma_start(x[g % XR][:, :, :],
                                     p.x1[:, bass.ds(it * 128 + g * IB, IB), bass.ds(kt * 128, 128)]
                                     ).then_inc(loaded[g % XR], 16)
                    for g in range(XR):
                        load(g)
                    for g in range(2 * G):
                        wait_lo(sp, q, (g + 1) * B)
                        parts, rows, blk = (p.b_parts, it, kt * G + (g - G)) if g >= G else (p.a_parts, kt, it * G + g)
                        store_stage(sp, stage[g % SR], parts, rows, blk).then_inc(stored[g % SR], 16)
                        if g + XR < G:
                            load(g + XR)
                squares(sp, body)
                for k in range(SR):
                    sp.wait_ge(stored[k], 16 * (KT * KT * 2 * G // SR + 1))

            @block.tensor
            def _(pe):
                def body(it, kt, q):
                    for g in range(2 * G):
                        right = g >= G
                        if right:
                            wh, wl = p.lbh, p.lbl
                        else:
                            wh, wl = p.lah, p.lal
                            pe.wait_ge(x_lo, q * G + (g + 1 + XR))
                        for m in range(B):
                            n = g * B + m
                            pe.wait_ge(valued, q * BATCHES + (n + 1))
                            for u in range(QT):
                                t = (g % G) * IB + m * QT + u
                                hi = yh[:, :, t] if right else yh[:, t, :]
                                lo = yl[:, :, t] if right else yl[:, t, :]
                                dst = bank[n % 8][:, u, :]
                                pe.matmul(dst, lhsT=hi, rhs=wh[:, :], start=True, stop=False)
                                pe.matmul(dst, lhsT=hi, rhs=wl[:, :], start=False, stop=False)
                                last = pe.matmul(dst, lhsT=lo, rhs=wh[:, :], start=False, stop=True)
                            last.then_inc(projected, 1)
                pe.sem_inc(projected, PROJ0)
                squares(pe, body)

            @block.scalar
            def _(act):
                for k in range(SR):
                    act.sem_inc(stored[k], 16)

                def body(it, kt, q):
                    def split(g):
                        act.wait_ge(loaded[g % XR], (q * (G // XR) + (g // XR + 1)) * 16)
                        if g == 0:
                            act.wait_ge(projected, q * BATCHES + PROJ0)
                        act.activation(yh[:, g * IB:(g + 1) * IB, :], x[g % XR][:, :, :], ACT.Copy,
                                       scale=p.st1[:, 0:1]).then_inc(x_hi, 1)

                    def value_hi(g, m):
                        if m == 0:
                            act.wait_ge(stored[g % SR], (q * (2 * G // SR) + (g // SR + 1)) * 16)
                        n = g * B + m
                        act.wait_ge(valued, q * BATCHES + (n + 1 + VAL0))
                        act.activation(stage_halves(g, 0, m), value_of(n), ACT.Copy).then_inc(v_hi, 1)
                    split(0)
                    for g in range(2 * G):
                        if g + 1 < G:
                            split(g + 1)
                        for m in range(B):
                            value_hi(g, m)
                squares(act, body)

            @block.gpsimd
            def _(pool):
                pool.sem_inc(lo_pool, LO0)

                def body(it, kt, q):
                    for g in range(2 * G):
                        for m in range(B):
                            if pool_takes(g * B + m):
                                pool.wait_ge(v_hi, q * BATCHES + (g * B + m + 1))
                                pool.tensor_tensor(stage_halves(g, 1, m), value_of(g * B + m),
                                                   stage_halves(g, 0, m), ALU.subtract).then_inc(lo_pool, 1)
                squares(pool, body)

            @block.vector
            def _(dve):
                dve.sem_inc(valued, VAL0)
                dve.sem_inc(x_lo, XR)
                dve.sem_inc(lo_dve, LO0)

                def body(it, kt, q):
                    def split(g):
                        dve.wait_ge(x_hi, q * G + (g + 1))
                        at = slice(g * IB, (g + 1) * IB)
                        dve.scalar_tensor_tensor(out=yl[:, at, :], in0=x[g % XR][:, :, :], scalar=p.st1[:, 0:1],
                                                 in1=yh[:, at, :], op0=ALU.mult, op1=ALU.subtract).then_inc(x_lo, 1)
                    def value_lo(n):
                        if not pool_takes(n):
                            dve.wait_ge(v_hi, q * BATCHES + (n + 1))
                            dve.tensor_tensor(stage_halves(n // B, 1, n % B), value_of(n),
                                              stage_halves(n // B, 0, n % B), ALU.subtract).then_inc(lo_dve, 1)
                    split(0)
                    for g in range(2 * G):
                        if g + 1 < G:
                            split(g + 1)
                        for m in range(B):
                            n = g * B + m
                            wait_lo(dve, q, max(n - 3, 0))
                            dve.wait_ge(projected, q * BATCHES + (n + 1 + PROJ0))
                            dve.scalar_tensor_tensor(
                                out=value[n % 4][:, :, :].rearrange("p i c -> p (i c)"),
                                in0=bank[n % 8][:, :, :].rearrange("p i c -> p (i c)"), scalar=1.0 / WS,
                                in1=p.const1[:, int(g >= G), :, :].rearrange("p i c -> p (i c)"),
                                op0=ALU.mult, op1=ALU.add).then_inc(valued, 1)
                            if n:
                                value_lo(n - 1)
                    value_lo(BATCHES - 1)
                squares(dve, body)


def batch_of(stage, ab, half, m):
    at = slice(m * QT, (m + 1) * QT)
    if ab:
        return stage[:, :, half, :, at].rearrange("p h c i -> p i h c")
    return stage[:, :, at, :, half].rearrange("p h i c -> p i h c")


def store_stage(engine, stage, parts, k_tile, block):
    src = stage[:]
    if len(src.shape) == 5:
        src = src.rearrange("p h a b c -> p h (a b c)")
    dst = parts[:, bass.ds(k_tile, 1), :, bass.ds(block, 1), :]
    return engine.dma_start(dst.rearrange("h t p b n -> p (h t b) n"), src)


def build(nc, x, ln_vectors, W_proj, W_gate, W_ab, WaT, WbT, bias_ab, identity, centering, group_mean,
          expand, row_masks, out):
    io = dict(x=x, ln_vectors=ln_vectors, W_proj=W_proj, W_gate=W_gate, W_ab=W_ab, WaT=WaT, WbT=WbT,
              bias_ab=bias_ab, identity=identity, centering=centering, group_mean=group_mean,
              expand=expand, row_masks=row_masks)
    p = Plan()
    p.N = x.shape[1]
    p.KT = p.N // 128
    p.NB = p.N // IB
    N, KT = p.N, p.KT
    with ExitStack() as ctx:
        sb = lambda n, s, d: ctx.enter_context(nc.sbuf_tensor(n, s, d))
        p.sem = lambda n: ctx.enter_context(nc.semaphore(n))
        p.a_parts = nc.dram_tensor("a_parts", [NCH, KT, 128, p.NB, 2 * CH * IB], F16, kind="Internal").ap()
        p.b_parts = nc.dram_tensor("b_parts", [NCH, KT, 128, p.NB, 2 * CH * IB], F16, kind="Internal").ap()
        p.ab = nc.dram_tensor("ab_sum", [C, N, N], F32, kind="Internal").ap()
        p.x1 = nc.dram_tensor("x1", [C, N, N], F32, kind="Internal").ap()
        p.r1_rows = nc.dram_tensor("r1_rows", [3, N, N], F16, kind="Internal").ap()
        p.std_rows = nc.dram_tensor("std_rows", [3, N, N], F16, kind="Internal").ap()
        p.r2_rows = nc.dram_tensor("r2_rows", [2, N, N], F16, kind="Internal").ap()
        p.ident = sb("ident", [C, C], F32)
        p.ident16 = sb("ident16", [C, C], F16)
        p.ones = sb("ones", [C, C], F32)
        p.mean_mat = sb("mean_mat", [C, C], F32)
        p.group_mat = sb("group_mat", [C, C], F32)
        p.expand = sb("expand_sb", [NG, C], F32)
        p.wa_t, p.wb_t = sb("wa_t", [C, C], F32), sb("wb_t", [C, C], F32)
        p.bias_ab = sb("bias_sb", [1, 2 * C], F32)
        p.gh, p.gl, p.ah, p.al = (sb(n, [C, C], F16) for n in ("gh", "gl", "ah", "al"))
        p.lah, p.lal, p.lbh, p.lbl = (sb(n, [C, C], F16) for n in ("lah", "lal", "lbh", "lbl"))
        p.vg, p.v2 = sb("vg", [C, 1], F32), sb("v2", [C, 1], F32)
        p.st0 = sb("st0", [C, 4], F32)
        p.st1 = sb("st1", [C, 2], F32)
        p.s_rows = sb("s_rows", [4, C], F16)
        p.res_st = sb("res_st", [128, 2, C], F32)
        p.const1 = sb("const1", [C, 2, QT, C], F32)
        with ExitStack() as first:
            sf = lambda n, s, d: first.enter_context(nc.sbuf_tensor(n, s, d))
            p.wh, p.wl = sf("wh", [C, 4 * C], F16), sf("wl", [C, 4 * C], F16)
            p.r64 = sf("r64", [C, KT, N], F32)
            p.const_rows = sf("const_rows", [64, IB, 4 * C], F16)
            with ExitStack() as prep:
                sp_ = lambda n, s, d: prep.enter_context(nc.sbuf_tensor(n, s, d))
                p.w64 = sp_("w64", [C, 4 * C], F32)
                p.vh, p.vl = sp_("vh", [C, 4 * C], F16), sp_("vl", [C, 4 * C], F16)
                p.masks = sp_("masks", [C, 2 * IB + 2], F32)
                prepare_weights(nc, p, io)
                stats0(nc, p, io)
            project0(nc, p, io)
        mix(nc, p, "mix0_", p.ab, None)
        join0(nc, p, io)
        project1(nc, p)
        mix(nc, p, "mix1_", out, p.x1)


def shape_constants():
    import numpy as np
    eye = np.eye(C, dtype=np.float32)
    group = np.kron(np.eye(NG, dtype=np.float32), np.ones((GROUP, GROUP), np.float32))
    expand = np.kron(np.eye(NG, dtype=np.float32), np.ones((1, GROUP), np.float32))
    masks = np.zeros((C, 2 * IB + 2), np.float32)
    for t in range(IB):
        masks[t, t] = masks[IB + t, t] = 1
        masks[2 * IB + t, IB + t] = 1
    masks[3 * IB, 2 * IB] = masks[3 * IB + 1, 2 * IB + 1] = 1
    return dict(identity=eye, centering=eye - np.float32(1.0 / C), group_mean=group / np.float32(GROUP),
                expand=expand, row_masks=masks)


def kernel(x, L0_conv_ln1_g, L0_conv_ln1_b, L0_conv_W_proj, L0_conv_W_gate, L0_conv_ln2_g, L0_conv_ln2_b,
           L0_conv_W_ab, L1_conv_Wa, L1_conv_ba, L1_conv_Wb, L1_conv_bb):
    import numpy as np
    import concourse.bacc as bacc
    from concourse.bass_utils import run_bass_kernel_spmd

    f = lambda a: np.ascontiguousarray(a)
    arrays = dict(
        x=f(np.transpose(np.asarray(x)[0], (2, 0, 1))),
        ln_vectors=f(np.stack([L0_conv_ln1_g, L0_conv_ln1_b, L0_conv_ln2_g, L0_conv_ln2_b], axis=1)),
        W_proj=f(L0_conv_W_proj), W_gate=f(L0_conv_W_gate), W_ab=f(L0_conv_W_ab),
        WaT=f(np.transpose(L1_conv_Wa)), WbT=f(np.transpose(L1_conv_Wb)),
        bias_ab=f(np.concatenate([np.asarray(L1_conv_ba), np.asarray(L1_conv_bb)])[None, :]),
        **shape_constants())
    nc = bacc.Bacc("TRN2", target_bir_lowering=False, num_devices=1)
    args = {n: nc.dram_tensor("in_" + n, a.shape, F32, kind="ExternalInput").ap() for n, a in arrays.items()}
    N = arrays["x"].shape[1]
    out = nc.dram_tensor("out_0", (C, N, N), F32, kind="ExternalOutput").ap()
    build(nc, out=out, **args)
    r = run_bass_kernel_spmd(nc, [{"in_" + n: a for n, a in arrays.items()}], core_ids=[0])
    return np.transpose(r.results[0]["out_0"], (1, 2, 0))[None]
```

```python
import concourse.bass as bass
from concourse import mybir
from contextlib import ExitStack

F32 = mybir.dt.float32
F16 = mybir.dt.float16
ALU = mybir.AluOpType
ACT = mybir.ActivationFunctionType
AX = mybir.AxisListType

C = 128
GROUP = 4
NG = C // GROUP
IB = 16
CH = 8
NCH = C // CH
WS = 64.0
EPS = 1e-5
QT = 4


class Plan:
    pass


def chained(engine, sem):
    count = [0]

    def step(ins):
        count[0] += 1
        ins.then_inc(sem, 1)
        engine.wait_ge(sem, count[0])
        return ins
    return step


def refined_rsqrt(dve, step, r, var, scratch):
    step(dve.tensor_tensor(scratch, r, r, ALU.mult))
    step(dve.tensor_tensor(scratch, scratch, var, ALU.mult))
    step(dve.tensor_scalar(scratch, scratch, -0.5, 1.5, ALU.mult, ALU.add))
    step(dve.tensor_tensor(r, r, scratch, ALU.mult))


def prepare_weights(nc, p, io):
    with ExitStack() as ctx:
        sb = lambda n, s, d: ctx.enter_context(nc.sbuf_tensor(n, s, d))
        w_proj = sb("w_proj", [C, 4 * C], F32)
        w_gate = sb("w_gate", [C, C], F32)
        w_ab = sb("w_ab", [C, C], F32)
        vec = sb("vec", [C, 4], F32)
        center = sb("center", [C, C], F32)
        scaled = sb("scaled", [C, 4 * C], F32)
        b1_bc = sb("b1_bc", [C, C], F32)
        psw = ctx.enter_context(nc.psum_tensor("psw", [C, 512], F32))
        psv = ctx.enter_context(nc.psum_tensor("psv", [C, 512], F32))
        loaded = p.sem("weights_loaded")
        dve_step = p.sem("w_dve_step")
        ready = p.sem("w_operand_ready")
        product = p.sem("w_product")
        with nc.Block() as block:
            @block.sync
            def _(sp):
                for dst, src in ((w_proj, io["W_proj"]), (w_gate, io["W_gate"]), (w_ab, io["W_ab"]),
                                 (vec, io["ln_vectors"]), (center, io["centering"]),
                                 (p.wa_t, io["WaT"]), (p.wb_t, io["WbT"]),
                                 (p.ident, io["identity"]), (p.masks, io["row_masks"]),
                                 (p.expand, io["expand"]), (p.bias_ab, io["bias_ab"]),
                                 (p.group_mat, io["group_mean"])):
                    sp.dma_start(dst[:, :], src).then_inc(loaded, 16)

            @block.vector
            def _(dve):
                step = chained(dve, dve_step)
                dve.wait_ge(loaded, 16 * 12)
                step(dve.memset(p.ones[:, :], 1.0))
                step(dve.memset(p.mean_mat[:, :], 1.0 / C))
                step(dve.tensor_copy(p.ident16[:, :], p.ident[:, :]))
                jobs = [(w_proj, vec[:, 0:1], 4 * C, p.w64, p.wh, p.wl),
                        (w_gate, vec[:, 0:1], C, None, p.gh, p.gl),
                        (w_ab, vec[:, 2:3], C, None, p.ah, p.al)]
                for n, (w, gain, width, keep, hi, lo) in enumerate(jobs):
                    dve.tensor_scalar(scaled[:, 0:width], w[:, 0:width], gain, None, ALU.mult).then_inc(ready, 1)
                    dve.wait_ge(product, n + 1)
                    dst = keep if keep is not None else scaled
                    if width == 4 * C:
                        out = dst[:, :].rearrange("c (h s f) -> c s h f", h=2, s=2)
                        step(dve.tensor_scalar(out, psw[:, :].rearrange("c (s h f) -> c s h f", s=2, h=2),
                                               WS, None, ALU.mult))
                    else:
                        step(dve.tensor_scalar(dst[:, 0:width], psw[:, 0:width], WS, None, ALU.mult))
                    step(dve.tensor_copy(hi[:, :], dst[:, 0:width]))
                    step(dve.tensor_tensor(lo[:, :], dst[:, 0:width], hi[:, :], ALU.subtract))
                step(dve.tensor_scalar(b1_bc[:, :], p.ones[:, :], vec[:, 1:2], None, ALU.mult))
                dve.sem_inc(ready, 1)
                dve.wait_ge(product, 4)
                out = scaled[:, :].rearrange("c (h s f) -> c s h f", h=2, s=2)
                step(dve.tensor_scalar(out, psw[:, :].rearrange("c (s h f) -> c s h f", s=2, h=2),
                                       WS, None, ALU.mult))
                step(dve.tensor_copy(p.v_rows[:, :], scaled[0:64, :]))
                step(dve.tensor_tensor(p.v_rows[32:64, :], scaled[32:64, :], p.v_rows[32:64, :], ALU.subtract))
                dve.wait_ge(product, 5)
                step(dve.tensor_copy(p.vg[:, :], psv[:, 0:1]))
                step(dve.tensor_scalar(p.v2[:, :], psv[:, 1:2], WS, None, ALU.mult))
                for w, hi, lo in ((p.wa_t, p.lah, p.lal), (p.wb_t, p.lbh, p.lbl)):
                    step(dve.tensor_scalar(scaled[:, 0:C], w[:, :], WS, None, ALU.mult))
                    step(dve.tensor_copy(hi[:, :], scaled[:, 0:C]))
                    step(dve.tensor_tensor(lo[:, :], scaled[:, 0:C], hi[:, :], ALU.subtract))

            @block.tensor
            def _(pe):
                for n, width in enumerate((4 * C, C, C)):
                    pe.wait_ge(ready, n + 1)
                    pe.matmul(psw[:, 0:width], lhsT=center[:, :], rhs=scaled[:, 0:width],
                              start=True, stop=True).then_inc(product, 1)
                pe.wait_ge(ready, 4)
                pe.matmul(psw[:, :], lhsT=b1_bc[:, :], rhs=w_proj[:, :], start=True, stop=True).then_inc(product, 1)
                pe.matmul(psv[:, 0:1], lhsT=w_gate[:, :], rhs=vec[:, 1:2], start=True, stop=True)
                pe.matmul(psv[:, 1:2], lhsT=w_ab[:, :], rhs=vec[:, 3:4], start=True, stop=True).then_inc(product, 1)


def stats0(nc, p, io):
    N, KT = p.N, p.KT
    ROW = KT * N
    XR = 4
    x_by_channel = io["x"].rearrange("c (t p) k -> c p t k", p=128)
    with ExitStack() as ctx:
        sb = lambda n, s, d: ctx.enter_context(nc.sbuf_tensor(n, s, d))
        ps = lambda n: ctx.enter_context(nc.psum_tensor(n, [128, 512], F32))
        xg = [p.x_rows[k][:, :, :].rearrange("p i k -> p (i k)")[:, 0:GROUP * ROW].rearrange(
            "p (c t k) -> p c t k", c=GROUP, t=KT) for k in range(2)]
        xg += [sb(f"xg{k}", [128, GROUP, KT, N], F32)[:, :, :, :] for k in range(2, XR)]
        sq = [sb(f"sq{k}", [128, GROUP, ROW], F32) for k in range(2)]
        csum = [sb(f"csum{k}", [128, ROW], F32) for k in range(2)]
        S1 = sb("S1", [128, ROW], F32)
        zeros = sb("zeros", [128, N], F32)
        scratch = sb("scratch", [128, (GROUP - 1) * ROW], F32)
        scratch3 = sb("scratch3", [128, ROW], F32)
        part = [sb(f"part{k}", [128, 4], F32) for k in range(2)]
        gst = [sb(f"gst{k}", [128, 8], F32) for k in range(2)]
        all_st = sb("all_st", [128, 3, NG], F32)
        expo = sb("expo", [128, 2], F32)
        diag = sb("diag", [NG, 3, NG], F32)
        cols = sb("cols", [NG, 3], F32)
        tbar = sb("tbar", [128, 2], F32)
        t_bc = sb("t_bc", [C, C], F32)
        kap = sb("kap", [C, 512], F32)
        kh = sb("kh", [C, 512], F16)
        kl = sb("kl", [C, 512], F16)
        mu = csum[0]
        rstd = sq[0]
        var = sq[1][:, 0, :]
        halves = sb("halves", [128, 2, 2, ROW], F16)
        s3 = sb("s3", [C, 4], F16)
        psS2 = [ps(f"psS2_{t}") for t in range(KT)]
        psG = ps("psG")
        psK = ps("psK")
        psH = ctx.enter_context(nc.psum_tensor("psH", [128, 128], F16))
        xload = [p.sem(f"xg_loaded{k}") for k in range(XR)]
        consts = p.sem("stats_consts")
        dve_step = p.sem("stats_dve_step")
        act_sums = p.sem("sums_by_act")
        dve_sums = p.sem("sums_by_dve")
        csum_full = p.sem("csum_full")
        gmean = p.sem("gmean_ready")
        gvar = p.sem("gvar_ready")
        s_ready = p.sem("s_ready")
        st_ready = p.sem("st_ready")
        sq_ready = p.sem("sq_ready")
        s2_added = p.sem("s2_added")
        csum_ready = p.sem("csum_ready")
        s1_added = p.sem("s1_added")
        pool_step = p.sem("stats_pool_step")
        col_ready = p.sem("col_ready")
        prod = p.sem("stats_product")
        var_ready = p.sem("var_ready")
        rstd_ready = p.sem("rstd_ready")
        halves_ready = p.sem("halves_ready")
        stored = p.sem("rstd_stored")
        root_ready = p.sem("root_ready")
        rows_set = p.sem("const_rows_set")
        kappa_ready = p.sem("kappa_ready")
        kappa_stored = p.sem("kappa_stored")
        BODIES = NG // XR

        def channel(k, c):
            return xg[k][:, c, :, :].rearrange("p t k -> p (t k)")

        with nc.Block() as block:
            @block.sync
            def _(sp):
                def load(k, first):
                    for c in range(GROUP):
                        sp.dma_start(xg[k][:, c, :, :], x_by_channel[first + c]).then_inc(xload[k], 16)
                for k in range(XR):
                    load(k, GROUP * k)
                with sp.Fori(0, BODIES - 1) as i:
                    for k in range(XR):
                        sp.wait_ge(sq_ready, XR * i + k + 1)
                        load(k, (XR * i + XR + k) * GROUP)
                for k in range(2):
                    g = NG - XR + k
                    sp.wait_ge(sq_ready, g + 1)
                    sp.dma_start(p.x_rows[k][:, :, :], io["x"][:, k * IB:(k + 1) * IB, :]).then_inc(p.x_loaded[k], 16)

                def store_rows(q, dst):
                    for row, half in enumerate((0, 1, 0)):
                        sp.dma_start(dst[row].rearrange("(t p) k -> p t k", p=128),
                                     halves[:, q, half, :].rearrange("p (t k) -> p t k", t=KT)).then_inc(stored, 16)
                sp.wait_ge(halves_ready, 1)
                store_rows(1, p.std_rows)
                sp.wait_ge(rows_set, IB)
                sp.wait_ge(kappa_ready, 1)
                for row, src in enumerate((kh, kl)):
                    sp.dma_start(p.kappa_rows[row], src[0:IB, :]).then_inc(kappa_stored, 16)
                sp.wait_ge(halves_ready, 2)
                store_rows(0, p.r1_rows)
                sp.wait_ge(kappa_stored, 32)
                sp.dma_start(p.const_rows[3 * IB:3 * IB + 2, :, :], p.kappa_rows[:, :, :]).then_inc(stored, 16)
                sp.wait_ge(stored, 16 * 7)

            @block.gpsimd
            def _(pool):
                pool.memset(expo[:, 0:1], -0.5).then_inc(pool_step, 1)
                pool.wait_ge(pool_step, 1)

                def add_channels(i, k):
                    g, c2 = XR * i + k, csum[k % 2]
                    pool.wait_ge(xload[k], (i + 1) * (16 * GROUP))
                    pool.wait_ge(s1_added, g + 1)
                    pool.tensor_tensor(c2[:, :], channel(k, 0), channel(k, 1), ALU.add).then_inc(pool_step, 1)
                    pool.wait_ge(pool_step, g + 2)
                    pool.tensor_tensor(c2[:, :], c2[:, :], channel(k, 2), ALU.add).then_inc(csum_ready, 1)

                def body(i, more):
                    for k in range(XR):
                        if k + 1 < XR:
                            add_channels(i, k + 1)
                        elif more:
                            add_channels(i + 1, 0)
                        pool.wait_ge(gvar, XR * i + k + 1)
                        pool.tensor_tensor(gst[k % 2][:, 3:4], gst[k % 2][:, 7:8], expo[:, 0:1], ALU.pow
                                           ).then_inc(s_ready, 1)
                add_channels(0, 0)
                with pool.Fori(0, BODIES - 1) as i:
                    body(i, True)
                body(BODIES - 1, False)

            @block.scalar
            def _(act):
                for t in range(IB):
                    act.activation(p.const_rows[:, t, :], p.v_rows[:, :], ACT.Copy,
                                   scale=p.masks[0:64, t:t + 1]).then_inc(rows_set, 1)
                act.sem_inc(act_sums, 1)

                def sum_squares(i, k):
                    act.wait_ge(xload[k], (i + 1) * (16 * GROUP))
                    act.wait_ge(act_sums, XR * i + k + 1)
                    act.activation(scratch[:, :], xg[k][:, 0:GROUP - 1, :, :].rearrange("p c t k -> p (c t k)"),
                                   ACT.Square, accum_out=part[k % 2][:, 1:2]).then_inc(act_sums, 1)

                def body(i, more):
                    for k in range(XR):
                        if k + 1 < XR:
                            sum_squares(i, k + 1)
                        elif more:
                            sum_squares(i + 1, 0)
                        act.wait_ge(st_ready, XR * i + k + 1)
                        act.wait_ge(s2_added, XR * i + k + 1)
                        act.activation(sq[k % 2][:, :, :].rearrange("p c n -> p (c n)"),
                                       xg[k][:, :, :, :].rearrange("p c t k -> p (c t k)"),
                                       ACT.Square, scale=gst[k % 2][:, 3:4], bias=gst[k % 2][:, 4:5]
                                       ).then_inc(sq_ready, 1)
                sum_squares(0, 0)
                with act.Fori(0, BODIES - 1) as i:
                    body(i, True)
                body(BODIES - 1, False)
                act.wait_ge(var_ready, 1)
                act.activation(rstd[:, 1, :], var, ACT.Sqrt).then_inc(root_ready, 1)

            @block.tensor
            def _(pe):
                pe.wait_ge(consts, 1)
                for t in range(KT):
                    pe.matmul(psS2[t][:, 0:N], lhsT=p.ident[:, :], rhs=zeros[:, :], start=True, stop=False)
                pe.sem_inc(s2_added, 2)

                def group_mean(i, k):
                    pe.wait_ge(act_sums, XR * i + k + 2)
                    pe.wait_ge(dve_sums, XR * i + k + 2)
                    pe.matmul(psG[:, 0:3], lhsT=p.mean_mat[:, :], rhs=part[k % 2][:, 0:3],
                              start=True, stop=True).then_inc(gmean, 1)

                def add_squares(i, k, last_group=False):
                    pe.wait_ge(sq_ready, XR * i + k + 1)
                    for c in range(GROUP):
                        for t in range(KT):
                            last = pe.matmul(psS2[t][:, 0:N], lhsT=p.ident[:, :],
                                             rhs=sq[k % 2][:, c, t * N:(t + 1) * N], start=False,
                                             stop=last_group and c == GROUP - 1)
                    last.then_inc(s2_added, 1)

                def body(i, more):
                    for k in range(XR):
                        if k + 1 < XR:
                            group_mean(i, k + 1)
                        elif more:
                            group_mean(i + 1, 0)
                        add_squares(i, k, k == XR - 1 and not more)
                group_mean(0, 0)
                with pe.Fori(0, BODIES - 1) as i:
                    body(i, True)
                body(BODIES - 1, False)
                pe.wait_ge(col_ready, 1)
                pe.matmul(psG[:, 0:3], lhsT=p.expand[:, :], rhs=cols[:, :], start=True, stop=True).then_inc(prod, 1)
                pe.wait_ge(col_ready, 2)
                pe.matmul(psK[:, :], lhsT=t_bc[:, :], rhs=p.w64[:, :], start=True, stop=True).then_inc(prod, 1)
                pe.wait_ge(col_ready, 3)
                pe.transpose(psH[0:4, :], s3[:, :], p.ident16[:, :]).then_inc(prod, 1)
                pe.wait_ge(rstd_ready, 1)
                for kt in range(KT):
                    for t in range(KT):
                        last = pe.transpose(psS2[kt][:, t * 128:(t + 1) * 128],
                                            rstd[:, 0, t * N + kt * 128:t * N + kt * 128 + 128], p.ident[:, :])
                    last.then_inc(prod, 1)

            @block.vector
            def _(dve):
                step = chained(dve, dve_step)
                step(dve.memset(S1[:, :], 0.0))
                dve.memset(zeros[:, :], 0.0).then_inc(consts, 1)
                dve.sem_inc(s1_added, 2)
                dve.sem_inc(dve_sums, 1)
                LOOP0 = 1
                FIRST, SECOND = 4, 3

                def sums(i, k):
                    g, h = XR * i + k, k % 2
                    dve.wait_ge(xload[k], (i + 1) * (16 * GROUP))
                    dve.wait_ge(csum_ready, g + 1)
                    dve.scalar_tensor_tensor(out=csum[h][:, :], in0=channel(k, GROUP - 1), scalar=1.0,
                                             in1=csum[h][:, :], op0=ALU.mult, op1=ALU.add,
                                             accum_out=part[h][:, 0:1]).then_inc(csum_full, 1)
                    dve.wait_ge(dve_sums, g + 1)
                    dve.scalar_tensor_tensor(out=scratch3[:, :], in0=channel(k, GROUP - 1), scalar=1.0,
                                             in1=channel(k, GROUP - 1), op0=ALU.mult, op1=ALU.mult,
                                             accum_out=part[h][:, 2:3]).then_inc(dve_sums, 1)

                def link(g, second, n):
                    base = LOOP0 + (FIRST if second else 0) + n
                    return lambda ins: (ins.then_inc(dve_step, 1),
                                        dve.wait_ge(dve_step, g * (FIRST + SECOND) + base))

                def variance(i, k):
                    g, h = XR * i + k, k % 2
                    dve.wait_ge(gmean, g + 1)
                    link(g, 0, 1)(dve.tensor_scalar(gst[h][:, 0:3], psG[:, 0:3], 1.0 / (GROUP * ROW), None, ALU.mult))
                    link(g, 0, 2)(dve.tensor_tensor(gst[h][:, 6:7], gst[h][:, 0:1], gst[h][:, 0:1], ALU.mult))
                    link(g, 0, 3)(dve.scalar_tensor_tensor(out=gst[h][:, 7:8], in0=gst[h][:, 1:2],
                                                           scalar=gst[h][:, 2:3], in1=gst[h][:, 6:7],
                                                           op0=ALU.add, op1=ALU.subtract))
                    link(g, 0, 4)(dve.tensor_scalar(gst[h][:, 5:6], gst[h][:, 0:1], -1.0, None, ALU.mult))
                    dve.tensor_scalar(gst[h][:, 7:8], gst[h][:, 7:8], 0.0, EPS, ALU.max, ALU.add).then_inc(gvar, 1)

                def apply(i, k):
                    g, h = XR * i + k, k % 2
                    dve.wait_ge(s_ready, g + 1)
                    dve.tensor_tensor(gst[h][:, 4:5], gst[h][:, 5:6], gst[h][:, 3:4], ALU.mult).then_inc(st_ready, 1)
                    dve.wait_ge(st_ready, g + 1)
                    link(g, 1, 1)(dve.tensor_copy(all_st[:, 0, bass.ds(g, 1)], gst[h][:, 3:4]))
                    link(g, 1, 2)(dve.tensor_copy(all_st[:, 1, bass.ds(g, 1)], gst[h][:, 4:5]))
                    link(g, 1, 3)(dve.tensor_copy(all_st[:, 2, bass.ds(g, 1)], gst[h][:, 5:6]))
                    dve.wait_ge(csum_full, g + 1)
                    dve.scalar_tensor_tensor(out=S1[:, :], in0=csum[h][:, :], scalar=gst[h][:, 3:4],
                                             in1=S1[:, :], op0=ALU.mult, op1=ALU.add).then_inc(s1_added, 1)
                    dve.wait_ge(s1_added, g + 3)

                def body(i, more):
                    for k in range(XR):
                        apply(i, k)
                        if k + 1 < XR:
                            sums(i, k + 1)
                            variance(i, k + 1)
                        elif more:
                            sums(i + 1, 0)
                            variance(i + 1, 0)
                sums(0, 0)
                variance(0, 0)
                with dve.Fori(0, BODIES - 1) as i:
                    body(i, True)
                body(BODIES - 1, False)
                total = [LOOP0 + (FIRST + SECOND) * NG]

                def step(ins):
                    total[0] += 1
                    ins.then_inc(dve_step, 1)
                    dve.wait_ge(dve_step, total[0])
                for q in range(3):
                    step(dve.tensor_tensor(diag[:, q, :], all_st[0:NG, q, :], p.ident[0:NG, 0:NG], ALU.mult))
                step(dve.tensor_reduce(cols[:, :], diag[:, :, :], axis=AX.X, op=ALU.add))
                dve.sem_inc(col_ready, 1)
                step(dve.tensor_reduce(tbar[:, 0:1], all_st[:, 1, :], axis=AX.X, op=ALU.add))
                step(dve.tensor_scalar(tbar[:, 1:2], tbar[:, 0:1], 1.0 / NG, None, ALU.mult))
                step(dve.tensor_scalar(mu[:, :], S1[:, :], 1.0 / C, tbar[:, 1:2], ALU.mult, ALU.add))
                step(dve.tensor_tensor(mu[:, :], mu[:, :], mu[:, :], ALU.mult))
                dve.wait_ge(s2_added, NG + 2)
                for t in range(KT):
                    step(dve.scalar_tensor_tensor(out=sq[1][:, 0, t * N:(t + 1) * N], in0=psS2[t][:, 0:N],
                                                  scalar=1.0 / C, in1=mu[:, t * N:(t + 1) * N],
                                                  op0=ALU.mult, op1=ALU.subtract))
                dve.tensor_scalar(var, var, 0.0, EPS, ALU.max, ALU.add).then_inc(var_ready, 1)
                dve.wait_ge(prod, 1)
                step(dve.tensor_copy(p.st0[:, 0:3], psG[:, 0:3]))
                step(dve.tensor_scalar(t_bc[:, :], p.ones[:, :], p.st0[:, 1:2], None, ALU.mult))
                dve.sem_inc(col_ready, 1)
                step(dve.tensor_copy(s3[:, 0:1], p.st0[:, 0:1]))
                step(dve.tensor_copy(s3[:, 1:2], p.st0[:, 0:1]))
                step(dve.tensor_tensor(s3[:, 2:3], p.st0[:, 0:1], s3[:, 0:1], ALU.subtract))
                step(dve.memset(s3[:, 3:4], 0.0))
                dve.sem_inc(col_ready, 1)
                dve.wait_ge(root_ready, 1)
                step(dve.reciprocal(rstd[:, 0, :], rstd[:, 1, :]))
                refined_rsqrt(dve, step, rstd[:, 0, :], var, mu[:, :])
                dve.sem_inc(rstd_ready, 1)
                step(dve.tensor_tensor(rstd[:, 1, :], rstd[:, 0, :], var, ALU.mult))

                def split(q):
                    step(dve.tensor_copy(halves[:, q, 0, :], rstd[:, q, :]))
                    step(dve.tensor_tensor(halves[:, q, 1, :], rstd[:, q, :], halves[:, q, 0, :], ALU.subtract))
                    dve.sem_inc(halves_ready, 1)
                split(1)
                dve.wait_ge(prod, 2)
                step(dve.tensor_copy(kap[:, :], psK[:, :]))
                step(dve.tensor_copy(kh[:, :], kap[:, :]))
                step(dve.tensor_tensor(kl[:, :], kap[:, :], kh[:, :], ALU.subtract))
                dve.sem_inc(kappa_ready, 1)
                split(0)
                dve.wait_ge(prod, 3)
                step(dve.tensor_copy(p.s_rows[:, :], psH[0:4, :]))
                for kt in range(KT):
                    dve.wait_ge(prod, 4 + kt)
                    step(dve.tensor_scalar(p.r64[:, kt, :], psS2[kt][:, 0:N], 1.0 / WS, None, ALU.mult))


def project0(nc, p, io):
    N, KT, NB = p.N, p.KT, p.NB
    NK = 3 * IB + 2
    with ExitStack() as ctx:
        sb = lambda n, s, d: ctx.enter_context(nc.sbuf_tensor("pj_" + n, s, d))
        x = p.x_rows
        yh = [sb(f"yh{k}", [C, IB, 128], F16) for k in range(2)]
        yl = [sb(f"yl{k}", [C, IB, 128], F16) for k in range(2)]
        std = [sb(f"std{k}", [64, N], F16) for k in range(2)]
        r_body = sb("r_body", [128, KT, 2 * IB], F32)
        sig = sb("sig", [128, 8, 2 * C], F32)
        prod = sb("prod", [128, 8, 2, C], F32)
        stage_a = [sb(f"stage_a{k}", [128, NCH, IB, CH, 2], F16) for k in range(2)]
        stage_b = [sb(f"stage_b{k}", [128, NCH, 2, CH, IB], F16) for k in range(2)]
        bank = [ctx.enter_context(nc.psum_tensor(f"bank{k}", [128, 4 * C], F32)) for k in range(8)]
        x_loaded = p.x_loaded
        std_loaded = [p.sem(f"std_loaded{k}") for k in range(2)]
        split = p.sem("y_split")
        projected = p.sem("projected")
        sig_done = p.sem("sig_done")
        prod_done = p.sem("prod_done")
        hi_done = p.sem("ab_hi_done")
        lo_a = p.sem("a_lo_done")
        lo_b = p.sem("b_lo_done")
        stored = [p.sem(f"ab_stored{k}") for k in range(2)]
        ones_set = p.sem("ones_set")
        yh_done = p.sem("yh_done")
        r_copied = p.sem("r_copied")
        CREDIT = 2 * IB

        BODY = 2 * KT
        TILES = BODY * IB
        BATCH = TILES // QT
        BODIES = NB // 2

        def staged(b, ab, half, m):
            return batch_of(stage_b[b % 2] if ab else stage_a[b % 2], ab, half, m % (IB // QT))

        with nc.Block() as block:
            @block.sync
            def _(sp):
                def load(row, k, with_x=True):
                    if with_x:
                        sp.dma_start(x[k][:, :, :], io["x"][:, bass.ds(row * IB, IB), :]).then_inc(x_loaded[k], 16)
                    for h in range(3):
                        sp.dma_start(std[k][h * IB:(h + 1) * IB, :],
                                     p.std_rows[h, bass.ds(row * IB, IB), :]).then_inc(std_loaded[k], 16)

                def store(i, b):
                    sp.wait_ge(lo_a, i * BATCH + (b + 1) * IB // QT)
                    sp.wait_ge(lo_b, i * BATCH + (b + 1) * IB // QT)
                    for stage, dst in ((stage_a, p.a_parts), (stage_b, p.b_parts)):
                        store_stage(sp, stage[b % 2], dst, b % KT, 2 * i + b // KT).then_inc(stored[b % 2], 16)
                sp.wait_ge(ones_set, 1)
                for k in range(2):
                    load(k, k, with_x=False)

                def body(i, more):
                    for b in range(BODY):
                        store(i, b)
                        if more and b % KT == KT - 1:
                            k = b // KT
                            load(2 * i + 2 + k, k)
                with sp.Fori(0, BODIES - 1) as i:
                    body(i, True)
                body(BODIES - 1, False)
                for k in range(2):
                    sp.wait_ge(stored[k], 32 * (BODIES * BODY // 2 + 1))

            @block.vector
            def _(dve):
                for k in range(2):
                    last = dve.memset(std[k][32:64, :], 1.0)
                last.then_inc(ones_set, 1)
                dve.sem_inc(prod_done, 8)

                def split_block(i, b):
                    k, kt = (b // KT) % 2, b % KT
                    it = i + (b // BODY)
                    if b % KT == 0:
                        dve.wait_ge(x_loaded[k], (it + 1) * 16)
                    blk = i * BODY + b
                    dve.wait_ge(projected, blk * IB + IB)
                    src = x[k][:, :, kt * 128:(kt + 1) * 128]
                    dve.tensor_scalar(yh[b % 2][:, :, :], src, p.st0[:, 0:1], None, ALU.mult).then_inc(yh_done, 1)
                    dve.wait_ge(yh_done, blk + 1)
                    dve.scalar_tensor_tensor(out=yl[b % 2][:, :, :], in0=src, scalar=p.st0[:, 0:1],
                                             in1=yh[b % 2][:, :, :], op0=ALU.mult, op1=ALU.subtract
                                             ).then_inc(split, 1)

                def lo_of_b(i, m):
                    b = m // (IB // QT)
                    dve.wait_ge(hi_done, i * BATCH + m + 1)
                    slot = QT * (m % 2)
                    dve.tensor_tensor(staged(b, 1, 1, m),
                                      prod[:, slot:slot + QT, 1, :].rearrange("p i (h c) -> p i h c", c=CH),
                                      staged(b, 1, 0, m), ALU.subtract).then_inc(lo_b, 1)

                def body(i, more):
                    dve.tensor_copy(r_body[:, :, :], p.r64[:, :, bass.ds(i * (2 * IB), 2 * IB)]).then_inc(r_copied, 1)
                    dve.wait_ge(r_copied, i + 1)
                    for b in range(BODY):
                        k, kt = b // KT, b % KT
                        for m in range(b * IB // QT, (b + 1) * IB // QT):
                            if m >= 2:
                                dve.wait_ge(lo_b, i * BATCH + m - 1)
                                dve.wait_ge(lo_a, i * BATCH + m - 1)
                            for q in range(QT):
                                n = m * QT + q
                                dve.wait_ge(sig_done, i * TILES + n + 1)
                                dve.scalar_tensor_tensor(
                                    out=prod[:, n % 8, :, :].rearrange("p s c -> p (s c)"),
                                    in0=bank[n % 8][:, 2 * C:4 * C],
                                    scalar=r_body[:, kt, k * IB + n % IB:k * IB + n % IB + 1],
                                    in1=sig[:, n % 8, :], op0=ALU.mult, op1=ALU.mult).then_inc(prod_done, 1)
                            if m >= 1:
                                lo_of_b(i, m - 1)
                            if m == b * IB // QT + 1 and (more or b + 1 < BODY):
                                split_block(i, b + 1)
                    lo_of_b(i, BATCH - 1)
                    dve.wait_ge(lo_b, i * BATCH + BATCH)
                    dve.wait_ge(lo_a, i * BATCH + BATCH)
                split_block(0, 0)
                with dve.Fori(0, BODIES - 1) as i:
                    body(i, True)
                body(BODIES - 1, False)

            @block.gpsimd
            def _(pool):
                def body(i):
                    for m in range(BATCH):
                        b = m // (IB // QT)
                        pool.wait_ge(hi_done, i * BATCH + m + 1)
                        slot = QT * (m % 2)
                        pool.tensor_tensor(staged(b, 0, 1, m),
                                           prod[:, slot:slot + QT, 0, :].rearrange("p i (h c) -> p i h c", c=CH),
                                           staged(b, 0, 0, m), ALU.subtract).then_inc(lo_a, 1)
                with pool.Fori(0, BODIES) as i:
                    body(i)

            @block.scalar
            def _(act):
                act.sem_inc(stored[0], 32)
                act.sem_inc(stored[1], 32)

                def hi_of(i, m):
                    b = m // (IB // QT)
                    if m % (IB // QT) == 0:
                        act.wait_ge(stored[b % 2], (i * (BODY // 2) + b // 2 + 1) * 32)
                    act.wait_ge(prod_done, i * TILES + (m + 1) * QT + 8)
                    slot = QT * (m % 2)
                    for ab in range(2):
                        last = act.activation(staged(b, ab, 0, m),
                                              prod[:, slot:slot + QT, ab, :].rearrange("p i (h c) -> p i h c", c=CH),
                                              ACT.Copy)
                    last.then_inc(hi_done, 1)

                with act.Fori(0, BODIES) as i:
                    act.wait_ge(r_copied, i + 1)
                    for m in range(BATCH):
                        for q in range(QT):
                            n = m * QT + q
                            kt, at = (n // IB) % KT, n // (IB * KT) * IB + n % IB
                            act.wait_ge(projected, i * TILES + (n + 1 + CREDIT))
                            act.activation(sig[:, n % 8, :], bank[n % 8][:, 0:2 * C], ACT.Sigmoid,
                                           scale=r_body[:, kt, at:at + 1]).then_inc(sig_done, 1)
                        if m:
                            hi_of(i, m - 1)
                    hi_of(i, BATCH - 1)

            @block.tensor
            def _(pe):
                pe.sem_inc(projected, CREDIT)
                with pe.Fori(0, BODIES) as i:
                    for b in range(BODY):
                        k, kt = b // KT, b % KT
                        pe.wait_ge(split, i * BODY + b + 1)
                        if kt == 0:
                            pe.wait_ge(std_loaded[k], (i + 1) * 48)
                        for t in range(IB):
                            n = b * IB + t
                            out = bank[n % 8][:, :]
                            pe.wait_ge(prod_done, i * TILES + n + 1)
                            pe.matmul(out, lhsT=yh[b % 2][:, t, :], rhs=p.wh[:, :], start=True, stop=False)
                            pe.matmul(out, lhsT=yh[b % 2][:, t, :], rhs=p.wl[:, :], start=False, stop=False)
                            pe.matmul(out, lhsT=yl[b % 2][:, t, :], rhs=p.wh[:, :], start=False, stop=False)
                            pe.matmul(out, lhsT=std[k][0:NK, kt * 128:(kt + 1) * 128],
                                      rhs=p.const_rows[0:NK, t, :], start=False, stop=True).then_inc(projected, 1)


def mix(nc, p, name, out, residual):
    N, KT, NB = p.N, p.KT, p.NB
    ROW = KT * N
    with ExitStack() as ctx:
        sb = lambda n, s, d: ctx.enter_context(nc.sbuf_tensor(name + n, s, d))
        pa = [sb(f"pa{k}", [128, KT, N, CH, 2], F16) for k in range(2)]
        pb = [sb(f"pb{k}", [128, KT, NB, 2, CH, IB], F16) for k in range(2)]
        OR = 4
        o = [sb(f"o{k}", [128, KT, N], F32) for k in range(OR)]
        bank = [[ctx.enter_context(nc.psum_tensor(f"{name}bank{k}_{t}", [128, 512], F32)) for t in range(KT)]
                for k in range(2)]
        loaded = [p.sem(f"{name}_parts_loaded{k}") for k in range(2)]
        mixed = p.sem(f"{name}_mixed")
        evacuated = p.sem(f"{name}_evacuated")
        stored = [p.sem(f"{name}_stored{k}") for k in range(OR)]
        out_v = out.rearrange("c (t p) j -> c p t j", p=128)
        sums = residual is None
        if sums:
            sq = [sb(f"sq{k}", [128, ROW], F32) for k in range(2)]
            S1 = sb("S1", [128, ROW], F32)
            S2 = sb("S2", [128, ROW], F32)
            halves = sb("halves", [128, 2, ROW], F16)
            sq_ready = p.sem(f"{name}_sq_ready")
            s1_added = p.sem(f"{name}_s1_added")
            s2_added = p.sem(f"{name}_s2_added")
            var_ready = p.sem(f"{name}_var_ready")
            root_ready = p.sem(f"{name}_root_ready")
            tail = p.sem(f"{name}_tail")
            halves_ready = p.sem(f"{name}_halves_ready")
            rows_stored = p.sem(f"{name}_rows_stored")
            init = p.sem(f"{name}_init")
        else:
            res = [sb(f"res{k}", [128, KT, N], F32) for k in range(OR)]
            res_loaded = [p.sem(f"{name}_res_loaded{k}") for k in range(OR)]
            res_v = residual.rearrange("c (t p) j -> c p t j", p=128)
            st = sb("st", [128, 2, 2 * CH], F32)
            scaled = p.sem(f"{name}_residual_scaled")
            st_ready = p.sem(f"{name}_factors_ready")
        BODY = 2 * CH
        BODIES = NCH // 2
        PIECES = ((0, 1), (2, 3), (4,), (5,), (6,), (7,), (), ())

        def flat(t3):
            return t3[:, :, :].rearrange("p t j -> p (t j)")

        with nc.Block() as block:
            @block.sync
            def _(sp):
                def load(chunk, k, piece):
                    at = slice((piece % 4) * (NB // 4), (piece % 4 + 1) * (NB // 4))
                    if piece < 4:
                        dst = pb[k][:, :, at, :, :, :].rearrange("p t b q c i -> p t (b q c i)")
                        src = p.b_parts
                    else:
                        rows = slice(at.start * IB, at.stop * IB)
                        dst = pa[k][:, :, rows, :, :].rearrange("p t i c q -> p t (i c q)")
                        src = p.a_parts
                    sp.dma_start(dst, src[chunk, :, :, at, :].rearrange("t p b n -> p t (b n)")).then_inc(loaded[k], 16)
                for piece in range(8):
                    load(0, 0, piece)
                if not sums:
                    for k in range(OR):
                        sp.dma_start(res[k][:, :, :], res_v[k]).then_inc(res_loaded[k], 16)

                def body(i, more):
                    for n in range(BODY):
                        if more or n < CH:
                            for piece in PIECES[n % CH]:
                                load(2 * i + 1 + n // CH, 1 - n // CH, piece)
                        sp.wait_ge(evacuated, i * BODY + n + 3)
                        sp.dma_start(out_v[i * BODY + n], o[n % OR][:, :, :]).then_inc(stored[n % OR], 16)
                        if not sums and (more or n + OR < BODY):
                            sp.dma_start(res[n % OR][:, :, :], res_v[i * BODY + n + OR]).then_inc(res_loaded[n % OR], 16)
                with sp.Fori(0, BODIES - 1) as i:
                    body(i, True)
                body(BODIES - 1, False)
                if sums:
                    sp.wait_ge(halves_ready, 1)
                    for row in range(2):
                        sp.dma_start(p.r2_rows[row].rearrange("(t p) k -> p t k", p=128),
                                     halves[:, row, :].rearrange("p (t k) -> p t k", t=KT)).then_inc(rows_stored, 16)
                    sp.wait_ge(rows_stored, 32)
                for k in range(OR):
                    sp.wait_ge(stored[k], 16 * (C // OR + 1))

            @block.tensor
            def _(pe):
                with pe.Fori(0, BODIES) as i:
                    for n in range(BODY):
                        k, c = n // CH, n % CH
                        if c == 0:
                            pe.wait_ge(loaded[k], (i + 1) * (16 * 8))
                        pe.wait_ge(evacuated, i * BODY + n + 1)
                        for t in range(KT):
                            dst = bank[n % 2][t][:, 0:N]
                            for kt in range(KT):
                                a_hi, a_lo = (pa[k][:, kt, t * 128:(t + 1) * 128, c, q] for q in (0, 1))
                                b_hi, b_lo = (pb[k][:, kt, :, q, c, :] for q in (0, 1))
                                pe.matmul(dst, lhsT=a_hi, rhs=b_hi, start=(kt == 0), stop=False)
                                pe.matmul(dst, lhsT=a_hi, rhs=b_lo, start=False, stop=False)
                                last = pe.matmul(dst, lhsT=a_lo, rhs=b_hi, start=False, stop=(kt == KT - 1))
                            last.then_inc(mixed, 1)

            if sums:
                @block.scalar
                def _(act):
                    act.sem_inc(evacuated, 2)
                    for k in range(OR):
                        act.sem_inc(stored[k], 16)
                    with act.Fori(0, BODIES) as i:
                        for n in range(BODY):
                            act.wait_ge(stored[n % OR], (i * (BODY // OR) + n // OR + 1) * 16)
                            act.wait_ge(s1_added, i * BODY + n + 1)
                            for t in range(KT):
                                act.wait_ge(mixed, i * (BODY * KT) + n * KT + t + 1)
                                last = act.activation(o[n % OR][:, t, :], bank[n % 2][t][:, 0:N], ACT.Copy)
                            last.then_inc(evacuated, 1)
                            act.wait_ge(evacuated, i * BODY + n + 3)
                            act.wait_ge(s2_added, i * BODY + n + 1)
                            act.activation(sq[n % 2][:, :], flat(o[n % OR]), ACT.Square).then_inc(sq_ready, 1)
                    act.wait_ge(var_ready, 1)
                    act.activation(sq[0][:, :], sq[1][:, :], ACT.Sqrt).then_inc(root_ready, 1)

                @block.gpsimd
                def _(pool):
                    pool.memset(S2[:, :], 0.0).then_inc(init, 1)
                    pool.wait_ge(init, 1)
                    pool.sem_inc(s2_added, 2)
                    with pool.Fori(0, BODIES) as i:
                        for n in range(BODY):
                            pool.wait_ge(sq_ready, i * BODY + n + 1)
                            pool.tensor_tensor(S2[:, :], S2[:, :], sq[n % 2][:, :], ALU.add).then_inc(s2_added, 1)
                            pool.wait_ge(s2_added, i * BODY + n + 3)

                @block.vector
                def _(dve):
                    dve.memset(S1[:, :], 0.0).then_inc(tail, 1)
                    dve.wait_ge(tail, 1)
                    dve.sem_inc(s1_added, 2)
                    with dve.Fori(0, BODIES) as i:
                        for n in range(BODY):
                            dve.wait_ge(evacuated, i * BODY + n + 3)
                            dve.tensor_tensor(S1[:, :], S1[:, :], flat(o[n % OR]), ALU.add).then_inc(s1_added, 1)
                            dve.wait_ge(s1_added, i * BODY + n + 3)
                    count = [1]

                    def step(ins):
                        count[0] += 1
                        ins.then_inc(tail, 1)
                        dve.wait_ge(tail, count[0])
                    dve.wait_ge(s2_added, C + 2)
                    step(dve.tensor_scalar(S1[:, :], S1[:, :], 1.0 / C, None, ALU.mult))
                    step(dve.tensor_tensor(S1[:, :], S1[:, :], S1[:, :], ALU.mult))
                    step(dve.scalar_tensor_tensor(out=sq[1][:, :], in0=S2[:, :], scalar=1.0 / C, in1=S1[:, :],
                                                  op0=ALU.mult, op1=ALU.subtract))
                    dve.tensor_scalar(sq[1][:, :], sq[1][:, :], 0.0, EPS, ALU.max, ALU.add).then_inc(var_ready, 1)
                    dve.wait_ge(root_ready, 1)
                    step(dve.reciprocal(S2[:, :], sq[0][:, :]))
                    refined_rsqrt(dve, step, S2[:, :], sq[1][:, :], S1[:, :])
                    step(dve.tensor_copy(halves[:, 0, :], S2[:, :]))
                    step(dve.tensor_tensor(halves[:, 1, :], S2[:, :], halves[:, 0, :], ALU.subtract))
                    dve.sem_inc(halves_ready, 1)
            else:
                @block.scalar
                def _(act):
                    with act.Fori(0, BODIES) as i:
                        act.wait_ge(scaled, i * BODY + 1)
                        act.activation(st[:, :, :], p.res_st[:, :, bass.ds(i * BODY, BODY)], ACT.Copy).then_inc(st_ready, 1)
                        act.wait_ge(st_ready, i + 1)
                        for n in range(BODY):
                            act.wait_ge(res_loaded[n % OR], (i * (BODY // OR) + n // OR + 1) * 16)
                            act.activation(flat(res[n % OR]), flat(res[n % OR]), ACT.Identity, scale=st[:, 0, n:n + 1],
                                           bias=st[:, 1, n:n + 1]).then_inc(scaled, 1)

                @block.vector
                def _(dve):
                    dve.sem_inc(evacuated, 2)
                    dve.sem_inc(scaled, 1)
                    for k in range(OR):
                        dve.sem_inc(stored[k], 16)
                    with dve.Fori(0, BODIES) as i:
                        for n in range(BODY):
                            dve.wait_ge(stored[n % OR], (i * (BODY // OR) + n // OR + 1) * 16)
                            dve.wait_ge(scaled, i * BODY + (n + 2))
                            for t in range(KT):
                                dve.wait_ge(mixed, i * (BODY * KT) + n * KT + t + 1)
                                last = dve.tensor_tensor(o[n % OR][:, t, :], bank[n % 2][t][:, 0:N],
                                                         res[n % OR][:, t, :], ALU.add)
                            last.then_inc(evacuated, 1)


def join0(nc, p, io):
    N = p.N
    SUB = 512
    TOK = 3 * SUB if (N * N) % (3 * SUB) == 0 else 2 * SUB
    NS = TOK // SUB
    TILES = N * N // TOK
    RING = 6 if TILES % 6 == 0 else 4
    BODIES = TILES // RING
    with ExitStack() as ctx:
        sb = lambda n, s, d: ctx.enter_context(nc.sbuf_tensor("join_" + n, s, d))
        ring = lambda n, s, d: [sb(f"{n}{k}", s, d) for k in range(RING)]
        two = lambda n, s, d: [sb(f"{n}{k}", s, d) for k in range(2)]
        x = ring("x", [C, TOK], F32)
        ab = ring("ab", [C, TOK], F32)
        r1 = ring("r1", [4, TOK], F16)
        r2 = ring("r2", [2, TOK], F16)
        yn = two("yn", [C, TOK], F32)
        yh = two("yh", [C, TOK], F16)
        yl = two("yl", [C, TOK], F16)
        zn = two("zn", [C, TOK], F32)
        zh = two("zh", [C, TOK], F16)
        zl = two("zl", [C, TOK], F16)
        gate = two("gate", [C, TOK], F32)
        x1 = two("x1", [C, TOK], F32)
        square = sb("square", [C, TOK], F32)
        sum_x1 = sb("sum_x1", [C, TILES], F32)
        sum_sq = sb("sum_sq", [C, TILES], F32)
        ones2 = sb("ones2", [2, C], F16)
        tot = sb("tot", [C, 8], F32)
        t_bc = sb("t_bc", [C, C], F32)
        diag = sb("diag", [C, 2, C], F32)
        psr = [ctx.enter_context(nc.psum_tensor(f"psr{k}", [128, SUB], F32)) for k in range(4)]
        psz = [ctx.enter_context(nc.psum_tensor(f"psz{k}", [128, SUB], F32)) for k in range(4)]
        loaded = [p.sem(f"join_loaded{k}") for k in range(RING)]
        spread = p.sem("join_r_spread")
        normed = p.sem("join_normed")
        hi = p.sem("join_hi")
        lo = p.sem("join_lo")
        prods = p.sem("join_products")
        gated = p.sem("join_gated")
        mul = p.sem("join_times_gate")
        done = p.sem("join_x1_done")
        squared = p.sem("join_squared")
        stored = [p.sem(f"join_stored{k}") for k in range(2)]
        ones_set = p.sem("join_ones_set")
        tail = p.sem("join_tail_step")
        operand = p.sem("join_tail_operand")
        tail_prod = p.sem("join_tail_product")
        s_ready = p.sem("join_s_ready")
        xf = io["x"].rearrange("c i k -> c (i k)")
        abf = p.ab.rearrange("c i k -> c (i k)")
        x1f = p.x1.rearrange("c i k -> c (i k)")
        r1f = p.r1_rows.rearrange("r i k -> r (i k)")
        r2f = p.r2_rows.rearrange("r i k -> r (i k)")
        NORM0, LO0, PROD0, MUL0, SQ0 = 4, 4, 4 * NS, 2, 2

        def cut(u):
            return slice(u * SUB, (u + 1) * SUB)

        def ahead(i, k, by):
            return i + (k + by) // RING, (k + by) % RING

        def over_tiles(engine, step):
            for k in range(RING):
                step(0, k, k)
            with engine.Fori(1, BODIES - 1) as i:
                for k in range(RING):
                    step(i, k, None)
            for k in range(RING):
                step(BODIES - 1, k, TILES - RING + k)

        def exists(t, by):
            return t is None or 0 <= t + by < TILES

        with nc.Block() as block:
            @block.sync
            def _(sp):
                def load(t, k):
                    at = bass.ds(t * TOK, TOK)
                    sp.dma_start(x[k][:, :], xf[:, at]).then_inc(loaded[k], 16)
                    sp.dma_start(ab[k][:, :], abf[:, at]).then_inc(loaded[k], 16)
                    sp.dma_start(r1[k][0:3, :], r1f[:, at]).then_inc(loaded[k], 16)
                    sp.dma_start(r2[k][:, :], r2f[:, at]).then_inc(loaded[k], 16)
                for k in range(RING):
                    load(k, k)

                def body(i, more):
                    for k in range(RING):
                        sp.wait_ge(done, i * RING + k + 1)
                        sp.dma_start(x1f[:, bass.ds((i * RING + k) * TOK, TOK)],
                                     x1[k % 2][:, :]).then_inc(stored[k % 2], 16)
                        if more:
                            load(i * RING + k + RING, k)
                with sp.Fori(0, BODIES - 1) as i:
                    body(i, True)
                body(BODIES - 1, False)
                for k in range(2):
                    sp.wait_ge(stored[k], 16 * (TILES // 2 + 1))

            @block.tensor
            def _(pe):
                pe.wait_ge(ones_set, 1)
                pe.sem_inc(prods, PROD0)

                def spread_r(i, k, u):
                    t = RING * i + k
                    if u == 0:
                        pe.wait_ge(loaded[k], (i + 1) * 64)
                    bank = 2 * ((NS * k + u) % 2)
                    pe.wait_ge(normed, t * (2 * NS) + (2 * u + NORM0 - 2))
                    pe.matmul(psr[bank][:, :], lhsT=p.s_rows[0:3, :], rhs=r1[k][0:3, cut(u)],
                              start=True, stop=True).then_inc(spread, 1)
                    pe.matmul(psr[bank + 1][:, :], lhsT=ones2[:, :], rhs=r2[k][:, cut(u)],
                              start=True, stop=True).then_inc(spread, 1)

                def products(i, k, u):
                    t, h = RING * i + k, k % 2
                    if u == 0:
                        pe.wait_ge(lo, t * 2 + (2 + LO0))
                    bank = 2 * ((NS * k + u) % 2)
                    pe.wait_ge(mul, t * NS + (u - 1 + MUL0))
                    for q, (wh, wl, vh, vl) in enumerate(((p.gh, p.gl, yh, yl), (p.ah, p.al, zh, zl))):
                        dst = psz[bank + q][:, :]
                        pe.matmul(dst, lhsT=wh[:, :], rhs=vh[h][:, cut(u)], start=True, stop=False)
                        pe.matmul(dst, lhsT=wh[:, :], rhs=vl[h][:, cut(u)], start=False, stop=False)
                        pe.matmul(dst, lhsT=wl[:, :], rhs=vh[h][:, cut(u)], start=False, stop=True
                                  ).then_inc(prods, 1)

                def step(i, k, t):
                    for u in range(NS):
                        if exists(t, 2):
                            spread_r(*ahead(i, k, 2), u)
                        products(i, k, u)
                for k in range(2):
                    for u in range(NS):
                        spread_r(0, k, u)
                over_tiles(pe, step)
                pe.wait_ge(operand, 1)
                pe.matmul(psr[0][:, 0:2], lhsT=p.group_mat[:, :], rhs=tot[:, 0:2],
                          start=True, stop=True).then_inc(tail_prod, 1)
                pe.wait_ge(operand, 3)
                for q, w in enumerate((p.wa_t, p.wb_t)):
                    pe.matmul(psr[1 + q][:, 0:C], lhsT=t_bc[:, :], rhs=w[:, :], start=True, stop=False)
                    pe.matmul(psr[1 + q][:, 0:C], lhsT=p.ones[0:1, :], rhs=p.bias_ab[0:1, q * C:(q + 1) * C],
                              start=False, stop=True).then_inc(tail_prod, 1)
                pe.wait_ge(operand, 4)
                pe.matmul(psr[3][:, 0:2 * C], lhsT=p.ones[:, :], rhs=diag[:, :, :].rearrange("p q c -> p (q c)"),
                          start=True, stop=True).then_inc(tail_prod, 1)

            @block.scalar
            def _(act):
                act.sem_inc(squared, SQ0)

                def halves(i, k, q):
                    t, h = RING * i + k, k % 2
                    if q == 0:
                        act.wait_ge(prods, t * (2 * NS) + (PROD0 - 2 * NS))
                        act.wait_ge(normed, t * (2 * NS) + (2 * NS + NORM0))
                    dst, src = ((yh, yn), (zh, zn))[q]
                    act.activation(dst[h][:, :], src[h][:, :], ACT.Copy).then_inc(hi, 1)

                def gates(i, k, u):
                    t, h = RING * i + k, k % 2
                    bank = 2 * ((NS * k + u) % 2)
                    act.wait_ge(prods, t * (2 * NS) + (2 * u + 1 + PROD0))
                    act.activation(gate[h][:, cut(u)], psz[bank][:, :], ACT.Sigmoid,
                                   scale=1.0 / WS, bias=p.vg[:, :]).then_inc(gated, 1)

                def squares(i, k):
                    t = RING * i + k
                    act.wait_ge(done, t + 1)
                    act.wait_ge(squared, t + SQ0)
                    act.activation(square[:, :], x1[k % 2][:, :], ACT.Square,
                                   accum_out=sum_sq[:, bass.ds(t, 1)]).then_inc(squared, 1)

                def step(i, k, t):
                    for u in range(NS):
                        if u < 2 and exists(t, 1):
                            halves(*ahead(i, k, 1), u)
                        gates(i, k, u)
                    if exists(t, -1):
                        squares(*ahead(i, k, -1))
                halves(0, 0, 0)
                halves(0, 0, 1)
                over_tiles(act, step)
                squares(BODIES - 1, RING - 1)

            @block.gpsimd
            def _(pool):
                pool.sem_inc(lo, LO0)
                with pool.Fori(0, BODIES) as i:
                    for k in range(RING):
                        for q, (src, h, dst) in enumerate(((yn, yh, yl), (zn, zh, zl))):
                            pool.wait_ge(hi, (RING * i + k) * 2 + (q + 1))
                            pool.tensor_tensor(dst[k % 2][:, :], src[k % 2][:, :], h[k % 2][:, :],
                                               ALU.subtract).then_inc(lo, 1)
                pool.wait_ge(operand, 2)
                pool.tensor_tensor(tot[:, 4:5], tot[:, 3:4], tot[:, 5:6], ALU.pow).then_inc(s_ready, 1)

            @block.vector
            def _(dve):
                dve.memset(ones2[:, :], 1.0).then_inc(ones_set, 1)
                dve.sem_inc(normed, NORM0)
                dve.sem_inc(mul, MUL0)
                dve.sem_inc(stored[0], 16)
                dve.sem_inc(stored[1], 16)

                def norm(i, k, u):
                    t, h = RING * i + k, k % 2
                    if u == 0:
                        dve.wait_ge(loaded[k], (i + 1) * 64)
                        dve.wait_ge(lo, t * 2 + (LO0 - 2))
                    bank = 2 * ((NS * k + u) % 2)
                    dve.wait_ge(spread, t * (2 * NS) + (2 * u + 1))
                    dve.scalar_tensor_tensor(out=yn[h][:, cut(u)], in0=x[k][:, cut(u)], scalar=p.st0[:, 2:3],
                                             in1=psr[bank][:, :], op0=ALU.add, op1=ALU.mult).then_inc(normed, 1)
                    dve.wait_ge(spread, t * (2 * NS) + (2 * u + 2))
                    dve.tensor_tensor(zn[h][:, cut(u)], ab[k][:, cut(u)], psr[bank + 1][:, :],
                                      ALU.mult).then_inc(normed, 1)

                def times_gate(i, k, u):
                    t, h = RING * i + k, k % 2
                    bank = 2 * ((NS * k + u) % 2)
                    dve.wait_ge(gated, t * NS + (u + 1))
                    dve.wait_ge(prods, t * (2 * NS) + (2 * u + 2 + PROD0))
                    dve.scalar_tensor_tensor(out=gate[h][:, cut(u)], in0=psz[bank + 1][:, :], scalar=p.v2[:, :],
                                             in1=gate[h][:, cut(u)], op0=ALU.add, op1=ALU.mult).then_inc(mul, 1)

                def finish(i, k):
                    t, h = RING * i + k, k % 2
                    dve.wait_ge(mul, t * NS + (NS + MUL0))
                    dve.wait_ge(stored[h], (i * (RING // 2) + k // 2 + 1) * 16)
                    dve.wait_ge(squared, t + (SQ0 - 1))
                    dve.scalar_tensor_tensor(out=x1[h][:, :], in0=gate[h][:, :], scalar=1.0 / WS, in1=x[k][:, :],
                                             op0=ALU.mult, op1=ALU.add,
                                             accum_out=sum_x1[:, bass.ds(t, 1)]).then_inc(done, 1)

                def step(i, k, t):
                    for u in range(NS):
                        if exists(t, 2):
                            norm(*ahead(i, k, 2), u)
                        times_gate(i, k, u)
                    finish(i, k)
                for k in range(2):
                    for u in range(NS):
                        norm(0, k, u)
                over_tiles(dve, step)

                chain = chained(dve, tail)
                dve.wait_ge(squared, TILES + SQ0)
                dve.wait_ge(done, TILES)
                chain(dve.tensor_reduce(tot[:, 0:1], sum_x1[:, :], axis=AX.X, op=ALU.add))
                chain(dve.tensor_reduce(tot[:, 1:2], sum_sq[:, :], axis=AX.X, op=ALU.add))
                chain(dve.tensor_scalar(tot[:, 0:2], tot[:, 0:2], 1.0 / (N * N), None, ALU.mult))
                dve.sem_inc(operand, 1)
                dve.wait_ge(tail_prod, 1)
                chain(dve.tensor_copy(tot[:, 2:3], psr[0][:, 0:1]))
                chain(dve.tensor_tensor(tot[:, 6:7], tot[:, 2:3], tot[:, 2:3], ALU.mult))
                chain(dve.tensor_tensor(tot[:, 3:4], psr[0][:, 1:2], tot[:, 6:7], ALU.subtract))
                chain(dve.tensor_scalar(tot[:, 3:4], tot[:, 3:4], 0.0, EPS, ALU.max, ALU.add))
                chain(dve.memset(tot[:, 5:6], -0.5))
                dve.sem_inc(operand, 1)
                chain(dve.tensor_scalar(tot[:, 7:8], tot[:, 2:3], -1.0, None, ALU.mult))
                dve.wait_ge(s_ready, 1)
                chain(dve.tensor_copy(p.st1[:, 0:1], tot[:, 4:5]))
                chain(dve.tensor_tensor(p.st1[:, 1:2], tot[:, 7:8], tot[:, 4:5], ALU.mult))
                chain(dve.tensor_scalar(t_bc[:, :], p.ones[:, :], p.st1[:, 1:2], None, ALU.mult))
                dve.sem_inc(operand, 1)
                dve.wait_ge(tail_prod, 3)
                for q in range(2):
                    for u in range(QT):
                        chain(dve.tensor_copy(p.const1[:, q, u, :], psr[1 + q][:, 0:C]))
                for q in range(2):
                    chain(dve.tensor_scalar(diag[:, q, :], p.ident[:, :], p.st1[:, q:q + 1], None, ALU.mult))
                dve.sem_inc(operand, 1)
                dve.wait_ge(tail_prod, 4)
                chain(dve.tensor_scalar(p.res_st[:, 0, :], psr[3][:, 0:C], 1.0, None, ALU.add))
                chain(dve.tensor_copy(p.res_st[:, 1, :], psr[3][:, C:2 * C]))


def project1(nc, p):
    KT = p.KT
    G = 128 // IB
    with ExitStack() as ctx:
        sb = lambda n, s, d: ctx.enter_context(nc.sbuf_tensor("sq_" + n, s, d))
        XR, SR = 4, 4
        x = [sb(f"x{k}", [C, IB, 128], F32) for k in range(XR)]
        yh = sb("yh", [C, 128, 128], F16)
        yl = sb("yl", [C, 128, 128], F16)
        value = [sb(f"value{k}", [128, QT, C], F32) for k in range(4)]
        stage = [sb(f"stage{k}", [128, NCH, 2 * CH * IB], F16) for k in range(SR)]
        bank = [ctx.enter_context(nc.psum_tensor(f"sqbank{k}", [128, QT, C], F32)) for k in range(8)]
        loaded = [p.sem(f"sq_loaded{k}") for k in range(XR)]
        x_hi = p.sem("sq_x_hi")
        x_lo = p.sem("sq_x_lo")
        projected = p.sem("sq_projected")
        valued = p.sem("sq_valued")
        v_hi = p.sem("sq_value_hi")
        lo_pool = p.sem("sq_value_lo_by_pool")
        lo_dve = p.sem("sq_value_lo_by_dve")
        seen = p.sem("sq_lo_by_pool_seen")
        stored = [p.sem(f"sq_stored{k}") for k in range(SR)]
        B = IB // QT
        BATCHES = 2 * G * B
        VAL0, LO0, PROJ0 = 8, 1, 1

        def pool_takes(n):
            if n < BATCHES // 2:
                return n < (G - 1) * B or n % 2 == 0
            return n % 8 in (0, 3, 6)

        def wait_lo(engine, q, n):
            pool_n = sum(pool_takes(m) for m in range(n))
            pool_all = sum(pool_takes(m) for m in range(BATCHES))
            engine.wait_ge(lo_pool, q * pool_all + (pool_n + LO0))
            if engine is nc.sync:
                engine.sem_inc(seen, 1)
            engine.wait_ge(lo_dve, q * (BATCHES - pool_all) + (n - pool_n + LO0))

        def squares(engine, body):
            if KT > 1:
                with engine.Fori(0, KT * KT - 1) as q:
                    body(q, True)
            body(KT * KT - 1, False)

        def stage_halves(g, half, m):
            tile = stage[g % SR][:, :, :]
            if g < G:
                return batch_of(tile.rearrange("p h (i c q) -> p h i c q", c=CH, q=2), 0, half, m)
            return batch_of(tile.rearrange("p h (q c i) -> p h q c i", q=2, c=CH), 1, half, m)

        def value_of(batch):
            return value[batch % 4][:, :, :].rearrange("p i (h c) -> p i h c", c=CH)

        with nc.Block() as block:
            @block.sync
            def _(sp):
                def load(it, kt, g):
                    sp.wait_ge(x_lo, (it * KT + kt) * G + (g + 1))
                    sp.dma_start(x[g % XR][:, :, :],
                                 p.x1[:, bass.ds(it * 128 + g * IB, IB), bass.ds(kt * 128, 128)]
                                 ).then_inc(loaded[g % XR], 16)

                def square(it, kt, following):
                    for g in range(2 * G):
                        if g + XR < G:
                            load(it, kt, g + XR)
                        elif following and G - 2 <= g < G + XR - 2:
                            load(*following, g - (G - 2))
                        wait_lo(sp, it * KT + kt, (g + 1) * B)
                        parts, rows, blk = (p.b_parts, it, kt * G + (g - G)) if g >= G else (p.a_parts, kt, it * G + g)
                        store_stage(sp, stage[g % SR], parts, rows, blk).then_inc(stored[g % SR], 16)

                def row(it, more):
                    for kt in range(KT):
                        square(it, kt, (it, kt + 1) if kt + 1 < KT else (it + 1, 0) if more else None)
                for g in range(XR):
                    load(0, 0, g)
                if KT > 1:
                    with sp.Fori(0, KT - 1) as it:
                        row(it, True)
                row(KT - 1, False)
                for k in range(SR):
                    sp.wait_ge(stored[k], 16 * (KT * KT * 2 * G // SR + 1))

            @block.tensor
            def _(pe):
                def body(q, more):
                    for g in range(2 * G):
                        right = g >= G
                        if right:
                            wh, wl = p.lbh, p.lbl
                        else:
                            wh, wl = p.lah, p.lal
                            pe.wait_ge(x_lo, q * G + (g + 1 + XR))
                        for m in range(B):
                            n = g * B + m
                            pe.wait_ge(valued, q * BATCHES + (n + 1))
                            for u in range(QT):
                                t = (g % G) * IB + m * QT + u
                                hi = yh[:, :, t] if right else yh[:, t, :]
                                lo = yl[:, :, t] if right else yl[:, t, :]
                                dst = bank[n % 8][:, u, :]
                                pe.matmul(dst, lhsT=hi, rhs=wh[:, :], start=True, stop=False)
                                pe.matmul(dst, lhsT=hi, rhs=wl[:, :], start=False, stop=False)
                                last = pe.matmul(dst, lhsT=lo, rhs=wh[:, :], start=False, stop=True)
                            last.then_inc(projected, 1)
                pe.sem_inc(projected, PROJ0)
                squares(pe, body)

            @block.scalar
            def _(act):
                for k in range(SR):
                    act.sem_inc(stored[k], 16)

                def body(q, more, start=False):
                    def split(g, q=q):
                        act.wait_ge(loaded[g % XR], (q * (G // XR) + (g // XR + 1)) * 16)
                        if g == 0:
                            act.wait_ge(projected, q * BATCHES + PROJ0)
                        act.activation(yh[:, g * IB:(g + 1) * IB, :], x[g % XR][:, :, :], ACT.Copy,
                                       scale=p.st1[:, 0:1]).then_inc(x_hi, 1)

                    def value_hi(g, m):
                        if m == 0:
                            act.wait_ge(stored[g % SR], (q * (2 * G // SR) + (g // SR + 1)) * 16)
                        n = g * B + m
                        act.wait_ge(valued, q * BATCHES + (n + 1 + VAL0))
                        act.activation(stage_halves(g, 0, m), value_of(n), ACT.Copy).then_inc(v_hi, 1)
                    if start:
                        split(0)
                        split(1)
                        return
                    for g in range(2 * G):
                        if g + 2 < G:
                            split(g + 2)
                        for m in range(B):
                            value_hi(g, m)
                            if more and (g, m) in ((2 * G - 2, 0), (2 * G - 2, B - 1)):
                                split(m // (B - 1), q + 1)
                body(0, True, start=True)
                squares(act, body)

            @block.gpsimd
            def _(pool):
                pool.sem_inc(lo_pool, LO0)

                def body(q, more):
                    for g in range(2 * G):
                        for m in range(B):
                            if pool_takes(g * B + m):
                                pool.wait_ge(v_hi, q * BATCHES + (g * B + m + 1))
                                pool.tensor_tensor(stage_halves(g, 1, m), value_of(g * B + m),
                                                   stage_halves(g, 0, m), ALU.subtract).then_inc(lo_pool, 1)
                squares(pool, body)

            @block.vector
            def _(dve):
                dve.sem_inc(valued, VAL0)
                dve.sem_inc(x_lo, XR)
                dve.sem_inc(lo_dve, LO0)

                def body(q, more, start=False):
                    def split(g, q=q):
                        dve.wait_ge(x_hi, q * G + (g + 1))
                        at = slice(g * IB, (g + 1) * IB)
                        dve.scalar_tensor_tensor(out=yl[:, at, :], in0=x[g % XR][:, :, :], scalar=p.st1[:, 0:1],
                                                 in1=yh[:, at, :], op0=ALU.mult, op1=ALU.subtract).then_inc(x_lo, 1)
                    def value_lo(n):
                        if not pool_takes(n):
                            dve.wait_ge(v_hi, q * BATCHES + (n + 1))
                            dve.tensor_tensor(stage_halves(n // B, 1, n % B), value_of(n),
                                              stage_halves(n // B, 0, n % B), ALU.subtract).then_inc(lo_dve, 1)
                    if start:
                        split(0)
                        return
                    for g in range(2 * G):
                        if g + 1 < G:
                            split(g + 1)
                        for m in range(B):
                            n = g * B + m
                            wait_lo(dve, q, max(n - 3, 0))
                            dve.wait_ge(projected, q * BATCHES + (n + 1 + PROJ0))
                            dve.scalar_tensor_tensor(
                                out=value[n % 4][:, :, :].rearrange("p i c -> p (i c)"),
                                in0=bank[n % 8][:, :, :].rearrange("p i c -> p (i c)"), scalar=1.0 / WS,
                                in1=p.const1[:, int(g >= G), :, :].rearrange("p i c -> p (i c)"),
                                op0=ALU.mult, op1=ALU.add).then_inc(valued, 1)
                            if n:
                                value_lo(n - 1)
                            if n == BATCHES - 4 and more:
                                split(0, q + 1)
                    value_lo(BATCHES - 1)
                body(0, True, start=True)
                squares(dve, body)


def batch_of(stage, ab, half, m):
    at = slice(m * QT, (m + 1) * QT)
    if ab:
        return stage[:, :, half, :, at].rearrange("p h c i -> p i h c")
    return stage[:, :, at, :, half].rearrange("p h i c -> p i h c")


def store_stage(engine, stage, parts, k_tile, block):
    src = stage[:]
    if len(src.shape) == 5:
        src = src.rearrange("p h a b c -> p h (a b c)")
    dst = parts[:, bass.ds(k_tile, 1), :, bass.ds(block, 1), :]
    return engine.dma_start(dst.rearrange("h t p b n -> p (h t b) n"), src)


def build(nc, x, ln_vectors, W_proj, W_gate, W_ab, WaT, WbT, bias_ab, identity, centering, group_mean,
          expand, row_masks, out):
    io = dict(x=x, ln_vectors=ln_vectors, W_proj=W_proj, W_gate=W_gate, W_ab=W_ab, WaT=WaT, WbT=WbT,
              bias_ab=bias_ab, identity=identity, centering=centering, group_mean=group_mean,
              expand=expand, row_masks=row_masks)
    p = Plan()
    p.N = x.shape[1]
    p.KT = p.N // 128
    p.NB = p.N // IB
    N, KT = p.N, p.KT
    with ExitStack() as ctx:
        sb = lambda n, s, d: ctx.enter_context(nc.sbuf_tensor(n, s, d))
        p.sem = lambda n: ctx.enter_context(nc.semaphore(n))
        p.a_parts = nc.dram_tensor("a_parts", [NCH, KT, 128, p.NB, 2 * CH * IB], F16, kind="Internal").ap()
        p.b_parts = nc.dram_tensor("b_parts", [NCH, KT, 128, p.NB, 2 * CH * IB], F16, kind="Internal").ap()
        p.ab = nc.dram_tensor("ab_sum", [C, N, N], F32, kind="Internal").ap()
        p.x1 = nc.dram_tensor("x1", [C, N, N], F32, kind="Internal").ap()
        p.r1_rows = nc.dram_tensor("r1_rows", [3, N, N], F16, kind="Internal").ap()
        p.std_rows = nc.dram_tensor("std_rows", [3, N, N], F16, kind="Internal").ap()
        p.r2_rows = nc.dram_tensor("r2_rows", [2, N, N], F16, kind="Internal").ap()
        p.kappa_rows = nc.dram_tensor("kappa_rows", [2, IB, 4 * C], F16, kind="Internal").ap()
        p.ident = sb("ident", [C, C], F32)
        p.ident16 = sb("ident16", [C, C], F16)
        p.ones = sb("ones", [C, C], F32)
        p.mean_mat = sb("mean_mat", [C, C], F32)
        p.group_mat = sb("group_mat", [C, C], F32)
        p.expand = sb("expand_sb", [NG, C], F32)
        p.wa_t, p.wb_t = sb("wa_t", [C, C], F32), sb("wb_t", [C, C], F32)
        p.bias_ab = sb("bias_sb", [1, 2 * C], F32)
        p.gh, p.gl, p.ah, p.al = (sb(n, [C, C], F16) for n in ("gh", "gl", "ah", "al"))
        p.lah, p.lal, p.lbh, p.lbl = (sb(n, [C, C], F16) for n in ("lah", "lal", "lbh", "lbl"))
        p.vg, p.v2 = sb("vg", [C, 1], F32), sb("v2", [C, 1], F32)
        p.st0 = sb("st0", [C, 4], F32)
        p.st1 = sb("st1", [C, 2], F32)
        p.s_rows = sb("s_rows", [4, C], F16)
        p.res_st = sb("res_st", [128, 2, C], F32)
        p.const1 = sb("const1", [C, 2, QT, C], F32)
        with ExitStack() as first:
            sf = lambda n, s, d: first.enter_context(nc.sbuf_tensor(n, s, d))
            p.wh, p.wl = sf("wh", [C, 4 * C], F16), sf("wl", [C, 4 * C], F16)
            p.r64 = sf("r64", [C, KT, N], F32)
            p.const_rows = sf("const_rows", [64, IB, 4 * C], F16)
            p.x_rows = [sf(f"x_rows{k}", [C, IB, N], F32) for k in range(2)]
            p.x_loaded = [p.sem(f"x_loaded{k}") for k in range(2)]
            with ExitStack() as prep:
                sp_ = lambda n, s, d: prep.enter_context(nc.sbuf_tensor(n, s, d))
                p.w64 = sp_("w64", [C, 4 * C], F32)
                p.v_rows = sp_("v_rows", [64, 4 * C], F16)
                p.masks = sp_("masks", [C, IB], F32)
                prepare_weights(nc, p, io)
                stats0(nc, p, io)
            project0(nc, p, io)
        mix(nc, p, "mix0_", p.ab, None)
        join0(nc, p, io)
        project1(nc, p)
        mix(nc, p, "mix1_", out, p.x1)


def shape_constants():
    import numpy as np
    eye = np.eye(C, dtype=np.float32)
    group = np.kron(np.eye(NG, dtype=np.float32), np.ones((GROUP, GROUP), np.float32))
    expand = np.kron(np.eye(NG, dtype=np.float32), np.ones((1, GROUP), np.float32))
    masks = np.zeros((C, IB), np.float32)
    for t in range(IB):
        masks[t, t] = masks[IB + t, t] = masks[2 * IB + t, t] = 1
    return dict(identity=eye, centering=eye - np.float32(1.0 / C), group_mean=group / np.float32(GROUP),
                expand=expand, row_masks=masks)


def kernel(x, L0_conv_ln1_g, L0_conv_ln1_b, L0_conv_W_proj, L0_conv_W_gate, L0_conv_ln2_g, L0_conv_ln2_b,
           L0_conv_W_ab, L1_conv_Wa, L1_conv_ba, L1_conv_Wb, L1_conv_bb):
    import numpy as np
    import concourse.bacc as bacc
    from concourse.bass_utils import run_bass_kernel_spmd

    f = lambda a: np.ascontiguousarray(a)
    arrays = dict(
        x=f(np.transpose(np.asarray(x)[0], (2, 0, 1))),
        ln_vectors=f(np.stack([L0_conv_ln1_g, L0_conv_ln1_b, L0_conv_ln2_g, L0_conv_ln2_b], axis=1)),
        W_proj=f(L0_conv_W_proj), W_gate=f(L0_conv_W_gate), W_ab=f(L0_conv_W_ab),
        WaT=f(np.transpose(L1_conv_Wa)), WbT=f(np.transpose(L1_conv_Wb)),
        bias_ab=f(np.concatenate([np.asarray(L1_conv_ba), np.asarray(L1_conv_bb)])[None, :]),
        **shape_constants())
    nc = bacc.Bacc("TRN2", target_bir_lowering=False, num_devices=1)
    args = {n: nc.dram_tensor("in_" + n, a.shape, F32, kind="ExternalInput").ap() for n, a in arrays.items()}
    N = arrays["x"].shape[1]
    out = nc.dram_tensor("out_0", (C, N, N), F32, kind="ExternalOutput").ap()
    build(nc, out=out, **args)
    r = run_bass_kernel_spmd(nc, [{"in_" + n: a for n, a in arrays.items()}], core_ids=[0])
    return np.transpose(r.results[0]["out_0"], (1, 2, 0))[None]
```
